# Optimizing a Trainium2 kernel written in Bass

```python
import numpy as np
import jax
import jax.numpy as jnp

def _softmax(x, axis=-1):
    return jax.nn.softmax(x, axis=axis)

def _gelu(x):
    return jax.nn.gelu(x, approximate=True)

def _silu(x):
    return jax.nn.silu(x)

def _sigmoid(x):
    return jax.nn.sigmoid(x)

def _layernorm(x, axis=-1, eps=1e-05):
    m = jnp.mean(x, axis=axis, keepdims=True)
    v = jnp.var(x, axis=axis, keepdims=True)
    return (x - m) / jnp.sqrt(v + eps)

def _scatter_add(tgt, idx, src, axis=0):
    return tgt.at[idx].add(src)

def _segment_sum(src, seg, n):
    return jax.ops.segment_sum(src, seg, n)
kernel_name = 'mk_xattn_ffn_d2_seqx_r8_a88123'

def setup_inputs(seed: int=0):
    np.random.seed(seed)
    _w = jnp.asarray

    def _rec_inputs():
        import jax
        import jax.numpy as jnp
        _rk = jax.random.key(seed)
        x = 7.22e-05 + 1 * jax.random.normal(jax.random.fold_in(_rk, 1), (32, 128, 128), jnp.float32)
        _lenS = 128 - jax.random.randint(jax.random.fold_in(_rk, 7), (32,), 0, max(1, 128 // 4) + 1, jnp.int32)
        _lenS2 = 77 - jax.random.randint(jax.random.fold_in(_rk, 8), (32,), 0, max(1, 77 // 4) + 1, jnp.int32)
        _ctx_1024P = jax.random.normal(jax.random.fold_in(_rk, 11), (32, 16, 128), jnp.float32)
        _ctx_1024c = jax.random.dirichlet(jax.random.fold_in(_rk, 511), 0.3 * jnp.ones((16,), jnp.float32), (32, 77))
        _ctx_1024t = jnp.einsum('bsk,bkd->bsd', _ctx_1024c, _ctx_1024P)
        _ctx_1024t = _ctx_1024t * jax.lax.rsqrt(jnp.mean(jnp.square(_ctx_1024t)) + 1e-12) * 0.953939
        ctx_1024 = 4.13588e-05 + 0.999923 * (_ctx_1024t + 0.3 * jax.random.normal(jax.random.fold_in(_rk, 611), (32, 77, 128), jnp.float32))
        return (x, ctx_1024)
    x, ctx_1024 = _rec_inputs()

    def _L0_xattn_setup():
        import jax, jax.numpy as jnp
        import numpy as np
        D_MODEL = 128
        N_HEAD = 16

        def _split_heads(x, n_head):
            B, S, D = x.shape
            return x.reshape(B, S, n_head, D // n_head).transpose(0, 2, 1, 3)
        key = jax.random.key(seed)
        ks = jax.random.split(key, 12)
        B, S, D = (4, 256, D_MODEL)
        scale = 1.0 / np.sqrt(D)
        inp = {'Q': jax.random.normal(ks[0], (B, S, D), jnp.float32), 'K': jax.random.normal(ks[1], (B, S, D), jnp.float32), 'V': jax.random.normal(ks[2], (B, S, D), jnp.float32), 'Wq': jax.random.normal(ks[3], (D, D), jnp.float32) * scale, 'bq': jax.random.normal(ks[4], (D,), jnp.float32) * scale, 'Wk': jax.random.normal(ks[5], (D, D), jnp.float32) * scale, 'bk': jax.random.normal(ks[6], (D,), jnp.float32) * scale, 'Wv': jax.random.normal(ks[7], (D, D), jnp.float32) * scale, 'bv': jax.random.normal(ks[8], (D,), jnp.float32) * scale, 'Wo': jax.random.normal(ks[9], (D, D), jnp.float32) * scale, 'bo': jax.random.normal(ks[10], (D,), jnp.float32) * scale}
        return inp
    _L0_xattn_all = _L0_xattn_setup()
    _L0_xattn_in = {k: v for k, v in _L0_xattn_all.items() if k in ('Wq', 'bq', 'Wk', 'bk', 'Wv', 'bv', 'Wo', 'bo')}
    del _L0_xattn_all

    def _L0_ffn_setup():
        import jax, jax.numpy as jnp
        import numpy as np
        B, S, H, DFF, E, K = (2, 256, 128, 256, 8, 2)

        def _moe(x, Wg, W1, b1, W2, b2, W3, b3):
            Bm, Sm, Hm = x.shape
            xt = x.reshape(-1, Hm)
            gout = xt @ Wg.T
            topv, topi = jax.lax.top_k(gout, K)
            w = jax.nn.softmax(topv, axis=-1)
            comb = jnp.einsum('tke,tk->te', jax.nn.one_hot(topi, E, dtype=x.dtype), w)
            g = jnp.einsum('th,efh->etf', xt, W1) + b1[:, None, :]
            v = jnp.einsum('th,efh->etf', xt, W2) + b2[:, None, :]
            h = jax.nn.silu(g) * v
            eo = jnp.einsum('etf,ehf->eth', h, W3) + b3[:, None, :]
            out = jnp.einsum('eth,te->th', eo, comb)
            return out.reshape(Bm, Sm, Hm)
        key = jax.random.key(seed)
        ks = jax.random.split(key, 8)
        sc_h = 1.0 / np.sqrt(H)
        sc_f = 1.0 / np.sqrt(DFF)
        x = jax.random.normal(ks[0], (B, S, H), dtype=jnp.float32)
        Wg = jax.random.uniform(ks[1], (E, H), jnp.float32, -sc_h, sc_h)
        W1 = jax.random.uniform(ks[2], (E, DFF, H), jnp.float32, -sc_h, sc_h)
        b1 = jax.random.uniform(ks[3], (E, DFF), jnp.float32, -sc_h, sc_h)
        W2 = jax.random.uniform(ks[4], (E, DFF, H), jnp.float32, -sc_h, sc_h)
        b2 = jax.random.uniform(ks[5], (E, DFF), jnp.float32, -sc_h, sc_h)
        W3 = jax.random.uniform(ks[6], (E, H, DFF), jnp.float32, -sc_f, sc_f)
        b3 = jax.random.uniform(ks[7], (E, H), jnp.float32, -sc_f, sc_f)
        return {'x': x, 'Wg': Wg, 'W1': W1, 'b1': b1, 'W2': W2, 'b2': b2, 'W3': W3, 'b3': b3}
    _L0_ffn_all = _L0_ffn_setup()
    _L0_ffn_in = {k: v for k, v in _L0_ffn_all.items() if k in ('Wg', 'W1', 'b1', 'W2', 'b2', 'W3', 'b3')}
    del _L0_ffn_all

    def _L1_xattn_setup():
        import jax, jax.numpy as jnp
        import numpy as np
        B, T, C, H = (4, 512, 128, 16)
        D = C // H

        def _heads(t):
            b, n, c = t.shape
            return t.reshape(b, n, H, D).transpose(0, 2, 1, 3)
        key = jax.random.key(seed)
        ks = jax.random.split(key, 10)
        s = 1.0 / np.sqrt(C)
        return {'x': jax.random.normal(ks[0], (B, T, C), jnp.float32), 'y': jax.random.normal(ks[1], (B, T, C), jnp.float32), 'Wq': jax.random.normal(ks[2], (C, C), jnp.float32) * s, 'bq': jnp.zeros((C,), jnp.float32), 'Wk': jax.random.normal(ks[3], (C, C), jnp.float32) * s, 'bk': jnp.zeros((C,), jnp.float32), 'Wv': jax.random.normal(ks[4], (C, C), jnp.float32) * s, 'bv': jnp.zeros((C,), jnp.float32), 'Wp': jax.random.normal(ks[5], (C, C), jnp.float32) * s, 'bp': jnp.zeros((C,), jnp.float32)}
    _L1_xattn_all = _L1_xattn_setup()
    _L1_xattn_in = {k: v for k, v in _L1_xattn_all.items() if k in ('Wq', 'bq', 'Wk', 'bk', 'Wv', 'bv', 'Wp', 'bp')}
    del _L1_xattn_all

    def _L1_ffn_setup():
        import jax, jax.numpy as jnp
        import numpy as np
        D_MODEL = 128
        HIDDEN = 512
        NUM_EXPERTS = 8
        TOP_K = 2
        NUM_SHARED = 2

        def _gelu(x):
            return jax.nn.gelu(x, approximate=False)
        key = jax.random.key(seed)
        ks = jax.random.split(key, 12)
        s = 0.02
        return {'x': jax.random.normal(ks[0], (2, 256, D_MODEL), dtype=jnp.float32), 'rW': jax.random.normal(ks[1], (D_MODEL, NUM_EXPERTS), dtype=jnp.float32) * s, 'rb': jnp.zeros((NUM_EXPERTS,), dtype=jnp.float32), 'W1': jax.random.normal(ks[2], (NUM_EXPERTS, D_MODEL, HIDDEN), dtype=jnp.float32) * s, 'b1': jnp.zeros((NUM_EXPERTS, HIDDEN), dtype=jnp.float32), 'W2': jax.random.normal(ks[3], (NUM_EXPERTS, HIDDEN, D_MODEL), dtype=jnp.float32) * s, 'b2': jnp.zeros((NUM_EXPERTS, D_MODEL), dtype=jnp.float32), 'sW1': jax.random.normal(ks[4], (NUM_SHARED, D_MODEL, HIDDEN), dtype=jnp.float32) * s, 'sb1': jnp.zeros((NUM_SHARED, HIDDEN), dtype=jnp.float32), 'sW2': jax.random.normal(ks[5], (NUM_SHARED, HIDDEN, D_MODEL), dtype=jnp.float32) * s, 'sb2': jnp.zeros((NUM_SHARED, D_MODEL), dtype=jnp.float32)}
    _L1_ffn_all = _L1_ffn_setup()
    _L1_ffn_in = {k: v for k, v in _L1_ffn_all.items() if k in ('rW', 'rb', 'W1', 'b1', 'W2', 'b2', 'sW1', 'sb1', 'sW2', 'sb2')}
    del _L1_ffn_all
    return {'x': x, 'ctx_1024': ctx_1024, 'L0_xattn_Wq': _L0_xattn_in['Wq'], 'L0_xattn_bq': _L0_xattn_in['bq'], 'L0_xattn_Wk': _L0_xattn_in['Wk'], 'L0_xattn_bk': _L0_xattn_in['bk'], 'L0_xattn_Wv': _L0_xattn_in['Wv'], 'L0_xattn_bv': _L0_xattn_in['bv'], 'L0_xattn_Wo': _L0_xattn_in['Wo'], 'L0_xattn_bo': _L0_xattn_in['bo'], 'L0_ffn_Wg': _L0_ffn_in['Wg'], 'L0_ffn_W1': _L0_ffn_in['W1'], 'L0_ffn_b1': _L0_ffn_in['b1'], 'L0_ffn_W2': _L0_ffn_in['W2'], 'L0_ffn_b2': _L0_ffn_in['b2'], 'L0_ffn_W3': _L0_ffn_in['W3'], 'L0_ffn_b3': _L0_ffn_in['b3'], 'L1_xattn_Wq': _L1_xattn_in['Wq'], 'L1_xattn_bq': _L1_xattn_in['bq'], 'L1_xattn_Wk': _L1_xattn_in['Wk'], 'L1_xattn_bk': _L1_xattn_in['bk'], 'L1_xattn_Wv': _L1_xattn_in['Wv'], 'L1_xattn_bv': _L1_xattn_in['bv'], 'L1_xattn_Wp': _L1_xattn_in['Wp'], 'L1_xattn_bp': _L1_xattn_in['bp'], 'L1_ffn_rW': _L1_ffn_in['rW'], 'L1_ffn_rb': _L1_ffn_in['rb'], 'L1_ffn_W1': _L1_ffn_in['W1'], 'L1_ffn_b1': _L1_ffn_in['b1'], 'L1_ffn_W2': _L1_ffn_in['W2'], 'L1_ffn_b2': _L1_ffn_in['b2'], 'L1_ffn_sW1': _L1_ffn_in['sW1'], 'L1_ffn_sb1': _L1_ffn_in['sb1'], 'L1_ffn_sW2': _L1_ffn_in['sW2'], 'L1_ffn_sb2': _L1_ffn_in['sb2']}

def reference(x, ctx_1024, L0_xattn_Wq, L0_xattn_bq, L0_xattn_Wk, L0_xattn_bk, L0_xattn_Wv, L0_xattn_bv, L0_xattn_Wo, L0_xattn_bo, L0_ffn_Wg, L0_ffn_W1, L0_ffn_b1, L0_ffn_W2, L0_ffn_b2, L0_ffn_W3, L0_ffn_b3, L1_xattn_Wq, L1_xattn_bq, L1_xattn_Wk, L1_xattn_bk, L1_xattn_Wv, L1_xattn_bv, L1_xattn_Wp, L1_xattn_bp, L1_ffn_rW, L1_ffn_rb, L1_ffn_W1, L1_ffn_b1, L1_ffn_W2, L1_ffn_b2, L1_ffn_sW1, L1_ffn_sb1, L1_ffn_sW2, L1_ffn_sb2):
    import jax
    import jax.numpy as jnp

    def _L0_xattn_ref(Q, K, V, Wq, bq, Wk, bk, Wv, bv, Wo, bo):
        import jax, jax.numpy as jnp
        import numpy as np
        D_MODEL = 128
        N_HEAD = 16

        def _split_heads(x, n_head):
            B, S, D = x.shape
            return x.reshape(B, S, n_head, D // n_head).transpose(0, 2, 1, 3)
        q = _split_heads(Q @ Wq.T + bq, N_HEAD)
        k = _split_heads(K @ Wk.T + bk, N_HEAD)
        v = _split_heads(V @ Wv.T + bv, N_HEAD)
        d_k = k.shape[-1]
        score = jnp.einsum('bhqd,bhkd->bhqk', q, k) / jnp.sqrt(jnp.float32(d_k))
        attn = jax.nn.softmax(score, axis=-1)
        out = jnp.einsum('bhqk,bhkd->bhqd', attn, v)
        B, H, S, dh = out.shape
        out = out.transpose(0, 2, 1, 3).reshape(B, S, H * dh)
        return out @ Wo.T + bo

    def _L0_ffn_ref(x, Wg, W1, b1, W2, b2, W3, b3):
        import jax, jax.numpy as jnp
        import numpy as np
        B, S, H, DFF, E, K = (2, 256, 128, 256, 8, 2)

        def _moe(x, Wg, W1, b1, W2, b2, W3, b3):
            Bm, Sm, Hm = x.shape
            xt = x.reshape(-1, Hm)
            gout = xt @ Wg.T
            topv, topi = jax.lax.top_k(gout, K)
            w = jax.nn.softmax(topv, axis=-1)
            comb = jnp.einsum('tke,tk->te', jax.nn.one_hot(topi, E, dtype=x.dtype), w)
            g = jnp.einsum('th,efh->etf', xt, W1) + b1[:, None, :]
            v = jnp.einsum('th,efh->etf', xt, W2) + b2[:, None, :]
            h = jax.nn.silu(g) * v
            eo = jnp.einsum('etf,ehf->eth', h, W3) + b3[:, None, :]
            out = jnp.einsum('eth,te->th', eo, comb)
            return out.reshape(Bm, Sm, Hm)
        return _moe(x, Wg, W1, b1, W2, b2, W3, b3)

    def _L1_xattn_ref(x, y, Wq, bq, Wk, bk, Wv, bv, Wp, bp):
        import jax, jax.numpy as jnp
        import numpy as np
        B, T, C, H = (4, 512, 128, 16)
        D = C // H

        def _heads(t):
            b, n, c = t.shape
            return t.reshape(b, n, H, D).transpose(0, 2, 1, 3)
        q = jax.nn.softmax(_heads(x @ Wq.T + bq), axis=-1)
        k = jax.nn.softmax(_heads(y @ Wk.T + bk), axis=-1)
        v = _heads(y @ Wv.T + bv)
        k_cumsum = jnp.sum(k, axis=-2, keepdims=True)
        D_inv = 1.0 / jnp.sum(q * k_cumsum, axis=-1, keepdims=True)
        kv = jnp.einsum('bhnd,bhne->bhde', k, v)
        out = q + jnp.einsum('bhnd,bhde->bhne', q, kv) * D_inv
        out = out.transpose(0, 2, 1, 3).reshape(x.shape[0], x.shape[1], C)
        return out @ Wp.T + bp

    def _L1_ffn_ref(x, rW, rb, W1, b1, W2, b2, sW1, sb1, sW2, sb2):
        import jax, jax.numpy as jnp
        import numpy as np
        D_MODEL = 128
        HIDDEN = 512
        NUM_EXPERTS = 8
        TOP_K = 2
        NUM_SHARED = 2

        def _gelu(x):
            return jax.nn.gelu(x, approximate=False)
        B, L, D = x.shape
        xf = x.reshape(-1, D)
        sh = _gelu(jnp.einsum('td,sdh->sth', xf, sW1) + sb1[:, None, :])
        shared = jnp.einsum('sth,shd->std', sh, sW2) + sb2[:, None, :]
        shared = shared.mean(axis=0)
        gates = xf @ rW + rb
        topk_vals, topk_idx = jax.lax.top_k(gates, TOP_K)
        topk_probs = jax.nn.softmax(topk_vals, axis=-1)
        onehot = topk_idx[:, :, None] == jnp.arange(NUM_EXPERTS)[None, None, :]
        w = jnp.sum(topk_probs[:, :, None] * onehot, axis=1)
        h = _gelu(jnp.einsum('td,edh->eth', xf, W1) + b1[:, None, :])
        y = jnp.einsum('eth,ehd->etd', h, W2) + b2[:, None, :]
        moe = jnp.einsum('te,etd->td', w, y)
        return (shared + moe).reshape(B, L, D)
    x = x + _L0_xattn_ref(_layernorm(x, axis=-1), ctx_1024, ctx_1024, L0_xattn_Wq, L0_xattn_bq, L0_xattn_Wk, L0_xattn_bk, L0_xattn_Wv, L0_xattn_bv, L0_xattn_Wo, L0_xattn_bo)
    x = x + _L0_ffn_ref(_layernorm(x, axis=-1), L0_ffn_Wg, L0_ffn_W1, L0_ffn_b1, L0_ffn_W2, L0_ffn_b2, L0_ffn_W3, L0_ffn_b3)
    x = x + _L1_xattn_ref(_layernorm(x, axis=-1), ctx_1024, L1_xattn_Wq, L1_xattn_bq, L1_xattn_Wk, L1_xattn_bk, L1_xattn_Wv, L1_xattn_bv, L1_xattn_Wp, L1_xattn_bp)
    x = x + _L1_ffn_ref(_layernorm(x, axis=-1), L1_ffn_rW, L1_ffn_rb, L1_ffn_W1, L1_ffn_b1, L1_ffn_W2, L1_ffn_b2, L1_ffn_sW1, L1_ffn_sb1, L1_ffn_sW2, L1_ffn_sb2)
    return x

_drawn_inputs = setup_inputs


def setup_inputs(seed=0):
    import zlib

    import numpy as np

    out = dict(_drawn_inputs(seed))
    spreads = {'L1_xattn_bq': (0.0, 0.571),
     'L1_xattn_bk': (0.0, 2.0),
     'L1_xattn_bv': (0.0, 0.1),
     'L1_xattn_bp': (0.0, 0.1),
     'L1_ffn_rb': (0.0, 0.1),
     'L1_ffn_b1': (0.0, 0.592),
     'L1_ffn_b2': (0.0, 0.1),
     'L1_ffn_sb1': (0.0, 0.589),
     'L1_ffn_sb2': (0.0, 0.1)}
    factors = {'L0_xattn_bq': 2.891, 'L0_xattn_bk': 64.0, 'L0_ffn_b1': 8.0, 'L0_ffn_b2': 8.0}
    for name, (base, spread) in spreads.items():
        noise = np.random.default_rng([zlib.crc32(name.encode()), seed]).standard_normal(out[name].shape)
        drawn = base * np.exp(spread * noise) if base else spread * noise
        out[name] = jnp.asarray(drawn.astype(out[name].dtype))
    for name, factor in factors.items():
        out[name] = (out[name] * factor).astype(out[name].dtype)
    return out
```

```python
import numpy as np
import concourse.bass as bass
from concourse import mybir
from contextlib import ExitStack

F32 = mybir.dt.float32
F32R = mybir.dt.float32r
BF16 = mybir.dt.bfloat16
I32 = mybir.dt.int32
ALU = mybir.AluOpType
ACT = mybir.ActivationFunctionType
AX = mybir.AxisListType

P = 128
NT = 32
NK = 77
H = 16
DH = P // H
HG = 4
NG = H // HG
E = 8
TOPK = 2
NSH = 2
NPAIR = NT * TOPK
NR = NPAIR + E
F0, F1 = 256, 512
UP = 512
W0C = UP + F0
W1C = UP + F1
C0 = E * W0C // NT
C1 = (E + NSH) * W1C // NT
BC = UP + P
ZR = 4
SCALE = float(1.0 / np.sqrt(np.float32(DH)))
EPS = 1e-5
BIG = 3.0e38

K_ID = 0
K_TRI = K_ID + P
K_PAIR = K_TRI + P
K_SAME = K_PAIR + P
K_BD = K_SAME + P
K_H16 = K_BD + P
K_H4 = K_H16 + H
K_REV = K_H4 + HG
K_LT = K_REV + E
K_LE = K_LT + E * E
K_TILE = K_LE + E * E
K_N = K_TILE + NR


def constants():
    c = np.zeros((P, K_N), np.float32)
    i = np.arange(P)
    c[:, K_ID:K_TRI] = np.eye(P)
    c[:, K_TRI:K_PAIR] = i[:, None] < i[None, :]
    same = i[:, None] % E == i[None, :] % E
    c[:, K_PAIR:K_SAME] = same & (i[:, None] // E < i[None, :] // E)
    c[:, K_SAME:K_BD] = same
    c[:, K_BD:K_H16] = i[:, None] // DH == i[None, :] // DH
    c[:, K_H16:K_H4] = i[:, None] // DH == np.arange(H)
    c[:, K_H4:K_REV] = i[:, None] // DH % HG == np.arange(HG)
    e = np.arange(E)
    c[:, K_REV:K_LT] = E - e
    c[:, K_LT:K_LE] = (e[None, :] < e[:, None]).reshape(-1)
    c[:, K_LE:K_TILE] = (e[None, :] <= e[:, None]).reshape(-1)
    c[:, K_TILE:] = np.arange(NR)
    return c


class Tile:

    def __init__(self, j, off):
        self.n = 2 * j + off
        self.half = j + off // 2
        self.par = off % 2
        self.j, self.off = j, off

    def __add__(self, k):
        return Tile(self.j, self.off + k)


def sweep(eng, n, ahead, behind, body):
    first = behind + 2
    first += 1 - first % 2
    last = n - ahead
    last -= (last - first) % 2
    for u in range(-ahead, first):
        body(Tile(0, u), lambda k: 0 <= u + k < n)
    with eng.Fori(first // 2, first // 2 + (last - first) // 2) as j:
        body(Tile(j, 1), lambda k: True)
        body(Tile(j, 2), lambda k: True)
    for u in range(last, n + behind):
        body(Tile(0, u), lambda k: 0 <= u + k < n)


def after(eng, sem, count):
    if isinstance(count, int) and count <= 0:
        return
    eng.wait_ge(sem, count)


def apart(eng, sem):
    eng.sem_inc(sem, 1)


def build(nc, a, out):
    ctx = ExitStack()
    with ctx:
        sems = {}

        def S(name):
            if name not in sems:
                sems[name] = ctx.enter_context(nc.semaphore(name))
            return sems[name]

        def sb(name, shape, dt=F32):
            return ctx.enter_context(nc.sbuf_tensor(name, shape, dt))

        x_sb = sb("x_sb", [P, NT, P])
        xn_sb = sb("xn_sb", [P, NT, P])
        w_hi = sb("w_hi", [P, (E + NSH) * W1C], F32R)
        w_lo = sb("w_lo", [P, (E + NSH) * W1C], F32R)
        w_st = sb("w_st", [P, 2, max(C0, C1)])
        cst = sb("cst", [P, K_N])
        wa = sb("wa", [P, 8, P])
        wr = sb("wr", [P, 2, E])
        qk_col = sb("qk_col", [P, 2])
        bias = sb("bias", [P, 6, P])
        rb = sb("rb", [P, E])
        b_st = xn_sb[0:2 * E + NSH, NT - BC // P:NT, :].rearrange("p t d -> p (t d)")
        b_hi = sb("b_hi", [2 * E + NSH, BC], F32R)
        b_lo = sb("b_lo", [2 * E + NSH, BC], F32R)
        b_row = sb("b_row", [2, (E + NSH) * BC], F32R)
        ones_r = sb("ones_r", [2, P], F32R)
        tri = sb("tri", [P, P], BF16)
        pairm = sb("pairm", [P, P], BF16)
        same = sb("same", [P, P], BF16)
        ones_b = sb("ones_b", [P, 1], BF16)
        half_neg = sb("half_neg", [P, 1])
        zeros = sb("zeros", [P, ZR, P])

        ident = cst[:, K_ID:K_TRI]

        stats = [[sb(f"stats{w}{i}", [P, 6]) for i in range(2)] for w in range(2)]
        meanv = [[sb(f"meanv{w}{i}", [P, 2]) for i in range(2)] for w in range(2)]
        vareps = [[sb(f"vareps{w}{i}", [P, 1]) for i in range(2)] for w in range(2)]
        rstd = [[sb(f"rstd{w}{i}", [P, 1]) for i in range(2)] for w in range(2)]
        xn = [sb(f"xn{i}", [P, P]) for i in range(2)]
        xnT = [sb(f"xnT{i}", [P, P]) for i in range(2)]
        xe = [sb(f"xe{i}", [P, P]) for i in range(2)]
        xeT = [sb(f"xeT{i}", [P, P]) for i in range(2)]
        ctxT = [sb(f"ctxT{i}", [P, P]) for i in range(2)]
        kf = [sb(f"kf{i}", [P, NK]) for i in range(2)]
        kblk = [sb(f"kblk{i}", [P, HG, NK]) for i in range(2)]
        vaug = [sb(f"vaug{i}", [NK, H, DH + 1]) for i in range(2)]
        qT = [sb(f"qT{i}", [P, P]) for i in range(2)]
        smax = [sb(f"smax{i}", [P, HG]) for i in range(2)]
        sm = [sb(f"sm{i}", [P, HG, NK]) for i in range(2)]
        wide = [sb(f"wide{g}", [P, 512]) for g in range(NG)]
        pT = [w[0:NK, :].rearrange("k (h q) -> k h q", h=HG) for w in wide]
        rden = [sb(f"rden{i}", [P, H]) for i in range(2)]
        oraw = [sb(f"oraw{i}", [P, P]) for i in range(2)]
        o = [sb(f"o{i}", [P, P]) for i in range(2)]
        oT = [sb(f"oT{i}", [P, P]) for i in range(2)]
        qkv = [wide[i][:, 0:3 * P + 1] for i in range(2)]
        fmax = [sb(f"fmax{i}", [P, 2 * H]) for i in range(2)]
        fsub = [wide[2 + i][:, 0:2 * P] for i in range(2)]
        fexp = [wide[2 + i][:, 2 * P:4 * P] for i in range(2)]
        fsum = [sb(f"fsum{i}", [P, 2 * H]) for i in range(2)]
        frec = [sb(f"frec{i}", [P, 2 * H]) for i in range(2)]
        fsm = [sb(f"fsm{i}", [P, 2 * P]) for i in range(2)]
        kvm = [s_[:].rearrange("p h k -> p (h k)")[:, 0:P + H] for s_ in sm]
        qsT = [k_[:].rearrange("p h k -> p (h k)")[:, 0:P] for k_ in kblk]
        yg = [sb(f"yg{i}", [P, TOPK, P]) for i in range(2)]
        idx = [sb(f"idx{i}", [P, TOPK], I32) for i in range(2)]

        lg = sb("lg", [P, NT, E])
        lg2 = wide[2][:, 0:NT * E].rearrange("p (t e) -> p t e", e=E)
        eqs = wide[2][:, NT * E:2 * NT * E].rearrange("p (t e) -> p t e", e=E)
        top = sb("top", [P, TOPK, NT])
        first = sb("first", [P, TOPK, NT])
        oh = sb("oh", [P, NT, TOPK, E], BF16)
        delta = sb("delta", [P, NT])
        exd = sb("exd", [P, NT])
        wsum = sb("wsum", [P, NT])
        gate = sb("gate", [P, NT, TOPK])
        csum = sb("csum", [P, 4, P], BF16)
        cnt = sb("cnt", [P, E])
        cnt_i = sb("cnt_i", [P, E], I32)
        til_i = sb("til_i", [P, E], I32)
        til = sb("til", [P, E])
        tmp64 = sb("tmp64", [P, 2, E, E])
        t_start = sb("t_start", [P, E])
        t_end = sb("t_end", [P, E])
        row0 = sb("row0", [P, E])
        posn = wide[3][:].rearrange("p (c e) -> p c e", e=E)
        slot = sb("slot", [P, NPAIR])
        slot_i = sb("slot_i", [P, NPAIR], I32)
        ecmp = sb("ecmp", [1, NR, E])
        eacc = sb("eacc", [1, NR])
        e_i = sb("e_i", [1, NR], I32)

        xr = qT
        xh = [sb(f"xh{i}", [P, P], F32R) for i in range(2)]
        xl = [sb(f"xl{i}", [P, P], F32R) for i in range(2)]
        hs = [wide[2 + i][:, 0:F0] for i in range(2)]
        hh = [wide[i] for i in range(2)]
        hTh = [sb(f"hTh{i}", [P, F1], F32R) for i in range(2)]
        hTl = [sb(f"hTl{i}", [P, F1], F32R) for i in range(2)]
        ysb = oraw

        bank = [ctx.enter_context(nc.psum_tensor(f"bank{i}", [P, 512], F32)) for i in range(8)]

        xs_dram = nc.dram_tensor("xs_sorted", (NR * P, P), F32).ap()
        ys_dram = nc.dram_tensor("ys_sorted", (NR * P, P), F32).ap()

        block = ctx.enter_context(nc.Block())

        SWEEPS = [dict(l=0, n=NR, f=F0, shared=None, base=0),
                  dict(l=1, n=NT, f=F1, shared=0, base=NR),
                  dict(l=1, n=NT, f=F1, shared=1, base=NR + NT),
                  dict(l=1, n=NR, f=F1, shared=None, base=NR + 2 * NT)]
        for s in SWEEPS:
            assert s["base"] % 2 == 0

        def cols(s):
            return W0C if s["l"] == 0 else W1C

        @block.sync
        def _(sp):
            sp.dma_start(cst[:], a["cst"]).then_inc(S("cst_in"), 16)
            sp.dma_start(x_sb[:, 0:2, :], a["x"][0:2].rearrange("b s d -> s b d")).then_inc(S("x_in0"), 16)
            for i, n in enumerate(("wq0", "wk0", "wv0", "wo0", "wq1", "wk1", "wv1", "wp1")):
                sp.dma_start(wa[:, i, :], a[n]).then_inc(S("wa_in"), 16)
            sp.dma_start(wr[:, 0, :], a["wr0"]).then_inc(S("wa_in"), 16)
            sp.dma_start(wr[:, 1, :], a["wr1"]).then_inc(S("wa_in"), 16)
            for i, n in enumerate(("bq0", "bk0")):
                sp.dma_start(qk_col[:, i:i + 1], a[n].rearrange("(p o) -> p o", o=1)).then_inc(S("bias_in"), 16)
            for i, n in enumerate(("bv0", "bo0", "bq1", "bk1", "bv1", "bp1")):
                sp.dma_start(bias[:, i, :], a[n].partition_broadcast(P)).then_inc(S("bias_in"), 16)
            sp.dma_start(rb[:], a["rb"].partition_broadcast(P)).then_inc(S("bias_in"), 16)
            sp.dma_start(x_sb[:, 2:NT, :], a["x"][2:NT].rearrange("b s d -> s b d")).then_inc(S("x_in"), 16)
            sp.dma_start(b_st[0:E, :], a["eb0"]).then_inc(S("b_in"), 16)
            sp.dma_start(b_st[E:, :], a["eb1"]).then_inc(S("b_in"), 16)

            sp.wait_ge(S("zeros_set"), 1)
            for r in range(0, NR * P, ZR * P):
                sp.dma_start(xs_dram[r:r + ZR * P, :].rearrange("(p r) d -> p r d", r=ZR), zeros[:])\
                    .then_inc(S("xs_zeroed"), 16)

            def bias_rows(l, n):
                sp.dma_start(b_row[0:1, 0:n * BC].bitcast(F32), b_hi[l * E:l * E + n, :].bitcast(F32)).then_inc(S("b_row_in"), 16)
                sp.dma_start(b_row[1:2, 0:n * BC].bitcast(F32), b_lo[l * E:l * E + n, :].bitcast(F32)).then_inc(S("b_row_in"), 16)

            sp.wait_ge(S("b_split"), 2)
            bias_rows(0, E)

            def feed(l, wsrc, c, done):
                def body(u, live):
                    if live(1):
                        t = u + 1
                        after(sp, S(done), t.n - 1)
                        sp.dma_start(ctxT[t.par][:, 0:NK], a["ctxT"][bass.ds(t.n, 1)].rearrange("o d k -> d (o k)"))\
                            .then_inc(S(f"ctx_in{l}{t.par}"), 16)
                    if live(0):
                        after(sp, S(f"w_split{l}"), u.n - 1)
                        sp.dma_start(w_st[:, u.par, 0:c], wsrc[:, bass.ds(u.n * c, c)])\
                            .then_inc(S(f"w_in{l}{u.par}"), 16)
                sweep(sp, NT, 1, 0, body)

            def rows(s):
                def body(u, live):
                    if live(2):
                        t = u + 2
                        after(sp, S("xT_done"), s["base"] + t.n - 1)
                        sp.dma_start(xr[t.par][:], xs_dram[bass.ds(t.n * P, P), :])\
                            .then_inc(S(f"xr_in{s['l']}{t.par}"), 16)
                    if live(-3):
                        t = u + -3
                        sp.wait_ge(S("y_ready"), s["base"] + t.n + 1)
                        sp.dma_start(ys_dram[bass.ds(t.n * P, P), :], ysb[t.par][:])\
                            .then_inc(S(f"y_out{s['l']}{t.par}"), 16)
                sweep(sp, s["n"], 2, 3, body)

            feed(0, a["w0"], C0, "kv0_done")
            for k in range(4):
                sp.wait_ge(S(f"rows0{k}"), 2 * 16 * (NT // 4))
            rows(SWEEPS[0])
            sp.wait_ge(S("y_out00"), 16 * NR // 2)
            sp.wait_ge(S("y_out01"), 16 * NR // 2)
            bias_rows(1, E + NSH)
            feed(1, a["w1"], C1, "kv1_done")
            for k in range(4):
                sp.wait_ge(S(f"rows1{k}"), 2 * 16 * (NT // 4))
            rows(SWEEPS[3])
            sp.wait_ge(S("y_out10"), 16 * NR // 2)
            sp.wait_ge(S("y_out11"), 16 * NR // 2)

            def store(u, live):
                sp.wait_ge(S("x_final"), u.n + 1)
                sp.dma_start(out[bass.ds(u.n, 1)].rearrange("o s d -> s (o d)"),
                             x_sb[:, bass.ds(u.n, 1), :].rearrange("p o d -> p (o d)")).then_inc(S("stored"), 16)
            sweep(sp, NT, 0, 0, store)
            sp.wait_ge(S("stored"), 16 * NT)

        @block.gpsimd
        def _(pool):
            g = nc.gpsimd
            g.memset(zeros[:], 0.0).then_inc(S("zeros_set"), 1)
            g.memset(half_neg[:], -0.5).then_inc(S("pool_const"), 1)
            for i in range(2):
                g.memset(vaug[i][:, :, DH:DH + 1], 1.0).then_inc(S("pool_const"), 1)
                g.memset(ctxT[i][:, NK:P], 0.0).then_inc(S("pool_const"), 1)
            pool.wait_ge(S("pool_const"), 5)
            pool.wait_ge(S("bias_in"), 16 * 9)
            pool.wait_ge(S("cst_in"), 16)
            pool.wait_ge(S("b_in"), 32)
            g.tensor_copy(b_hi[:], b_st).then_inc(S("b_split"), 1)
            pool.wait_ge(S("b_split"), 1)
            g.tensor_tensor(b_lo[:], b_st, b_hi[:].bitcast(F32), ALU.subtract).then_inc(S("b_split"), 1)

            def inverse_std(tag, w, t):
                pool.wait_ge(S(f"{tag}_var"), t.n + 1)
                apart(pool, S("pool_apart"))
                g.tensor_scalar(vareps[w][t.par][:], meanv[w][t.par][:, 1:2], EPS, None, ALU.add)\
                    .then_inc(S(f"{tag}_eps"), 1)
                pool.wait_ge(S(f"{tag}_eps"), t.n + 1)
                g.tensor_tensor(rstd[w][t.par][:], vareps[w][t.par][:], half_neg[:], ALU.pow)\
                    .then_inc(S(f"{tag}_rstd"), 1)

            def split_weights(l, c, t):
                pool.wait_ge(S(f"w_in{l}{t.par}"), 16 * (t.half + 1))
                g.tensor_copy(w_hi[:, bass.ds(t.n * c, c)], w_st[:, t.par, 0:c]).then_inc(S(f"w_half{l}"), 1)
                pool.wait_ge(S(f"w_half{l}"), t.n + 1)
                g.tensor_tensor(w_lo[:, bass.ds(t.n * c, c)], w_st[:, t.par, 0:c],
                                w_hi[:, bass.ds(t.n * c, c)].bitcast(F32), ALU.subtract)\
                    .then_inc(S(f"w_split{l}"), 1)

            def residual_bias(l, b, normed, t):
                pool.wait_ge(S(normed), t.n + 1)
                xt = x_sb[:, bass.ds(t.n, 1), :].rearrange("p o d -> p (o d)")
                g.tensor_tensor(xt, xt, bias[:, b, :], ALU.add).then_inc(S(f"x_bias{l}"), 1)

            def attention0(u, live):
                if live(-1):
                    t = u + -1
                    pool.wait_ge(S("o_raw0"), t.n + 1)
                    after(pool, S("oT_done0"), t.n - 1)
                    g.tensor_tensor(o[t.par][:], oraw[t.par][:], bias[:, 0, :], ALU.add).then_inc(S("o_ready0"), 1)
                if live(0):
                    residual_bias(0, 1, "xn_ready0", u)
                if live(2):
                    inverse_std("ln0", 0, u + 2)
                if live(-1):
                    inverse_std("lne0", 1, u + -1)
                if live(1):
                    t = u + 1
                    pool.wait_ge(S("kf_ready"), t.n + 1)
                    after(pool, S("s_done"), NG * (t.n - 1))
                    g.tensor_tensor(kblk[t.par][:], kf[t.par][:].unsqueeze(1).to_broadcast([P, HG, NK]),
                                    cst[:, K_H4:K_REV].unsqueeze(2).to_broadcast([P, HG, NK]), ALU.mult)\
                        .then_inc(S("kblk_ready"), 1)
                if live(0):
                    split_weights(0, C0, u)
            sweep(pool, NT, 2, 1, attention0)

            def scatter(l):
                pool.wait_ge(S("slots"), l + 1)
                if l == 0:
                    pool.wait_ge(S("xs_zeroed"), 16 * (NR // ZR))

                def turn_of_four(j):
                    for k in range(4):
                        t = 4 * j + k
                        after(pool, S(f"rows{l}{k}"), 32 * j)
                        src = [xn, xnT][k // 2][k % 2]
                        ix = sidx[k]
                        g.tensor_copy(src[:], xn_sb[:, bass.ds(t, 1), :].rearrange("p o d -> p (o d)"))\
                            .then_inc(S(f"sc_copy{l}"), 1)
                        g.tensor_copy(ix[:], slot_i[:, bass.ds(TOPK * t, TOPK)]).then_inc(S(f"sc_copy{l}"), 1)
                        pool.wait_ge(S(f"sc_copy{l}"), 2 * (t + 1))
                        apart(pool, S("pool_apart"))
                        for c in range(TOPK):
                            g.indirect_dma_start(xs_dram, bass.IndirectOffsetOnAxis(ap=ix[:, c:c + 1], axis=0),
                                                 src[:], None).then_inc(S(f"rows{l}{k}"), 16)
                turn_of_four(0)
                with pool.Fori(1, NT // 4) as j:
                    turn_of_four(j)

            sidx = [sb(f"sidx{k}", [P, TOPK], I32) for k in range(4)]

            def gather(l, t):
                after(pool, S(("combined0", "x_final")[l]), t.n - 1)
                g.tensor_copy(idx[t.par][:], slot_i[:, bass.ds(TOPK * t.n, TOPK)]).then_inc(S(f"ga_idx{l}"), 1)
                pool.wait_ge(S(f"ga_idx{l}"), t.n + 1)
                apart(pool, S("pool_apart"))
                for c in range(TOPK):
                    g.indirect_dma_start(yg[t.par][:, c, :], None, ys_dram,
                                         bass.IndirectOffsetOnAxis(ap=idx[t.par][:, c:c + 1], axis=0))\
                        .then_inc(S(f"yg_in{l}{t.par}"), 16)

            scatter(0)
            for p in range(2):
                pool.wait_ge(S(f"y_out0{p}"), 16 * NR // 2)

            for i in range(2):
                g.memset(qkv[i][:, 3 * P:3 * P + 1], 1.0).then_inc(S("v_ones"), 1)

            def attention1(u, live):
                if live(3):
                    gather(0, u + 3)
                if live(-1):
                    t = u + -1
                    pool.wait_ge(S("o_raw1"), t.n + 1)
                    after(pool, S("oT_done1"), t.n - 1)
                    g.tensor_tensor(o[t.par][:], oraw[t.par][:], fsm[t.par][:, 0:P], ALU.add)\
                        .then_inc(S("o_ready1"), 1)
                if live(2):
                    inverse_std("ln1", 0, u + 2)
                if live(0):
                    residual_bias(1, 5, "xn_ready1", u)
                if live(1):
                    t = u + 1
                    pool.wait_ge(S("f_max"), t.n + 1)
                    after(pool, S("f_exp"), t.n - 1)
                    g.tensor_tensor(fsub[t.par][:].rearrange("p (h d) -> p h d", d=DH),
                                    qkv[t.par][:, 0:2 * P].rearrange("p (h d) -> p h d", d=DH),
                                    fmax[t.par][:].unsqueeze(2).to_broadcast([P, 2 * H, DH]), ALU.subtract)\
                        .then_inc(S("f_sub"), 1)
                if live(-1):
                    inverse_std("lne1", 1, u + -1)
                if live(0):
                    split_weights(1, C1, u)
            sweep(pool, NT, 3, 2, attention1)
            scatter(1)

            for p in range(2):
                pool.wait_ge(S(f"y_out1{p}"), 16 * NR // 2)
            sweep(pool, NT, 0, 0, lambda u, live: gather(1, u))

        @block.scalar
        def _(act):
            s_ = nc.scalar
            act.wait_ge(S("bias_in"), 16 * 9)
            act.wait_ge(S("pool_const"), 5)

            def copy_out(dst, src):
                return s_.activation(dst, src, ACT.Copy)

            def attention0(u, live):
                def exps(gr):
                    G = NG * u.n + gr
                    act.wait_ge(S("t_done"), G + 1)
                    after(act, S("pv_done"), G - NG + 1)
                    s_.activation(pT[gr][:], bank[2 + gr % 2][0:NK, :].rearrange("k (h q) -> k h q", h=HG),
                                  ACT.Exp, scale=SCALE).then_inc(S("exp_done"), 1)
                if live(-1):
                    t = u + -1
                    act.wait_ge(S("oT_done0"), t.n + 1)
                    copy_out(oT[t.par][:], bank[7][:, 0:P]).then_inc(S("oT_ready0"), 1)
                if live(0):
                    exps(0)
                    exps(1)
                    exps(2)
                if live(1):
                    t = u + 1
                    act.wait_ge(S("kv0_done"), t.n + 1)
                    after(act, S("qT_done"), t.n - 1)
                    copy_out(xnT[t.par][:], bank[4][:, 0:P]).then_inc(S("xnT_ready0"), 1)
                    after(act, S("kblk_ready"), t.n - 1)
                    s_.activation(kf[t.par][:], bank[4][:, P:P + NK], ACT.Identity, bias=qk_col[:, 1:2])\
                        .then_inc(S("kf_ready"), 1)
                    after(act, S("pv_done"), NG * (t.n - 1))
                    copy_out(vaug[t.par][:, :, 0:DH], bank[4][0:NK, 2 * P:3 * P].rearrange("k (h d) -> k h d", d=DH))\
                        .then_inc(S("vaug_ready"), 1)
                if live(0):
                    exps(3)
                if live(1):
                    t = u + 1
                    act.wait_ge(S("qT_done"), t.n + 1)
                    after(act, S("s_done"), NG * (t.n - 1))
                    s_.activation(qT[t.par][:], bank[5][:, 0:P], ACT.Identity, bias=qk_col[:, 0:1])\
                        .then_inc(S("qT_ready"), 1)
                if live(-1):
                    t = u + -1
                    act.wait_ge(S("xeT_done0"), t.n + 1)
                    copy_out(xeT[t.par][:], bank[7][:, 0:P]).then_inc(S("xeT_ready0"), 1)
            sweep(act, NT, 1, 1, attention0)

            def gate_exp(l):
                act.wait_ge(S("delta"), l + 1)
                s_.activation(exd[:], delta[:], ACT.Exp).then_inc(S("exd"), 1)

            def experts(s):
                b, nf = s["base"], s["f"]

                def body(u, live):
                    if live(0):
                        act.wait_ge(S("up_done"), b + u.n + 1)
                        if s["l"] == 0:
                            after(act, S("h_ready"), b + u.n - 1)
                            s_.activation(hs[u.par][:], bank[u.par][:, 0:F0], ACT.Silu).then_inc(S("silu_done"), 1)
                        else:
                            after(act, S("hT_done"), b + u.n - 1)
                            s_.activation(hh[u.par][:], bank[u.par][:], ACT.Gelu).then_inc(S("h_ready"), 1)
                    if live(-1):
                        t = u + -1
                        act.wait_ge(S("hT_done"), b + t.n + 1)
                        after(act, S("down_done"), b + t.n - 1)
                        copy_out(hTh[t.par][:, 0:nf], bank[2 + t.par][:, 0:nf]).then_inc(S("hTh_ready"), 1)
                    if live(1):
                        t = u + 1
                        act.wait_ge(S("xT_done"), b + t.n + 1)
                        after(act, S("up_done"), b + t.n - 1)
                        copy_out(xh[t.par][:], bank[6][:, 0:P]).then_inc(S("xh_ready"), 1)
                sweep(act, s["n"], 1, 1, body)

            gate_exp(0)
            experts(SWEEPS[0])

            def attention1(u, live):
                if live(0):
                    act.wait_ge(S("f_sub"), u.n + 1)
                    after(act, S("f_soft"), u.n - 1)
                    s_.activation(fexp[u.par][:], fsub[u.par][:], ACT.Exp).then_inc(S("f_exp"), 1)
                if live(1):
                    t = u + 1
                    act.wait_ge(S("xnT_done1"), t.n + 1)
                    after(act, S("kv1_done"), t.n - 1)
                    copy_out(xnT[t.par][:], bank[0][:, 0:P]).then_inc(S("xnT_ready1"), 1)
                if live(-2):
                    t = u + -2
                    act.wait_ge(S("xeT_done1"), t.n + 1)
                    copy_out(xeT[t.par][:], bank[7][:, 0:P]).then_inc(S("xeT_ready1"), 1)
                if live(0):
                    act.wait_ge(S("qsT_done"), u.n + 1)
                    after(act, S("num_done"), u.n - 1)
                    copy_out(qsT[u.par][:], bank[3][:, 0:P]).then_inc(S("qsT_ready"), 1)
                if live(-1):
                    t = u + -1
                    act.wait_ge(S("oT_done1"), t.n + 1)
                    after(act, S("proj_done1"), t.n - 1)
                    copy_out(oT[t.par][:], bank[5][:, 0:P]).then_inc(S("oT_ready1"), 1)
            sweep(act, NT, 1, 2, attention1)
            gate_exp(1)
            for s in SWEEPS[1:]:
                experts(s)

        @block.vector
        def _(dve):
            v = nc.vector
            dve.wait_ge(S("cst_in"), 16)
            v.tensor_copy(tri[:], cst[:, K_TRI:K_PAIR]).then_inc(S("dve_const"), 1)
            v.tensor_copy(pairm[:], cst[:, K_PAIR:K_SAME]).then_inc(S("dve_const"), 1)
            v.tensor_copy(same[:], cst[:, K_SAME:K_BD]).then_inc(S("dve_const"), 1)
            v.memset(ones_b[:], 1.0).then_inc(S("dve_const"), 1)
            v.tensor_scalar(ones_r[:], cst[0:2, K_ID:K_TRI], 0.0, 1.0, ALU.mult, ALU.add).then_inc(S("dve_const"), 1)
            dve.wait_ge(S("bias_in"), 16 * 9)
            dve.wait_ge(S("pool_const"), 5)

            def xt(t):
                return x_sb[:, bass.ds(t.n, 1), :].rearrange("p o d -> p (o d)")

            def ln_stats(tag, w, t):
                apart(dve, S("dve_apart"))
                v.bn_stats(stats[w][t.par][:], xt(t)).then_inc(S(f"{tag}_stats"), 1)
                dve.wait_ge(S(f"{tag}_stats"), t.n + 1)
                apart(dve, S("dve_apart"))
                v.bn_aggr(meanv[w][t.par][:], stats[w][t.par][:]).then_inc(S(f"{tag}_var"), 1)

            def ln_apply(tag, w, t, dst):
                dve.wait_ge(S(f"{tag}_rstd"), t.n + 1)
                return v.tensor_scalar(dst, xt(t), meanv[w][t.par][:, 0:1], rstd[w][t.par][:],
                                       ALU.subtract, ALU.mult)

            def expert_input(l, t):
                after(dve, S(f"xeT_done{l}"), t.n - 1)
                ln_apply(f"lne{l}", 1, t, xe[t.par][:]).then_inc(S(f"xe_ready{l}"), 1)
                v.tensor_scalar(xn_sb[:, bass.ds(t.n, 1), :].rearrange("p o d -> p (o d)"), xt(t),
                                meanv[1][t.par][:, 0:1], rstd[1][t.par][:], ALU.subtract, ALU.mult)\
                    .then_inc(S(f"xn_kept{l}"), 1)

            def add_projection(l, bnk, t):
                dve.wait_ge(S(f"proj_done{l}"), t.n + 1)
                dve.wait_ge(S(f"x_bias{l}"), t.n + 1)
                v.tensor_tensor(xt(t), xt(t), bnk, ALU.add).then_inc(S(f"x_added{l}"), 1)
                dve.wait_ge(S(f"x_added{l}"), t.n + 1)

            def attention0(u, live):
                def scores(gr):
                    G = NG * u.n + gr
                    sc = bank[gr % 2][:, 0:HG * NK].rearrange("q (h k) -> q h k", h=HG)
                    dve.wait_ge(S("s_done"), G + 1)
                    v.reduce_max(smax[gr % 2][:], sc, AX.X).then_inc(S("s_max"), 1)
                    dve.wait_ge(S("s_max"), G + 1)
                    after(dve, S("t_done"), G - 1)
                    v.tensor_tensor(sm[gr % 2][:], sc, smax[gr % 2][:].unsqueeze(2).to_broadcast([P, HG, NK]),
                                    ALU.subtract).then_inc(S("s_sub"), 1)
                if live(-1):
                    t = u + -1
                    ov = bank[6][:, 0:H * (DH + 1)].rearrange("q (h d) -> q h d", h=H)
                    dve.wait_ge(S("pv_done"), NG * (t.n + 1))
                    v.reciprocal(rden[t.par][:], ov[:, :, DH]).then_inc(S("rden0"), 1)
                    dve.wait_ge(S("rden0"), t.n + 1)
                    after(dve, S("o_ready0"), t.n - 1)
                    v.tensor_tensor(oraw[t.par][:].rearrange("q (h d) -> q h d", h=H), ov[:, :, 0:DH],
                                    rden[t.par][:].unsqueeze(2).to_broadcast([P, H, DH]), ALU.mult)\
                        .then_inc(S("o_raw0"), 1)
                if live(0):
                    scores(0)
                    scores(1)
                if live(2):
                    t = u + 2
                    if isinstance(t.n, int) and t.n == 0:
                        dve.wait_ge(S("x_in0"), 16)
                    if isinstance(t.n, int) and t.n == 2:
                        dve.wait_ge(S("x_in"), 16)
                    ln_stats("ln0", 0, t)
                if live(0):
                    scores(2)
                if live(-1):
                    t = u + -1
                    add_projection(0, bank[7][:, P:2 * P], t)
                    ln_stats("lne0", 1, t)
                if live(0):
                    scores(3)
                if live(2):
                    t = u + 2
                    after(dve, S("kv0_done"), t.n - 1)
                    ln_apply("ln0", 0, t, xn[t.par][:]).then_inc(S("xn_ready0"), 1)
                if live(-1):
                    t = u + -1
                    expert_input(0, t)
                    dve.wait_ge(S("logit_done0"), t.n + 1)
                    v.tensor_copy(lg[:, bass.ds(t.n, 1), :].rearrange("p o e -> p (o e)"), bank[7][:, 2 * P:2 * P + E])\
                        .then_inc(S("lg_ready0"), 1)
            sweep(dve, NT, 2, 1, attention0)

            def route(l):
                count = [0]
                link_sem = S(f"route{l}")

                def link(ins):
                    count[0] += 1
                    ins.then_inc(link_sem, 1)
                    dve.wait_ge(link_sem, count[0])

                def over_e(ap):
                    return ap.unsqueeze(2).to_broadcast([P, NT, E])

                rev = cst[:, K_REV:K_LT].unsqueeze(1).to_broadcast([P, NT, E])
                dve.wait_ge(S(f"lg_ready{l}"), NT)
                src = lg
                for c in range(TOPK):
                    link(v.reduce_max(top[:, c, :], src[:], AX.X))
                    link(v.tensor_tensor(eqs[:], src[:], over_e(top[:, c, :]), ALU.is_equal))
                    link(v.tensor_tensor(eqs[:], eqs[:], rev, ALU.mult))
                    link(v.reduce_max(first[:, c, :], eqs[:], AX.X))
                    link(v.tensor_tensor(oh[:, :, c, :], rev, over_e(first[:, c, :]), ALU.is_equal))
                    if c == 0:
                        link(v.tensor_scalar(eqs[:], oh[:, :, 0, :], -BIG, None, ALU.mult))
                        link(v.tensor_tensor(lg2[:], eqs[:], lg[:], ALU.add))
                        src = lg2
                v.tensor_tensor(delta[:], top[:, 1, :], top[:, 0, :], ALU.subtract).then_inc(S("delta"), 1)
                dve.wait_ge(S("colsum"), l + 1)
                link(v.tensor_copy(csum[:], bank[7][:, 0:4].unsqueeze(2).to_broadcast([P, 4, P])))
                v.tensor_copy(ones_b[:], ones_b[:]).then_inc(S("csum"), 1)
                dve.wait_ge(S("counts"), l + 1)
                link(v.tensor_scalar(cnt[:], bank[7][:, 16:16 + E], float(P - 1), None, ALU.add))
                link(v.tensor_copy(cnt_i[:], cnt[:]))
                link(v.tensor_single_scalar(til_i[:], cnt_i[:], 7, ALU.arith_shift_right))
                link(v.tensor_copy(til[:], til_i[:]))
                tb = til[:].unsqueeze(1).to_broadcast([P, E, E])
                for i, (k, dst) in enumerate(((K_LT, t_start), (K_LE, t_end))):
                    link(v.tensor_tensor(tmp64[:, i], tb, cst[:, k:k + E * E].rearrange("p (a b) -> p a b", a=E),
                                         ALU.mult))
                    link(v.reduce_sum(dst[:], tmp64[:, i], AX.X))
                link(v.tensor_scalar(row0[:], t_start[:], float(P), None, ALU.mult))
                link(v.tensor_tensor(posn[:], bank[5][:].rearrange("p (c e) -> p c e", e=E),
                                     row0[:].unsqueeze(1).to_broadcast([P, NPAIR, E]), ALU.add))
                link(v.tensor_tensor(posn[:], posn[:], oh[:].rearrange("p t c e -> p (t c) e"), ALU.mult))
                link(v.reduce_sum(slot[:], posn[:], AX.X))
                v.tensor_copy(slot_i[:], slot[:]).then_inc(S("slots"), 1)
                link(v.tensor_tensor(ecmp[:], t_end[0:1, :].unsqueeze(1).to_broadcast([1, NR, E]),
                                     cst[0:1, K_TILE:K_TILE + NR].unsqueeze(2).to_broadcast([1, NR, E]), ALU.is_le))
                link(v.reduce_sum(eacc[:], ecmp[:], AX.X))
                link(v.tensor_scalar(eacc[:], eacc[:], float(E - 1), None, ALU.min))
                v.tensor_copy(e_i[:], eacc[:]).then_inc(S("emap"), 1)
                dve.wait_ge(S("exd"), l + 1)
                link(v.tensor_scalar(wsum[:], exd[:], 1.0, None, ALU.add))
                link(v.reciprocal(gate[:, :, 0], wsum[:]))
                link(v.tensor_tensor(gate[:, :, 1], exd[:], gate[:, :, 0], ALU.mult))

            def experts(s):
                b, nf = s["base"], s["f"]

                def body(u, live):
                    if live(0) and s["l"] == 0:
                        dve.wait_ge(S("silu_done"), b + u.n + 1)
                        after(dve, S("hT_done"), b + u.n - 1)
                        v.tensor_tensor(hh[u.par][:, 0:F0], hs[u.par][:], bank[u.par][:, F0:2 * F0], ALU.mult)\
                            .then_inc(S("h_ready"), 1)
                    if live(-1):
                        t = u + -1
                        dve.wait_ge(S("hTh_ready"), b + t.n + 1)
                        v.tensor_tensor(hTl[t.par][:, 0:nf], bank[2 + t.par][:, 0:nf], hTh[t.par][:, 0:nf].bitcast(F32),
                                        ALU.subtract).then_inc(S("hTl_ready"), 1)
                    if live(1):
                        t = u + 1
                        dve.wait_ge(S("xh_ready"), b + t.n + 1)
                        v.tensor_tensor(xl[t.par][:], bank[6][:, 0:P], xh[t.par][:].bitcast(F32), ALU.subtract)\
                            .then_inc(S("xl_ready"), 1)
                    if live(2) and s["shared"] is not None:
                        t = u + 2
                        after(dve, S("xT_done"), b + t.n - 1)
                        v.tensor_copy(xr[t.par][:], xn_sb[:, bass.ds(t.n, 1), :].rearrange("p o d -> p (o d)"))\
                            .then_inc(S("xr_copied"), 1)
                    if live(-2):
                        t = u + -2
                        dve.wait_ge(S("down_done"), b + t.n + 1)
                        if s["shared"] is not None:
                            v.scalar_tensor_tensor(xt(t), bank[4 + t.par][:, 0:P], 1.0 / NSH, xt(t), ALU.mult, ALU.add)\
                                .then_inc(S("y_ready"), 1)
                        else:
                            after(dve, S(f"y_out{s['l']}{t.par}"), 16 * t.half)
                            v.tensor_copy(ysb[t.par][:], bank[4 + t.par][:, 0:P]).then_inc(S("y_ready"), 1)
                sweep(dve, s["n"], 2, 2, body)

            def combine(l, t, done):
                dve.wait_ge(S(f"yg_in{l}{t.par}"), 32 * (t.half + 1))
                for c in range(TOPK):
                    v.scalar_tensor_tensor(xt(t), yg[t.par][:, c, :], gate[:, bass.ds(t.n, 1), c], xt(t),
                                           ALU.mult, ALU.add).then_inc(S(f"comb{l}" if c == 0 else done), 1)
                    dve.wait_ge(S(f"comb{l}" if c == 0 else done), t.n + 1)

            route(0)
            experts(SWEEPS[0])

            def attention1(u, live):
                if live(-1):
                    t = u + -1
                    dve.wait_ge(S("num_done"), t.n + 1)
                    v.reciprocal(rden[t.par][:], bank[4][:, P:P + H]).then_inc(S("rden1"), 1)
                    dve.wait_ge(S("rden1"), t.n + 1)
                    after(dve, S("o_ready1"), t.n - 1)
                    v.tensor_tensor(oraw[t.par][:].rearrange("q (h d) -> q h d", h=H),
                                    bank[4][:, 0:P].rearrange("q (h d) -> q h d", h=H),
                                    rden[t.par][:].unsqueeze(2).to_broadcast([P, H, DH]), ALU.mult)\
                        .then_inc(S("o_raw1"), 1)
                if live(2):
                    t = u + 2
                    combine(0, t, "combined0")
                    ln_stats("ln1", 0, t)
                if live(0):
                    fe = fexp[u.par][:].rearrange("p (h d) -> p h d", d=DH)
                    dve.wait_ge(S("f_exp"), u.n + 1)
                    v.reduce_sum(fsum[u.par][:], fe, AX.X).then_inc(S("f_sum"), 1)
                    dve.wait_ge(S("f_sum"), u.n + 1)
                    v.reciprocal(frec[u.par][:], fsum[u.par][:]).then_inc(S("f_rec"), 1)
                    dve.wait_ge(S("f_rec"), u.n + 1)
                    after(dve, S("o_ready1"), u.n - 1)
                    after(dve, S("qsT_done"), u.n - 1)
                    v.tensor_tensor(fsm[u.par][:].rearrange("p (h d) -> p h d", d=DH), fe,
                                    frec[u.par][:].unsqueeze(2).to_broadcast([P, 2 * H, DH]), ALU.mult)\
                        .then_inc(S("f_soft"), 1)
                if live(-2):
                    expert_input(1, u + -2)
                if live(0):
                    dve.wait_ge(S("kvp_done"), u.n + 1)
                    after(dve, S("num_done"), u.n - 1)
                    v.tensor_tensor(kvm[u.par][:, 0:P], bank[2][:, 0:P], cst[:, K_BD:K_H16], ALU.mult)\
                        .then_inc(S("kvm_ready"), 1)
                    v.tensor_scalar(kvm[u.par][:, P:P + H], cst[:, K_H16:K_H4], bank[2][:, P:P + 1], None, ALU.mult)\
                        .then_inc(S("kvm_ready"), 1)
                if live(2):
                    t = u + 2
                    after(dve, S("xnT_done1"), t.n - 1)
                    ln_apply("ln1", 0, t, xn[t.par][:]).then_inc(S("xn_ready1"), 1)
                if live(1):
                    t = u + 1
                    dve.wait_ge(S("kv1_done"), t.n + 1)
                    after(dve, S("f_sub"), t.n - 1)
                    after(dve, S("kvp_done"), t.n - 1)
                    v.tensor_tensor(qkv[t.par][:, 0:3 * P], bank[1][:, 0:3 * P],
                                    bias[:, 2:5, :].rearrange("p i d -> p (i d)"), ALU.add).then_inc(S("f_bias"), 1)
                    dve.wait_ge(S("f_bias"), t.n + 1)
                    v.reduce_max(fmax[t.par][:], qkv[t.par][:, 0:2 * P].rearrange("p (h d) -> p h d", d=DH), AX.X)\
                        .then_inc(S("f_max"), 1)
                if live(-2):
                    t = u + -2
                    dve.wait_ge(S("logit_done1"), t.n + 1)
                    v.tensor_tensor(lg[:, bass.ds(t.n, 1), :].rearrange("p o e -> p (o e)"), bank[7][:, 2 * P:2 * P + E],
                                    rb[:], ALU.add).then_inc(S("lg_ready1"), 1)
                if live(-1):
                    t = u + -1
                    add_projection(1, bank[6][:, 0:P], t)
                    ln_stats("lne1", 1, t)
            sweep(dve, NT, 2, 2, attention1)
            route(1)
            for s in SWEEPS[1:]:
                experts(s)
            sweep(dve, NT, 0, 0, lambda u, live: combine(1, u, "x_final"))

        @block.tensor
        def _(pe):
            mm = nc.tensor.matmul
            pe.wait_ge(S("cst_in"), 16)
            pe.wait_ge(S("wa_in"), 160)
            pe.wait_ge(S("dve_const"), 5)

            def one(out_, l_, r_):
                return mm(out_, l_, r_, start=True, stop=True)

            def turn(out_, in_):
                return nc.tensor.transpose(out_, in_, ident)

            def attention0(u, live):
                def scores(gr):
                    G = NG * u.n + gr
                    if gr == 0:
                        pe.wait_ge(S("qT_ready"), u.n + 1)
                        pe.wait_ge(S("kblk_ready"), u.n + 1)
                    after(pe, S("s_sub"), G - 1)
                    r = slice(32 * gr, 32 * gr + 32)
                    one(bank[gr % 2][:, 0:HG * NK], qT[u.par][r, :],
                        kblk[u.par][r, :, :].rearrange("p h k -> p (h k)")).then_inc(S("s_done"), 1)

                def turns(gr):
                    G = NG * u.n + gr
                    pe.wait_ge(S("s_sub"), G + 1)
                    after(pe, S("exp_done"), G - 1)
                    for h in range(HG):
                        last = turn(bank[2 + gr % 2][0:NK, h * P:(h + 1) * P], sm[gr % 2][:, h, :])
                    last.then_inc(S("t_done"), 1)

                def values(gr):
                    if gr == 0:
                        pe.wait_ge(S("vaug_ready"), u.n + 1)
                        after(pe, S("o_raw0"), u.n)
                    pe.wait_ge(S("exp_done"), NG * u.n + gr + 1)
                    for h in range(HG):
                        hh_ = HG * gr + h
                        last = one(bank[6][:, hh_ * (DH + 1):(hh_ + 1) * (DH + 1)], pT[gr][:, h, :],
                                   vaug[u.par][:, hh_, :])
                    last.then_inc(S("pv_done"), 1)

                if live(0):
                    scores(0)
                    scores(1)
                if live(-1):
                    t = u + -1
                    pe.wait_ge(S("o_ready0"), t.n + 1)
                    after(pe, S("lg_ready0"), t.n)
                    turn(bank[7][:, 0:P], o[t.par][:]).then_inc(S("oT_done0"), 1)
                if live(0):
                    turns(0)
                    scores(2)
                    turns(1)
                    scores(3)
                if live(-1):
                    t = u + -1
                    pe.wait_ge(S("oT_ready0"), t.n + 1)
                    one(bank[7][:, P:2 * P], oT[t.par][:], wa[:, 3, :]).then_inc(S("proj_done0"), 1)
                if live(0):
                    turns(2)
                if live(1):
                    t = u + 1
                    pe.wait_ge(S("xn_ready0"), t.n + 1)
                    pe.wait_ge(S(f"ctx_in0{t.par}"), 16 * (t.half + 1))
                    after(pe, S("vaug_ready"), t.n)
                    turn(bank[4][:, 0:P], xn[t.par][:])
                    one(bank[4][:, P:P + NK], wa[:, 1, :], ctxT[t.par][:, 0:NK])
                    one(bank[4][0:NK, 2 * P:3 * P], ctxT[t.par][:, 0:NK], wa[:, 2, :]).then_inc(S("kv0_done"), 1)
                if live(0):
                    turns(3)
                    values(0)
                    values(1)
                if live(1):
                    t = u + 1
                    pe.wait_ge(S("xnT_ready0"), t.n + 1)
                    after(pe, S("qT_ready"), t.n)
                    one(bank[5][:, 0:P], wa[:, 0, :], xnT[t.par][:]).then_inc(S("qT_done"), 1)
                if live(0):
                    values(2)
                if live(-1):
                    t = u + -1
                    pe.wait_ge(S("xe_ready0"), t.n + 1)
                    turn(bank[7][:, 0:P], xe[t.par][:]).then_inc(S("xeT_done0"), 1)
                if live(0):
                    values(3)
                if live(-1):
                    t = u + -1
                    pe.wait_ge(S("xeT_ready0"), t.n + 1)
                    one(bank[7][:, 2 * P:2 * P + E], xeT[t.par][:], wr[:, 0, :]).then_inc(S("logit_done0"), 1)
            sweep(pe, NT, 1, 1, attention0)

            def positions(l):
                oh2 = oh[:].rearrange("p t c e -> p (t c e)")
                pe.wait_ge(S("delta"), l + 1)
                for c in range(4):
                    last = one(bank[7][:, c:c + 1], oh2[:, c * P:(c + 1) * P], ones_b[:])
                last.then_inc(S("colsum"), 1)
                pe.wait_ge(S("csum"), l + 1)
                for c in range(4):
                    for k in range(4):
                        mm(bank[7][:, 16:16 + E], csum[:, k, :], same[:, 0:E], start=(k == 0), stop=(k == 3))\
                            if c == 0 else None
                    o_ = bank[5][:, c * P:(c + 1) * P]
                    mm(o_, tri[:], oh2[:, c * P:(c + 1) * P], start=True, stop=False)
                    for k in range(c):
                        mm(o_, csum[:, k, :], same[:], start=False, stop=False)
                    last = mm(o_, csum[:, c, :], pairm[:], start=False, stop=True)
                last.then_inc(S("counts"), 1)

            def experts(s):
                b, nf, wc = s["base"], s["f"], cols(s)
                nb = nf // P
                scale = 1

                def expert(t):
                    if s["shared"] is not None:
                        return E + s["shared"]
                    return nc.tensor.value_load(e_i[0:1, bass.ds(t.n, 1)], min_val=0, max_val=E - 1)

                def body(u, live):
                    if live(0):
                        ex = expert(u)
                        pe.wait_ge(S("xl_ready"), b + u.n + 1)
                        after(pe, S("h_ready"), b + u.n - 1)
                        wu = bass.ds(ex * wc, UP)
                        bk = bank[u.par][:]
                        mm(bk, ones_r[:], b_row[:, bass.ds(ex * BC, UP)], start=True, stop=False)
                        mm(bk, xh[u.par][:], w_hi[:, wu], start=False, stop=False)
                        mm(bk, xh[u.par][:], w_lo[:, wu], start=False, stop=False)
                        mm(bk, xl[u.par][:], w_hi[:, wu], start=False, stop=True).then_inc(S("up_done"), 1)
                    if live(-1):
                        t = u + -1
                        pe.wait_ge(S("h_ready"), b + t.n + 1)
                        after(pe, S("hTl_ready"), b + t.n - 1)
                        for c in range(nb):
                            last = turn(bank[2 + t.par][:, c * P:(c + 1) * P], hh[t.par][:, c * P:(c + 1) * P])
                        last.then_inc(S("hT_done"), 1)
                    if live(1):
                        t = u + 1
                        if s["shared"] is not None:
                            pe.wait_ge(S("xr_copied"), s["shared"] * NT + t.n + 1)
                        else:
                            pe.wait_ge(S(f"xr_in{s['l']}{t.par}"), 16 * (t.half + 1))
                        after(pe, S("xl_ready"), b + t.n)
                        turn(bank[6][:, 0:P], xr[t.par][:]).then_inc(S("xT_done"), 1)
                    if live(-2):
                        t = u + -2
                        ex = expert(t)
                        pe.wait_ge(S("hTl_ready"), b + t.n + 1)
                        after(pe, S("y_ready"), b + t.n - 1)
                        bk = bank[4 + t.par][:, 0:P]
                        mm(bk, ones_r[:], b_row[:, bass.ds(ex * BC + UP, P)], start=True, stop=False)
                        for c in range(nb):
                            wd = bass.ds(ex * wc + UP + c * P, P)
                            mm(bk, hTh[t.par][:, c * P:(c + 1) * P], w_hi[:, wd], start=False, stop=False)
                            mm(bk, hTh[t.par][:, c * P:(c + 1) * P], w_lo[:, wd], start=False, stop=False)
                            last = mm(bk, hTl[t.par][:, c * P:(c + 1) * P], w_hi[:, wd], start=False,
                                      stop=(c == nb - 1))
                        last.then_inc(S("down_done"), 1)
                sweep(pe, s["n"], 1, 2, body)

            positions(0)
            pe.wait_ge(S("emap"), 1)
            pe.wait_ge(S("w_split0"), NT)
            pe.wait_ge(S("b_row_in"), 32)
            experts(SWEEPS[0])

            def attention1(u, live):
                if live(-1):
                    t = u + -1
                    pe.wait_ge(S("kvm_ready"), 2 * (t.n + 1))
                    pe.wait_ge(S("qsT_ready"), t.n + 1)
                    after(pe, S("o_raw1"), t.n)
                    one(bank[4][:, 0:P + H], qsT[t.par][:], kvm[t.par][:]).then_inc(S("num_done"), 1)
                if live(1):
                    t = u + 1
                    pe.wait_ge(S("xn_ready1"), t.n + 1)
                    after(pe, S("xnT_ready1"), t.n)
                    turn(bank[0][:, 0:P], xn[t.par][:]).then_inc(S("xnT_done1"), 1)
                if live(-2):
                    t = u + -2
                    pe.wait_ge(S("xe_ready1"), t.n + 1)
                    after(pe, S("lg_ready1"), t.n)
                    turn(bank[7][:, 0:P], xe[t.par][:]).then_inc(S("xeT_done1"), 1)
                if live(0):
                    if isinstance(u.n, int) and u.n == 0:
                        pe.wait_ge(S("v_ones"), 2)
                    pe.wait_ge(S("f_soft"), u.n + 1)
                    after(pe, S("kvm_ready"), 2 * u.n)
                    one(bank[2][:, 0:P + 1], fsm[u.par][0:NK, P:2 * P], qkv[u.par][0:NK, 2 * P:3 * P + 1])\
                        .then_inc(S("kvp_done"), 1)
                    after(pe, S("qsT_ready"), u.n)
                    turn(bank[3][:, 0:P], fsm[u.par][:, 0:P]).then_inc(S("qsT_done"), 1)
                if live(-1):
                    t = u + -1
                    pe.wait_ge(S("o_ready1"), t.n + 1)
                    after(pe, S("oT_ready1"), t.n)
                    turn(bank[5][:, 0:P], o[t.par][:]).then_inc(S("oT_done1"), 1)
                if live(1):
                    t = u + 1
                    pe.wait_ge(S("xnT_ready1"), t.n + 1)
                    pe.wait_ge(S(f"ctx_in1{t.par}"), 16 * (t.half + 1))
                    after(pe, S("f_bias"), t.n)
                    one(bank[1][:, 0:P], xnT[t.par][:], wa[:, 4, :])
                    one(bank[1][:, P:3 * P], ctxT[t.par][:], wa[:, 5:7, :].rearrange("p i d -> p (i d)"))\
                        .then_inc(S("kv1_done"), 1)
                if live(-2):
                    t = u + -2
                    pe.wait_ge(S("xeT_ready1"), t.n + 1)
                    one(bank[7][:, 2 * P:2 * P + E], xeT[t.par][:], wr[:, 1, :]).then_inc(S("logit_done1"), 1)
                if live(-1):
                    t = u + -1
                    pe.wait_ge(S("oT_ready1"), t.n + 1)
                    after(pe, S("x_added1"), t.n)
                    one(bank[6][:, 0:P], oT[t.par][:], wa[:, 7, :]).then_inc(S("proj_done1"), 1)
            sweep(pe, NT, 1, 2, attention1)
            positions(1)
            pe.wait_ge(S("emap"), 2)
            pe.wait_ge(S("w_split1"), NT)
            pe.wait_ge(S("b_row_in"), 64)
            for s in SWEEPS[1:]:
                experts(s)


def kernel(**inputs):
    import concourse.bacc as _bacc
    from concourse.bass_utils import run_bass_kernel_spmd as _run

    i = {k: np.asarray(v) for k, v in inputs.items()}
    A0, A1, M0, M1 = "L0_xattn_", "L1_xattn_", "L0_ffn_", "L1_ffn_"

    def rows_first(w):
        return np.moveaxis(w, -2, 0)

    def halves(w):
        e, f, d = w.shape
        return w.reshape(e, f // P, P, d).transpose(2, 0, 1, 3).reshape(P, e, f // P * d)

    w0 = np.concatenate([rows_first(i[M0 + "W1"].transpose(0, 2, 1)), rows_first(i[M0 + "W2"].transpose(0, 2, 1)),
                         halves(i[M0 + "W3"].transpose(0, 2, 1))], axis=2).reshape(P, -1)
    up = np.concatenate([i[M1 + "W1"], i[M1 + "sW1"]], axis=0)
    down = np.concatenate([i[M1 + "W2"], i[M1 + "sW2"]], axis=0)
    w1 = np.concatenate([rows_first(up), halves(down)], axis=2).reshape(P, -1)
    arrays = {
        "x": i["x"], "ctxT": i["ctx_1024"].transpose(0, 2, 1), "cst": constants(), "w0": w0, "w1": w1,
        "wq0": i[A0 + "Wq"].T, "wk0": i[A0 + "Wk"].T, "wv0": i[A0 + "Wv"].T, "wo0": i[A0 + "Wo"].T,
        "wq1": i[A1 + "Wq"].T, "wk1": i[A1 + "Wk"].T, "wv1": i[A1 + "Wv"].T, "wp1": i[A1 + "Wp"].T,
        "wr0": i[M0 + "Wg"].T, "wr1": i[M1 + "rW"], "rb": i[M1 + "rb"],
        "bq0": i[A0 + "bq"], "bk0": i[A0 + "bk"], "bv0": i[A0 + "bv"], "bo0": i[A0 + "bo"],
        "bq1": i[A1 + "bq"], "bk1": i[A1 + "bk"], "bv1": i[A1 + "bv"], "bp1": i[A1 + "bp"],
        "eb0": np.concatenate([i[M0 + "b1"], i[M0 + "b2"], i[M0 + "b3"]], axis=1),
        "eb1": np.concatenate([np.concatenate([i[M1 + "b1"], i[M1 + "sb1"]], axis=0),
                               np.concatenate([i[M1 + "b2"], i[M1 + "sb2"]], axis=0)], axis=1),
    }
    arrays = {"in_" + k: np.ascontiguousarray(v) for k, v in arrays.items()}
    nc = _bacc.Bacc("TRN2", target_bir_lowering=False, num_devices=1)
    aps = {k[3:]: nc.dram_tensor(k, v.shape, mybir.dt.from_np(v.dtype), kind="ExternalInput").ap()
           for k, v in arrays.items()}
    out = nc.dram_tensor("out", (NT, P, P), F32, kind="ExternalOutput").ap()
    build(nc, aps, out)
    r = _run(nc, [arrays], core_ids=[0])
    return r.results[0]["out"]
```

```python
import numpy as np
import concourse.bass as bass
from concourse import mybir
from contextlib import ExitStack

F32 = mybir.dt.float32
F32R = mybir.dt.float32r
BF16 = mybir.dt.bfloat16
F16 = mybir.dt.float16
I32 = mybir.dt.int32
ALU = mybir.AluOpType
ACT = mybir.ActivationFunctionType
AX = mybir.AxisListType

P = 128
NT = 32
NK = 77
H = 16
DH = P // H
HG = 4
NG = H // HG
E = 8
TOPK = 2
NSH = 2
NPAIR = NT * TOPK
NR = NPAIR + E
F0, F1 = 256, 512
UP = 512
W0C = UP + F0
W1C = UP + F1
C0 = E * W0C // NT
C1 = (E + NSH) * W1C // NT
BC = UP + P
ZR = 4
SCALE = float(1.0 / np.sqrt(np.float32(DH)))
EPS = 1e-5
BIG = 3.0e38

K_ID = 0
K_TRI = K_ID + P
K_PAIR = K_TRI + P
K_SAME = K_PAIR + P
K_BD = K_SAME + P
K_H16 = K_BD + P
K_H4 = K_H16 + H
K_REV = K_H4 + HG
K_LT = K_REV + E
K_LE = K_LT + E * E
K_TILE = K_LE + E * E
K_N = K_TILE + NR


def constants():
    c = np.zeros((P, K_N), np.float32)
    i = np.arange(P)
    c[:, K_ID:K_TRI] = np.eye(P)
    c[:, K_TRI:K_PAIR] = i[:, None] < i[None, :]
    same = i[:, None] % E == i[None, :] % E
    c[:, K_PAIR:K_SAME] = same & (i[:, None] // E < i[None, :] // E)
    c[:, K_SAME:K_BD] = same
    c[:, K_BD:K_H16] = i[:, None] // DH == i[None, :] // DH
    c[:, K_H16:K_H4] = i[:, None] // DH == np.arange(H)
    c[:, K_H4:K_REV] = i[:, None] // DH % HG == np.arange(HG)
    e = np.arange(E)
    c[:, K_REV:K_LT] = E - e
    c[:, K_LT:K_LE] = (e[None, :] < e[:, None]).reshape(-1)
    c[:, K_LE:K_TILE] = (e[None, :] <= e[:, None]).reshape(-1)
    c[:, K_TILE:] = np.arange(NR)
    return c


class Tile:

    def __init__(self, j, off):
        self.n = 2 * j + off
        self.half = j + off // 2
        self.par = off % 2
        self.j, self.off = j, off

    def __add__(self, k):
        return Tile(self.j, self.off + k)


def sweep(eng, n, ahead, behind, body):
    first = behind + 2
    first += 1 - first % 2
    last = n - ahead
    last -= (last - first) % 2
    for u in range(-ahead, first):
        body(Tile(0, u), lambda k: 0 <= u + k < n)
    with eng.Fori(first // 2, first // 2 + (last - first) // 2) as j:
        body(Tile(j, 1), lambda k: True)
        body(Tile(j, 2), lambda k: True)
    for u in range(last, n + behind):
        body(Tile(0, u), lambda k: 0 <= u + k < n)


def after(eng, sem, count):
    if isinstance(count, int) and count <= 0:
        return
    eng.wait_ge(sem, count)


def apart(eng, sem):
    eng.sem_inc(sem, 1)


def build(nc, a, out):
    ctx = ExitStack()
    with ctx:
        sems = {}

        def S(name):
            if name not in sems:
                sems[name] = ctx.enter_context(nc.semaphore(name))
            return sems[name]

        def sb(name, shape, dt=F32):
            return ctx.enter_context(nc.sbuf_tensor(name, shape, dt))

        x_sb = sb("x_sb", [P, NT, P])
        xn_sb = sb("xn_sb", [P, NT, P])
        w_r = sb("w_r", [P, 2, (E + NSH) * W1C], F32R)
        w_st = sb("w_st", [P, 2, max(C0, C1)])
        cst = sb("cst", [P, K_N])
        wa = sb("wa", [P, 8, P])
        wr = sb("wr", [P, 2, E])
        qk_col = sb("qk_col", [P, 2])
        bias = sb("bias", [P, 6, P])
        rb = sb("rb", [P, E])
        b_st = xn_sb[0:2 * E + NSH, NT - BC // P:NT, :].rearrange("p t d -> p (t d)")
        b_rest = xn_sb[0:2 * E + NSH, NT - 2 * BC // P:NT - BC // P, :].rearrange("p t d -> p (t d)")
        b_part = [sb(f"b_part{i}", [2 * E + NSH, BC], BF16) for i in range(3)]
        b_row = sb("b_row", [3, (E + NSH) * BC], BF16)
        ones_3 = sb("ones_3", [3, P], BF16)
        tri = sb("tri", [P, P], BF16)
        pairm = sb("pairm", [P, P], BF16)
        same = sb("same", [P, P], BF16)
        ones_b = sb("ones_b", [P, 1], BF16)
        half_neg = sb("half_neg", [P, 1])
        zeros = sb("zeros", [P, ZR, P])

        ident = cst[:, K_ID:K_TRI]

        stats = [[sb(f"stats{w}{i}", [P, 6]) for i in range(2)] for w in range(2)]
        meanv = [[sb(f"meanv{w}{i}", [P, 2]) for i in range(2)] for w in range(2)]
        vareps = [[sb(f"vareps{w}{i}", [P, 1]) for i in range(2)] for w in range(2)]
        rstd = [[sb(f"rstd{w}{i}", [P, 1]) for i in range(2)] for w in range(2)]
        xn = [sb(f"xn{i}", [P, P]) for i in range(2)]
        xnT = [sb(f"xnT{i}", [P, P]) for i in range(2)]
        xe = [sb(f"xe{i}", [P, P]) for i in range(2)]
        oxT = [sb(f"oxT{i}", [P, 2 * P]) for i in range(2)]
        ctxT = [sb(f"ctxT{i}", [P, P]) for i in range(2)]
        kf = [sb(f"kf{i}", [P, NK]) for i in range(2)]
        kblk = [sb(f"kblk{i}", [P, HG, NK]) for i in range(2)]
        vpart = [sb(f"vpart{i}", [NK, H, 3, DH + 1], BF16) for i in range(2)]
        vrest = [sb(f"vrest{i}", [NK, P]) for i in range(2)]
        qz = [sb(f"qz{i}", [P, NG, P]) for i in range(2)]
        smax = [sb(f"smax{i}", [P, HG]) for i in range(2)]
        sm = [sb(f"sm{i}", [P, HG, NK]) for i in range(2)]
        wide = [sb(f"wide{g}", [P, 512]) for g in range(NG)]
        pT = [w[0:NK, :].rearrange("k (h q) -> k h q", h=HG) for w in wide]
        p_hi = [sb(f"p_hi{g}", [NK, HG, P], F16) for g in range(NG)]
        p_lo = [sb(f"p_lo{g}", [NK, HG, P], F16) for g in range(NG)]
        osum = [sb(f"osum{i}", [P, H, DH + 1]) for i in range(2)]
        rden = [sb(f"rden{i}", [P, H]) for i in range(2)]
        oraw = [sb(f"oraw{i}", [P, P]) for i in range(2)]
        o = [sb(f"o{i}", [P, P]) for i in range(2)]
        oT = [b[:, 0:P] for b in oxT]
        xeT = [b[:, P:2 * P] for b in oxT]
        qkv = [wide[i][:, 0:3 * P + 1] for i in range(2)]
        fmax = [sb(f"fmax{i}", [P, 2 * H]) for i in range(2)]
        fsub = [wide[2 + i][:, 0:2 * P] for i in range(2)]
        fexp = [wide[2 + i][:, 2 * P:4 * P] for i in range(2)]
        fsum = [sb(f"fsum{i}", [P, 2 * H]) for i in range(2)]
        frec = [sb(f"frec{i}", [P, 2 * H]) for i in range(2)]
        fsm = [sb(f"fsm{i}", [P, 2 * P]) for i in range(2)]
        kvm = [s_[:].rearrange("p h k -> p (h k)")[:, 0:P + H] for s_ in sm]
        qsT = [k_[:].rearrange("p h k -> p (h k)")[:, 0:P] for k_ in kblk]
        yg = [sb(f"yg{i}", [P, TOPK, P]) for i in range(2)]
        idx = [sb(f"idx{i}", [P, TOPK], I32) for i in range(2)]

        lg = sb("lg", [P, NT, E])
        lg2 = wide[2][:, 0:NT * E].rearrange("p (t e) -> p t e", e=E)
        eqs = wide[2][:, NT * E:2 * NT * E].rearrange("p (t e) -> p t e", e=E)
        top = sb("top", [P, TOPK, NT])
        first = sb("first", [P, TOPK, NT])
        oh = sb("oh", [P, NT, TOPK, E], BF16)
        delta = sb("delta", [P, NT])
        exd = sb("exd", [P, NT])
        wsum = sb("wsum", [P, NT])
        gate = sb("gate", [P, NT, TOPK])
        csum = sb("csum", [P, 4, P], BF16)
        cnt = sb("cnt", [P, E])
        cnt_i = sb("cnt_i", [P, E], I32)
        til_i = sb("til_i", [P, E], I32)
        til = sb("til", [P, E])
        tmp64 = sb("tmp64", [P, 2, E, E])
        t_start = sb("t_start", [P, E])
        t_end = sb("t_end", [P, E])
        row0 = sb("row0", [P, E])
        posn = wide[3][:].rearrange("p (c e) -> p c e", e=E)
        slot = sb("slot", [P, NPAIR])
        slot_i = sb("slot_i", [P, NPAIR], I32)
        ecmp = sb("ecmp", [1, NR, E])
        eacc = sb("eacc", [1, NR])
        e_i = sb("e_i", [1, NR], I32)

        xr = [sb(f"xr{i}", [P, P]) for i in range(2)]
        xh = [sb(f"xh{i}", [P, P], F32R) for i in range(2)]
        xl = [sb(f"xl{i}", [P, P], F32R) for i in range(2)]
        hs = [wide[2 + i][:, 0:F0] for i in range(2)]
        hh = [wide[i] for i in range(2)]
        hTh = [sb(f"hTh{i}", [P, F1], F32R) for i in range(2)]
        hTl = [sb(f"hTl{i}", [P, F1], F32R) for i in range(2)]
        ysb = oraw

        bank = [ctx.enter_context(nc.psum_tensor(f"bank{i}", [P, 512], F32)) for i in range(8)]

        xs_dram = nc.dram_tensor("xs_sorted", (NR * P, P), F32).ap()
        ys_dram = nc.dram_tensor("ys_sorted", (NR * P, P), F32).ap()

        block = ctx.enter_context(nc.Block())

        SWEEPS = [dict(l=0, n=NR, f=F0, shared=None, base=0),
                  dict(l=1, n=NT, f=F1, shared=0, base=NR),
                  dict(l=1, n=NR, f=F1, shared=None, base=NR + NT),
                  dict(l=1, n=NT, f=F1, shared=1, base=2 * NR + NT)]
        for s in SWEEPS:
            assert s["base"] % 2 == 0

        def cols(s):
            return W0C if s["l"] == 0 else W1C

        @block.sync
        def _(sp):
            sp.dma_start(cst[:], a["cst"]).then_inc(S("cst_in"), 16)
            sp.dma_start(x_sb[:, 0:2, :], a["x"][0:2].rearrange("b s d -> s b d")).then_inc(S("x_in0"), 16)
            for i, n in enumerate(("wq0", "wk0", "wv0", "wo0", "wq1", "wk1", "wv1", "wp1")):
                sp.dma_start(wa[:, i, :], a[n]).then_inc(S("wa_in"), 16)
            sp.dma_start(wr[:, 0, :], a["wr0"]).then_inc(S("wa_in"), 16)
            sp.dma_start(wr[:, 1, :], a["wr1"]).then_inc(S("wa_in"), 16)
            for i, n in enumerate(("bq0", "bk0")):
                sp.dma_start(qk_col[:, i:i + 1], a[n].rearrange("(p o) -> p o", o=1)).then_inc(S("bias_in"), 16)
            for i, n in enumerate(("bv0", "bo0", "bq1", "bk1", "bv1", "bp1")):
                sp.dma_start(bias[:, i, :], a[n].partition_broadcast(P)).then_inc(S("bias_in"), 16)
            sp.dma_start(rb[:], a["rb"].partition_broadcast(P)).then_inc(S("bias_in"), 16)
            sp.dma_start(x_sb[:, 2:NT, :], a["x"][2:NT].rearrange("b s d -> s b d")).then_inc(S("x_in"), 16)
            sp.dma_start(b_st[0:E, :], a["eb0"]).then_inc(S("b_in"), 16)
            sp.dma_start(b_st[E:, :], a["eb1"]).then_inc(S("b_in"), 16)

            sp.wait_ge(S("zeros_set"), 1)
            for r in range(0, NR * P, ZR * P):
                sp.dma_start(xs_dram[r:r + ZR * P, :].rearrange("(p r) d -> p r d", r=ZR), zeros[:])\
                    .then_inc(S("xs_zeroed"), 16)

            def bias_rows(l, n):
                for i in range(3):
                    sp.dma_start(b_row[i:i + 1, 0:n * BC], b_part[i][l * E:l * E + n, :]).then_inc(S("b_row_in"), 16)

            sp.wait_ge(S("b_split"), 4)
            bias_rows(0, E)

            def feed(l, wsrc, c, done):
                def body(u, live):
                    if live(1):
                        t = u + 1
                        after(sp, S(done), t.n - 1)
                        sp.dma_start(ctxT[t.par][:, 0:NK], a["ctxT"][bass.ds(t.n, 1)].rearrange("o d k -> d (o k)"))\
                            .then_inc(S(f"ctx_in{l}{t.par}"), 16)
                    if live(0):
                        after(sp, S(f"w_split{l}"), u.n - 1)
                        sp.dma_start(w_st[:, u.par, 0:c], wsrc[:, bass.ds(u.n * c, c)])\
                            .then_inc(S(f"w_in{l}{u.par}"), 16)
                sweep(sp, NT, 1, 0, body)

            def rows(s):
                def body(u, live):
                    if live(2):
                        t = u + 2
                        after(sp, S("xT_done"), s["base"] + t.n - 1)
                        sp.dma_start(xr[t.par][:], xs_dram[bass.ds(t.n * P, P), :])\
                            .then_inc(S(f"xr_in{s['l']}{t.par}"), 16)
                    if live(-3):
                        t = u + -3
                        sp.wait_ge(S("y_ready"), s["base"] + t.n + 1)
                        sp.dma_start(ys_dram[bass.ds(t.n * P, P), :], ysb[t.par][:])\
                            .then_inc(S(f"y_out{s['l']}{t.par}"), 16)
                sweep(sp, s["n"], 2, 3, body)

            feed(0, a["w0"], C0, "v_done")
            sp.wait_ge(S("rows0"), TOPK * 16 * NT)
            rows(SWEEPS[0])
            sp.wait_ge(S("y_out00"), 16 * NR // 2)
            sp.wait_ge(S("y_out01"), 16 * NR // 2)
            bias_rows(1, E + NSH)
            feed(1, a["w1"], C1, "kv1_done")
            sp.wait_ge(S("rows1"), TOPK * 16 * NT)
            rows(SWEEPS[2])
            sp.wait_ge(S("y_out10"), 16 * NR // 2)
            sp.wait_ge(S("y_out11"), 16 * NR // 2)

            def store(u, live):
                sp.wait_ge(S("x_final"), u.n + 1)
                sp.dma_start(out[bass.ds(u.n, 1)].rearrange("o s d -> s (o d)"),
                             x_sb[:, bass.ds(u.n, 1), :].rearrange("p o d -> p (o d)")).then_inc(S("stored"), 16)
            sweep(sp, NT, 0, 0, store)
            sp.wait_ge(S("stored"), 16 * NT)

        @block.gpsimd
        def _(pool):
            g = nc.gpsimd
            g.memset(zeros[:], 0.0).then_inc(S("zeros_set"), 1)
            g.memset(half_neg[:], -0.5).then_inc(S("pool_const"), 1)
            for i in range(2):
                g.memset(vpart[i][:, :, 0, DH:DH + 1], 1.0).then_inc(S("pool_const"), 1)
                g.memset(vpart[i][:, :, 1:3, DH:DH + 1], 0.0).then_inc(S("pool_const"), 1)
                g.memset(qz[i][:], 0.0).then_inc(S("pool_const"), 1)
                g.memset(ctxT[i][:, NK:P], 0.0).then_inc(S("pool_const"), 1)
            pool.wait_ge(S("pool_const"), 9)
            pool.wait_ge(S("bias_in"), 16 * 9)
            pool.wait_ge(S("cst_in"), 16)
            pool.wait_ge(S("b_in"), 32)
            g.tensor_copy(b_part[0][:], b_st).then_inc(S("b_split"), 1)
            pool.wait_ge(S("b_split"), 1)
            g.tensor_tensor(b_rest, b_st, b_part[0][:], ALU.subtract).then_inc(S("b_split"), 1)
            pool.wait_ge(S("b_split"), 2)
            g.tensor_copy(b_part[1][:], b_rest).then_inc(S("b_split"), 1)
            pool.wait_ge(S("b_split"), 3)
            g.tensor_tensor(b_part[2][:], b_rest, b_part[1][:], ALU.subtract).then_inc(S("b_split"), 1)

            def inverse_std(tag, w, t):
                pool.wait_ge(S(f"{tag}_var"), t.n + 1)
                apart(pool, S("pool_apart"))
                g.tensor_scalar(vareps[w][t.par][:], meanv[w][t.par][:, 1:2], EPS, None, ALU.add)\
                    .then_inc(S(f"{tag}_eps"), 1)
                pool.wait_ge(S(f"{tag}_eps"), t.n + 1)
                g.tensor_tensor(rstd[w][t.par][:], vareps[w][t.par][:], half_neg[:], ALU.pow)\
                    .then_inc(S(f"{tag}_rstd"), 1)

            def split_weights(l, c, t):
                if l == 0:
                    pool.wait_ge(S(f"w_in{l}{t.par}"), 16 * (t.half + 1))
                    g.tensor_copy(w_r[:, 0, bass.ds(t.n * c, c)], w_st[:, t.par, 0:c]).then_inc(S(f"w_half{l}"), 1)
                pool.wait_ge(S(f"w_half{l}"), t.n + 1)
                g.tensor_tensor(w_r[:, 1, bass.ds(t.n * c, c)], w_st[:, t.par, 0:c],
                                w_r[:, 0, bass.ds(t.n * c, c)].bitcast(F32), ALU.subtract)\
                    .then_inc(S(f"w_split{l}"), 1)

            def residual_bias(l, b, normed, t):
                pool.wait_ge(S(normed), t.n + 1)
                xt = x_sb[:, bass.ds(t.n, 1), :].rearrange("p o d -> p (o d)")
                g.tensor_tensor(xt, xt, bias[:, b, :], ALU.add).then_inc(S(f"x_bias{l}"), 1)

            def attention0(u, live):
                if live(-2):
                    t = u + -2
                    pool.wait_ge(S("o_raw0"), t.n + 1)
                    after(pool, S("ox_done"), t.n - 1)
                    g.tensor_tensor(o[t.par][:], oraw[t.par][:], bias[:, 0, :], ALU.add).then_inc(S("o_ready0"), 1)
                if live(-3):
                    inverse_std("lne0", 1, u + -3)
                if live(1):
                    t = u + 1
                    pool.wait_ge(S("kf_ready"), t.n + 1)
                    after(pool, S("s_done"), NG * (t.n - 1))
                    g.tensor_tensor(kblk[t.par][:], kf[t.par][:].unsqueeze(1).to_broadcast([P, HG, NK]),
                                    cst[:, K_H4:K_REV].unsqueeze(2).to_broadcast([P, HG, NK]), ALU.mult)\
                        .then_inc(S("kblk_ready"), 1)
                if live(0):
                    pool.wait_ge(S("v_rest"), u.n + 1)
                    after(pool, S("pv_done"), NG * (u.n - 1))
                    apart(pool, S("pool_apart"))
                    vr = vrest[u.par][:].rearrange("k (h d) -> k h d", d=DH)
                    g.tensor_copy(vpart[u.par][:, :, 1, 0:DH], vr).then_inc(S("v_part2"), 1)
                    pool.wait_ge(S("v_part2"), u.n + 1)
                    g.tensor_tensor(vpart[u.par][:, :, 2, 0:DH], vr, vpart[u.par][:, :, 1, 0:DH], ALU.subtract)\
                        .then_inc(S("v_ready"), 1)
                if live(2):
                    inverse_std("ln0", 0, u + 2)
                if live(-1):
                    residual_bias(0, 1, "xn_ready0", u + -1)
                if live(0):
                    split_weights(0, C0, u)
            sweep(pool, NT, 2, 3, attention0)

            def scatter(l):
                pool.wait_ge(S("slots"), l + 1)
                if l == 0:
                    pool.wait_ge(S("xs_zeroed"), 16 * (NR // ZR))
                for t in range(NT):
                    for c in range(TOPK):
                        g.indirect_dma_start(xs_dram, bass.IndirectOffsetOnAxis(
                            ap=slot_i[:, TOPK * t + c:TOPK * t + c + 1], axis=0), xn_sb[:, t, :], None)\
                            .then_inc(S(f"rows{l}"), 16)

            def gather(l, t):
                after(pool, S(("combined0", "x_final")[l]), t.n - 1)
                if isinstance(t.n, int):
                    cols_ = [slot_i[:, TOPK * t.n + c:TOPK * t.n + c + 1] for c in range(TOPK)]
                    apart(pool, S("pool_apart"))
                    g.tensor_copy(idx[t.par][:], slot_i[:, TOPK * t.n:TOPK * (t.n + 1)]).then_inc(S(f"ga_idx{l}"), 1)\
                        if l == 0 else None
                else:
                    g.tensor_copy(idx[t.par][:], slot_i[:, bass.ds(TOPK * t.n, TOPK)]).then_inc(S(f"ga_idx{l}"), 1)
                    pool.wait_ge(S(f"ga_idx{l}"), t.n + 1)
                    apart(pool, S("pool_apart"))
                    cols_ = [idx[t.par][:, c:c + 1] for c in range(TOPK)]
                for c in range(TOPK):
                    g.indirect_dma_start(yg[t.par][:, c, :], None, ys_dram,
                                         bass.IndirectOffsetOnAxis(ap=cols_[c], axis=0))\
                        .then_inc(S(f"yg_in{l}{t.par}"), 16)

            scatter(0)
            for p in range(2):
                pool.wait_ge(S(f"y_out0{p}"), 16 * NR // 2)

            for i in range(2):
                g.memset(qkv[i][:, 3 * P:3 * P + 1], 1.0).then_inc(S("v_ones"), 1)

            def attention1(u, live):
                if live(4):
                    gather(0, u + 4)
                if live(1):
                    t = u + 1
                    pool.wait_ge(S("f_max"), t.n + 1)
                    after(pool, S("f_exp"), t.n - 1)
                    g.tensor_tensor(fsub[t.par][:].rearrange("p (h d) -> p h d", d=DH),
                                    qkv[t.par][:, 0:2 * P].rearrange("p (h d) -> p h d", d=DH),
                                    fmax[t.par][:].unsqueeze(2).to_broadcast([P, 2 * H, DH]), ALU.subtract)\
                        .then_inc(S("f_sub"), 1)
                if live(0):
                    residual_bias(1, 5, "xn_ready1", u)
                if live(3):
                    inverse_std("ln1", 0, u + 3)
                if live(0):
                    split_weights(1, C1, u)
                if live(-1):
                    inverse_std("lne1", 1, u + -1)
            sweep(pool, NT, 4, 2, attention1)
            scatter(1)

            for p in range(2):
                pool.wait_ge(S(f"y_out1{p}"), 16 * NR // 2)
            for t in range(NT):
                gather(1, Tile(0, t))

        @block.scalar
        def _(act):
            s_ = nc.scalar
            act.wait_ge(S("bias_in"), 16 * 9)
            act.wait_ge(S("pool_const"), 9)

            def copy_out(dst, src):
                return s_.activation(dst, src, ACT.Copy)

            def attention0(u, live):
                def exps(t, gr):
                    G = NG * t.n + gr
                    src = bank[2 + gr % 2][0:NK, :].rearrange("k (h q) -> k h q", h=HG)
                    act.wait_ge(S("t_done"), G + 1)
                    after(act, S("p_split"), G - NG + 1)
                    s_.activation(pT[gr], src, ACT.Exp, scale=SCALE)
                    after(act, S("pv_done"), G - NG + 1)
                    s_.activation(p_hi[gr][:], src, ACT.Exp, scale=SCALE).then_inc(S("exp_done"), 1)
                if live(-1):
                    exps(u + -1, 2)
                if live(1):
                    t = u + 1
                    act.wait_ge(S("kx_done"), t.n + 1)
                    after(act, S("qT_done"), t.n - 1)
                    copy_out(xnT[t.par][:], bank[4][:, 0:P]).then_inc(S("xnT_ready0"), 1)
                    after(act, S("kblk_ready"), t.n - 1)
                    s_.activation(kf[t.par][:], bank[4][:, P:P + NK], ACT.Identity, bias=qk_col[:, 1:2])\
                        .then_inc(S("kf_ready"), 1)
                if live(0):
                    act.wait_ge(S("v_done"), u.n + 1)
                    after(act, S("pv_done"), NG * (u.n - 1))
                    copy_out(vpart[u.par][:, :, 0, 0:DH], bank[4][0:NK, 2 * P:3 * P].rearrange("k (h d) -> k h d", d=DH))\
                        .then_inc(S("v_part1"), 1)
                if live(-1):
                    exps(u + -1, 3)
                if live(-2) or live(-4):
                    w = u + -2
                    c = slice(0 if live(-2) else P, 2 * P if live(-4) else P)
                    act.wait_ge(S("ox_done"), w.n + 1)
                    after(act, S("pl_done"), w.n - 1)
                    copy_out(oxT[w.par][:, c], bank[7][:, c]).then_inc(S("ox_ready"), 1)
                if live(0):
                    exps(u, 0)
                if live(1):
                    t = u + 1
                    act.wait_ge(S("qT_done"), t.n + 1)
                    after(act, S("s_done"), NG * (t.n - 1))
                    for gr in range(NG):
                        r = slice(32 * gr, 32 * gr + 32)
                        last = s_.activation(qz[t.par][r, gr, :], bank[4][r, 3 * P:4 * P], ACT.Identity,
                                             bias=qk_col[r, 0:1])
                    last.then_inc(S("qT_ready"), 1)
                if live(0):
                    exps(u, 1)
            sweep(act, NT, 1, 4, attention0)

            def gate_exp(l):
                act.wait_ge(S("delta"), l + 1)
                s_.activation(exd[:], delta[:], ACT.Exp).then_inc(S("exd"), 1)

            def experts(s):
                b, nf = s["base"], s["f"]

                def body(u, live):
                    if live(0):
                        act.wait_ge(S("up_done"), b + u.n + 1)
                        if s["l"] == 0:
                            after(act, S("h_ready"), b + u.n - 1)
                            s_.activation(hs[u.par][:], bank[u.par][:, 0:F0], ACT.Silu).then_inc(S("silu_done"), 1)
                        else:
                            after(act, S("hT_done"), b + u.n - 1)
                            s_.activation(hh[u.par][:], bank[u.par][:], ACT.Gelu).then_inc(S("h_ready"), 1)
                    if live(-1):
                        t = u + -1
                        act.wait_ge(S("hT_done"), b + t.n + 1)
                        after(act, S("down_done"), b + t.n - 1)
                        copy_out(hTh[t.par][:, 0:nf], bank[2 + t.par][:, 0:nf]).then_inc(S("hTh_ready"), 1)
                    if live(1):
                        t = u + 1
                        act.wait_ge(S("xT_done"), b + t.n + 1)
                        after(act, S("up_done"), b + t.n - 1)
                        copy_out(xh[t.par][:], bank[6][:, 0:P]).then_inc(S("xh_ready"), 1)
                sweep(act, s["n"], 1, 1, body)

            gate_exp(0)
            experts(SWEEPS[0])

            def attention1(u, live):
                if live(0):
                    act.wait_ge(S("f_sub"), u.n + 1)
                    after(act, S("f_soft"), u.n - 1)
                    s_.activation(fexp[u.par][:], fsub[u.par][:], ACT.Exp).then_inc(S("f_exp"), 1)
                if live(0):
                    act.wait_ge(S("qsT_done"), u.n + 1)
                    after(act, S("num_done"), u.n - 1)
                    after(act, S("oT_ready1"), u.n - 1)
                    copy_out(qsT[u.par][:], bank[3][:, 0:P]).then_inc(S("qsT_ready"), 1)
                if live(-2):
                    t = u + -2
                    act.wait_ge(S("xeT_done1"), t.n + 1)
                    after(act, S("logit_done1"), t.n - 1)
                    copy_out(xeT[t.par], bank[7][:, 0:P]).then_inc(S("xeT_ready1"), 1)
                if live(2):
                    t = u + 2
                    act.wait_ge(S("xnT_done1"), t.n + 1)
                    after(act, S("kv1_done"), t.n - 1)
                    copy_out(xnT[t.par][:], bank[0][:, 0:P]).then_inc(S("xnT_ready1"), 1)
                if live(0):
                    act.wait_ge(S(f"w_in1{u.par}"), 16 * (u.half + 1))
                    copy_out(w_r[:, 0, bass.ds(u.n * C1, C1)], w_st[:, u.par, 0:C1]).then_inc(S("w_half1"), 1)
            act.wait_ge(S("down_done"), NR)
            sweep(act, NT, 2, 2, attention1)
            gate_exp(1)
            for s in SWEEPS[1:]:
                experts(s)

        @block.vector
        def _(dve):
            v = nc.vector
            dve.wait_ge(S("cst_in"), 16)
            v.tensor_copy(tri[:], cst[:, K_TRI:K_PAIR]).then_inc(S("dve_const"), 1)
            v.tensor_copy(pairm[:], cst[:, K_PAIR:K_SAME]).then_inc(S("dve_const"), 1)
            v.tensor_copy(same[:], cst[:, K_SAME:K_BD]).then_inc(S("dve_const"), 1)
            v.memset(ones_b[:], 1.0).then_inc(S("dve_const"), 1)
            v.memset(ones_3[:], 1.0).then_inc(S("dve_const"), 1)
            dve.wait_ge(S("bias_in"), 16 * 9)
            dve.wait_ge(S("pool_const"), 9)

            def xt(t):
                return x_sb[:, bass.ds(t.n, 1), :].rearrange("p o d -> p (o d)")

            def ln_stats(tag, w, t):
                apart(dve, S("dve_apart"))
                v.bn_stats(stats[w][t.par][:], xt(t)).then_inc(S(f"{tag}_stats"), 1)
                dve.wait_ge(S(f"{tag}_stats"), t.n + 1)
                apart(dve, S("dve_apart"))
                v.bn_aggr(meanv[w][t.par][:], stats[w][t.par][:]).then_inc(S(f"{tag}_var"), 1)

            def ln_apply(tag, w, t, dst):
                dve.wait_ge(S(f"{tag}_rstd"), t.n + 1)
                return v.tensor_scalar(dst, xt(t), meanv[w][t.par][:, 0:1], rstd[w][t.par][:],
                                       ALU.subtract, ALU.mult)

            def expert_input(l, t):
                after(dve, S(f"xeT_done{l}"), t.n - 1)
                ln_apply(f"lne{l}", 1, t, xe[t.par][:]).then_inc(S(f"xe_ready{l}"), 1)
                v.tensor_scalar(xn_sb[:, bass.ds(t.n, 1), :].rearrange("p o d -> p (o d)"), xt(t),
                                meanv[1][t.par][:, 0:1], rstd[1][t.par][:], ALU.subtract, ALU.mult)\
                    .then_inc(S(f"xn_kept{l}"), 1)

            def add_projection(l, bnk, t):
                dve.wait_ge(S(f"proj_done{l}"), t.n + 1)
                dve.wait_ge(S(f"x_bias{l}"), t.n + 1)
                v.tensor_tensor(xt(t), xt(t), bnk, ALU.add).then_inc(S(f"x_added{l}"), 1)
                dve.wait_ge(S(f"x_added{l}"), t.n + 1)

            def attention0(u, live):
                def scores(gr):
                    G = NG * u.n + gr
                    sc = bank[gr % 2][:, 0:HG * NK].rearrange("q (h k) -> q h k", h=HG)
                    dve.wait_ge(S("s_done"), G + 1)
                    v.reduce_max(smax[gr % 2][:], sc, AX.X).then_inc(S("s_max"), 1)
                    dve.wait_ge(S("s_max"), G + 1)
                    after(dve, S("t_done"), G - 1)
                    v.tensor_tensor(sm[gr % 2][:], sc, smax[gr % 2][:].unsqueeze(2).to_broadcast([P, HG, NK]),
                                    ALU.subtract).then_inc(S("s_sub"), 1)

                def split(t, gr):
                    G = NG * t.n + gr
                    dve.wait_ge(S("exp_done"), G + 1)
                    after(dve, S("pv_done"), G - NG + 1)
                    v.tensor_tensor(p_lo[gr][:], pT[gr], p_hi[gr][:], ALU.subtract).then_inc(S("p_split"), 1)

                if live(-2):
                    t = u + -2
                    ov = osum[t.par]
                    dve.wait_ge(S("pv_done"), NG * (t.n + 1))
                    v.reduce_sum(ov[:], bank[5 + t.par][:, 0:3 * H * (DH + 1)]
                                 .rearrange("q (h c d) -> q h d c", h=H, c=3), AX.X).then_inc(S("o_sum"), 1)
                    dve.wait_ge(S("o_sum"), t.n + 1)
                    v.reciprocal(rden[t.par][:], ov[:, :, DH]).then_inc(S("rden0"), 1)
                    dve.wait_ge(S("rden0"), t.n + 1)
                    after(dve, S("o_ready0"), t.n - 1)
                    v.tensor_tensor(oraw[t.par][:].rearrange("q (h d) -> q h d", h=H), ov[:, :, 0:DH],
                                    rden[t.par][:].unsqueeze(2).to_broadcast([P, H, DH]), ALU.mult)\
                        .then_inc(S("o_raw0"), 1)
                if live(0):
                    scores(0)
                if live(-1):
                    split(u + -1, 1)
                if live(0):
                    dve.wait_ge(S("v_part1"), u.n + 1)
                    after(dve, S("v_ready"), u.n - 1)
                    v.tensor_tensor(vrest[u.par][:].rearrange("k (h d) -> k h d", d=DH),
                                    bank[4][0:NK, 2 * P:3 * P].rearrange("k (h d) -> k h d", d=DH),
                                    vpart[u.par][:, :, 0, 0:DH], ALU.subtract).then_inc(S("v_rest"), 1)
                if live(-3) or live(-5):
                    w = u + -3
                    dve.wait_ge(S("pl_done"), w.n + 1)
                if live(-5):
                    t = u + -5
                    lgt = lg[:, bass.ds(t.n, 1), :].rearrange("p o e -> p (o e)")
                    v.tensor_copy(lgt, bank[7][:, 3 * P:3 * P + E])\
                        .then_inc(S("lg_ready0"), 1)
                    if not live(-3):
                        dve.wait_ge(S("lg_ready0"), t.n + 1)
                if live(-3):
                    t = u + -3
                    dve.wait_ge(S("x_bias0"), t.n + 1)
                    v.tensor_tensor(xt(t), xt(t), bank[7][:, 2 * P:3 * P], ALU.add).then_inc(S("x_added0"), 1)
                    dve.wait_ge(S("x_added0"), t.n + 1)
                    ln_stats("lne0", 1, t)
                if live(0):
                    scores(1)
                if live(-1):
                    split(u + -1, 2)
                if live(2):
                    t = u + 2
                    if isinstance(t.n, int) and t.n == 0:
                        dve.wait_ge(S("x_in0"), 16)
                    if isinstance(t.n, int) and t.n == 2:
                        dve.wait_ge(S("x_in"), 16)
                    ln_stats("ln0", 0, t)
                if live(0):
                    scores(2)
                if live(-1):
                    split(u + -1, 3)
                if live(-3):
                    t = u + -3
                    after(dve, S("ox_done"), t.n + 1)
                    ln_apply("lne0", 1, t, xe[t.par][:]).then_inc(S("xe_ready0"), 1)
                    v.tensor_scalar(xn_sb[:, bass.ds(t.n, 1), :].rearrange("p o d -> p (o d)"), xt(t),
                                    meanv[1][t.par][:, 0:1], rstd[1][t.par][:], ALU.subtract, ALU.mult)\
                        .then_inc(S("xn_kept0"), 1)
                if live(0):
                    scores(3)
                    split(u, 0)
                if live(2):
                    t = u + 2
                    after(dve, S("kx_done"), t.n - 1)
                    ln_apply("ln0", 0, t, xn[t.par][:]).then_inc(S("xn_ready0"), 1)
            sweep(dve, NT, 2, 5, attention0)

            def route(l):
                count = [0]
                link_sem = S(f"route{l}")

                def link(ins):
                    count[0] += 1
                    ins.then_inc(link_sem, 1)
                    dve.wait_ge(link_sem, count[0])

                def over_e(ap):
                    return ap.unsqueeze(2).to_broadcast([P, NT, E])

                rev = cst[:, K_REV:K_LT].unsqueeze(1).to_broadcast([P, NT, E])
                dve.wait_ge(S(f"lg_ready{l}"), NT)
                src = lg
                for c in range(TOPK):
                    link(v.reduce_max(top[:, c, :], src[:], AX.X))
                    link(v.tensor_tensor(eqs[:], src[:], over_e(top[:, c, :]), ALU.is_equal))
                    link(v.tensor_tensor(eqs[:], eqs[:], rev, ALU.mult))
                    link(v.reduce_max(first[:, c, :], eqs[:], AX.X))
                    link(v.tensor_tensor(oh[:, :, c, :], rev, over_e(first[:, c, :]), ALU.is_equal))
                    if c == 0:
                        link(v.tensor_scalar(eqs[:], oh[:, :, 0, :], -BIG, None, ALU.mult))
                        link(v.tensor_tensor(lg2[:], eqs[:], lg[:], ALU.add))
                        src = lg2
                v.tensor_tensor(delta[:], top[:, 1, :], top[:, 0, :], ALU.subtract).then_inc(S("delta"), 1)
                dve.wait_ge(S("colsum"), l + 1)
                link(v.tensor_copy(csum[:], bank[7][:, 0:4].unsqueeze(2).to_broadcast([P, 4, P])))
                v.tensor_copy(ones_b[:], ones_b[:]).then_inc(S("csum"), 1)
                dve.wait_ge(S("counts"), l + 1)
                link(v.tensor_scalar(cnt[:], bank[7][:, 16:16 + E], float(P - 1), None, ALU.add))
                link(v.tensor_copy(cnt_i[:], cnt[:]))
                link(v.tensor_single_scalar(til_i[:], cnt_i[:], 7, ALU.arith_shift_right))
                link(v.tensor_copy(til[:], til_i[:]))
                tb = til[:].unsqueeze(1).to_broadcast([P, E, E])
                for i, (k, dst) in enumerate(((K_LT, t_start), (K_LE, t_end))):
                    link(v.tensor_tensor(tmp64[:, i], tb, cst[:, k:k + E * E].rearrange("p (a b) -> p a b", a=E),
                                         ALU.mult))
                    link(v.reduce_sum(dst[:], tmp64[:, i], AX.X))
                link(v.tensor_scalar(row0[:], t_start[:], float(P), None, ALU.mult))
                link(v.tensor_tensor(posn[:], bank[5][:].rearrange("p (c e) -> p c e", e=E),
                                     row0[:].unsqueeze(1).to_broadcast([P, NPAIR, E]), ALU.add))
                link(v.tensor_tensor(posn[:], posn[:], oh[:].rearrange("p t c e -> p (t c) e"), ALU.mult))
                link(v.reduce_sum(slot[:], posn[:], AX.X))
                v.tensor_copy(slot_i[:], slot[:]).then_inc(S("slots"), 1)
                link(v.tensor_tensor(ecmp[:], t_end[0:1, :].unsqueeze(1).to_broadcast([1, NR, E]),
                                     cst[0:1, K_TILE:K_TILE + NR].unsqueeze(2).to_broadcast([1, NR, E]), ALU.is_le))
                link(v.reduce_sum(eacc[:], ecmp[:], AX.X))
                link(v.tensor_scalar(eacc[:], eacc[:], float(E - 1), None, ALU.min))
                v.tensor_copy(e_i[:], eacc[:]).then_inc(S("emap"), 1)
                dve.wait_ge(S("exd"), l + 1)
                link(v.tensor_scalar(wsum[:], exd[:], 1.0, None, ALU.add))
                link(v.reciprocal(gate[:, :, 0], wsum[:]))
                link(v.tensor_tensor(gate[:, :, 1], exd[:], gate[:, :, 0], ALU.mult))

            def experts(s):
                b, nf = s["base"], s["f"]

                def body(u, live):
                    if live(0) and s["l"] == 0:
                        dve.wait_ge(S("silu_done"), b + u.n + 1)
                        after(dve, S("hT_done"), b + u.n - 1)
                        v.tensor_tensor(hh[u.par][:, 0:F0], hs[u.par][:], bank[u.par][:, F0:2 * F0], ALU.mult)\
                            .then_inc(S("h_ready"), 1)
                    if live(-1):
                        t = u + -1
                        dve.wait_ge(S("hTh_ready"), b + t.n + 1)
                        v.tensor_tensor(hTl[t.par][:, 0:nf], bank[2 + t.par][:, 0:nf], hTh[t.par][:, 0:nf].bitcast(F32),
                                        ALU.subtract).then_inc(S("hTl_ready"), 1)
                    if live(1):
                        t = u + 1
                        dve.wait_ge(S("xh_ready"), b + t.n + 1)
                        v.tensor_tensor(xl[t.par][:], bank[6][:, 0:P], xh[t.par][:].bitcast(F32), ALU.subtract)\
                            .then_inc(S("xl_ready"), 1)
                    if live(2) and s["shared"] is not None:
                        t = u + 2
                        after(dve, S("xT_done"), b + t.n - 1)
                        v.tensor_copy(xr[t.par][:], xn_sb[:, bass.ds(t.n, 1), :].rearrange("p o d -> p (o d)"))\
                            .then_inc(S("xr_copied"), 1)
                    if live(-2):
                        t = u + -2
                        dve.wait_ge(S("down_done"), b + t.n + 1)
                        bk = bank[4 + t.par]
                        if s["shared"] is not None:
                            v.scalar_tensor_tensor(xt(t), bk[:, 0:P], 1.0 / NSH, xt(t), ALU.mult, ALU.add)\
                                .then_inc(S("y_half"), 1)
                            dve.wait_ge(S("y_half"), s["shared"] * NT + t.n + 1)
                            v.scalar_tensor_tensor(xt(t), bk[:, P:2 * P], 1.0 / NSH, xt(t), ALU.mult, ALU.add)\
                                .then_inc(S("y_ready"), 1)
                        else:
                            after(dve, S(f"y_out{s['l']}{t.par}"), 16 * t.half)
                            v.reduce_sum(ysb[t.par][:], bk[:, 0:2 * P].rearrange("p (a d) -> p d a", a=2), AX.X)\
                                .then_inc(S("y_ready"), 1)
                    if s["shared"] == 1 and live(-6):
                        dve.wait_ge(S("y_ready"), b + u.n - 6 + 1)
                        combine(1, u + -6, "x_final")
                sweep(dve, s["n"], 2, 6 if s["shared"] == 1 else 2, body)

            def combine(l, t, done):
                dve.wait_ge(S(f"yg_in{l}{t.par}"), 32 * (t.half + 1))
                for c in range(TOPK):
                    v.scalar_tensor_tensor(xt(t), yg[t.par][:, c, :], gate[:, bass.ds(t.n, 1), c], xt(t),
                                           ALU.mult, ALU.add).then_inc(S(f"comb{l}" if c == 0 else done), 1)
                    dve.wait_ge(S(f"comb{l}" if c == 0 else done), t.n + 1)

            route(0)
            experts(SWEEPS[0])

            def attention1(u, live):
                if live(0):
                    fe = fexp[u.par][:].rearrange("p (h d) -> p h d", d=DH)
                    dve.wait_ge(S("f_exp"), u.n + 1)
                    v.reduce_sum(fsum[u.par][:], fe, AX.X).then_inc(S("f_sum"), 1)
                    dve.wait_ge(S("f_sum"), u.n + 1)
                    v.reciprocal(frec[u.par][:], fsum[u.par][:]).then_inc(S("f_rec"), 1)
                    dve.wait_ge(S("f_rec"), u.n + 1)
                    after(dve, S("qsT_done"), u.n - 1)
                    v.tensor_tensor(fsm[u.par][:].rearrange("p (h d) -> p h d", d=DH), fe,
                                    frec[u.par][:].unsqueeze(2).to_broadcast([P, 2 * H, DH]), ALU.mult)\
                        .then_inc(S("f_soft"), 1)
                if live(1):
                    t = u + 1
                    dve.wait_ge(S("kv1_done"), t.n + 1)
                    after(dve, S("f_sub"), t.n - 1)
                    after(dve, S("kvp_done"), t.n - 1)
                    v.tensor_tensor(qkv[t.par][:, 0:3 * P], bank[1][:, 0:3 * P],
                                    bias[:, 2:5, :].rearrange("p i d -> p (i d)"), ALU.add).then_inc(S("f_bias"), 1)
                    dve.wait_ge(S("f_bias"), t.n + 1)
                    v.reduce_max(fmax[t.par][:], qkv[t.par][:, 0:2 * P].rearrange("p (h d) -> p h d", d=DH), AX.X)\
                        .then_inc(S("f_max"), 1)
                if live(-1):
                    t = u + -1
                    dve.wait_ge(S("num_done"), t.n + 1)
                    v.reciprocal(rden[t.par][:], bank[4][:, P:P + H]).then_inc(S("rden1"), 1)
                    dve.wait_ge(S("rden1"), t.n + 1)
                    after(dve, S("oT_done1"), t.n - 1)
                    v.tensor_tensor(oraw[t.par][:].rearrange("q (h d) -> q h d", h=H),
                                    bank[4][:, 0:P].rearrange("q (h d) -> q h d", h=H),
                                    rden[t.par][:].unsqueeze(2).to_broadcast([P, H, DH]), ALU.mult)\
                        .then_inc(S("o_raw1"), 1)
                if live(-2):
                    expert_input(1, u + -2)
                if live(0):
                    dve.wait_ge(S("kvp_done"), u.n + 1)
                    after(dve, S("num_done"), u.n - 1)
                    v.tensor_tensor(kvm[u.par][:, 0:P], bank[2][:, 0:P], cst[:, K_BD:K_H16], ALU.mult)\
                        .then_inc(S("kvm_ready"), 1)
                    v.tensor_scalar(kvm[u.par][:, P:P + H], cst[:, K_H16:K_H4], bank[2][:, P:P + 1], None, ALU.mult)\
                        .then_inc(S("kvm_ready"), 1)
                if live(-1):
                    t = u + -1
                    dve.wait_ge(S("oT_done1"), t.n + 1)
                    dve.wait_ge(S("qsT_ready"), t.n + 1)
                    after(dve, S("proj_done1"), t.n - 1)
                    v.tensor_tensor(oT[t.par], bank[5][:, 0:P], qsT[t.par][:], ALU.add).then_inc(S("oT_ready1"), 1)
                if live(2):
                    t = u + 2
                    after(dve, S("xnT_done1"), t.n - 1)
                    ln_apply("ln1", 0, t, xn[t.par][:]).then_inc(S("xn_ready1"), 1)
                if live(3):
                    t = u + 3
                    combine(0, t, "combined0")
                    ln_stats("ln1", 0, t)
                if live(-2):
                    t = u + -2
                    dve.wait_ge(S("logit_done1"), t.n + 1)
                    v.tensor_tensor(lg[:, bass.ds(t.n, 1), :].rearrange("p o e -> p (o e)"), bank[7][:, 2 * P:2 * P + E],
                                    rb[:], ALU.add).then_inc(S("lg_ready1"), 1)
                if live(-1):
                    t = u + -1
                    add_projection(1, bank[6][:, 0:P], t)
                    ln_stats("lne1", 1, t)
            sweep(dve, NT, 3, 2, attention1)
            route(1)
            for s in SWEEPS[1:]:
                experts(s)

        @block.tensor
        def _(pe):
            mm = nc.tensor.matmul
            pe.wait_ge(S("cst_in"), 16)
            pe.wait_ge(S("wa_in"), 160)
            pe.wait_ge(S("dve_const"), 5)

            def one(out_, l_, r_):
                return mm(out_, l_, r_, start=True, stop=True)

            def turn(out_, in_):
                return nc.tensor.transpose(out_, in_, ident)

            def attention0(u, live):
                def scores(gr):
                    G = NG * u.n + gr
                    if gr == 0:
                        pe.wait_ge(S("qT_ready"), u.n + 1)
                        pe.wait_ge(S("kblk_ready"), u.n + 1)
                    after(pe, S("s_sub"), G - 1)
                    one(bank[gr % 2][:, 0:HG * NK], qz[u.par][:, gr, :],
                        kblk[u.par][:].rearrange("p h k -> p (h k)")).then_inc(S("s_done"), 1)

                def turns(t, gr):
                    G = NG * t.n + gr
                    pe.wait_ge(S("s_sub"), G + 1)
                    after(pe, S("exp_done"), G - 1)
                    for h in range(HG):
                        last = turn(bank[2 + gr % 2][0:NK, h * P:(h + 1) * P], sm[gr % 2][:, h, :])
                    last.then_inc(S("t_done"), 1)

                def values(t, gr):
                    if gr == 0:
                        pe.wait_ge(S("v_ready"), t.n + 1)
                        after(pe, S("o_sum"), t.n - 1)
                    pe.wait_ge(S("p_split"), NG * t.n + gr + 1)
                    for h in range(HG):
                        hd = HG * gr + h
                        w = 3 * (DH + 1)
                        vp = vpart[t.par][:, hd, :, :].rearrange("k c d -> k (c d)")
                        mm(bank[5 + t.par][:, hd * w:(hd + 1) * w], p_hi[gr][:, h, :], vp, start=True, stop=False)
                        last = mm(bank[5 + t.par][:, hd * w:(hd + 1) * w], p_lo[gr][:, h, :], vp, start=False, stop=True)
                    last.then_inc(S("pv_done"), 1)

                prev = u + -1
                if live(-1):
                    turns(prev, 2)
                if live(0):
                    scores(0)
                if live(0) or live(1):
                    after(pe, S("qT_ready"), u.n + 1)
                if live(0):
                    one(bank[4][0:NK, 2 * P:3 * P], ctxT[u.par][:, 0:NK], wa[:, 2, :]).then_inc(S("v_done"), 1)
                if live(1):
                    t = u + 1
                    pe.wait_ge(S("xn_ready0"), t.n + 1)
                    pe.wait_ge(S(f"ctx_in0{t.par}"), 16 * (t.half + 1))
                    turn(bank[4][:, 0:P], xn[t.par][:])
                    one(bank[4][:, P:P + NK], wa[:, 1, :], ctxT[t.par][:, 0:NK]).then_inc(S("kx_done"), 1)
                if live(-1):
                    values(prev, 0)
                    turns(prev, 3)
                if live(0):
                    scores(1)
                if live(-1):
                    values(prev, 1)
                if live(-2) or live(-4):
                    w = u + -2
                    if live(-3):
                        after(pe, S("x_added0"), w.n)
                    if live(-5):
                        after(pe, S("lg_ready0"), w.n - 2)
                    if live(-2):
                        t = u + -2
                        pe.wait_ge(S("o_ready0"), t.n + 1)
                        last = turn(bank[7][:, 0:P], o[t.par][:])
                    if live(-4):
                        t = u + -4
                        pe.wait_ge(S("xe_ready0"), t.n + 1)
                        last = turn(bank[7][:, P:2 * P], xe[t.par][:])
                    last.then_inc(S("ox_done"), 1)
                if live(0):
                    turns(u, 0)
                    scores(2)
                if live(1):
                    t = u + 1
                    pe.wait_ge(S("xnT_ready0"), t.n + 1)
                    pe.wait_ge(S("kf_ready"), t.n + 1)
                    if live(0):
                        pe.wait_ge(S("v_rest"), u.n + 1)
                    one(bank[4][:, 3 * P:4 * P], wa[:, 0, :], xnT[t.par][:]).then_inc(S("qT_done"), 1)
                if live(-1):
                    values(prev, 2)
                if live(0):
                    turns(u, 1)
                    scores(3)
                if live(-1):
                    values(prev, 3)
                if live(-2) or live(-4):
                    w = u + -2
                    pe.wait_ge(S("ox_ready"), w.n + 1)
                    if live(-2):
                        last = one(bank[7][:, 2 * P:3 * P], oT[w.par], wa[:, 3, :])
                    if live(-4):
                        last = one(bank[7][:, 3 * P:3 * P + E], xeT[w.par], wr[:, 0, :])
                    last.then_inc(S("pl_done"), 1)
            sweep(pe, NT, 1, 4, attention0)

            def positions(l):
                oh2 = oh[:].rearrange("p t c e -> p (t c e)")
                pe.wait_ge(S("delta"), l + 1)
                for c in range(4):
                    last = one(bank[7][:, c:c + 1], oh2[:, c * P:(c + 1) * P], ones_b[:])
                last.then_inc(S("colsum"), 1)
                pe.wait_ge(S("csum"), l + 1)
                for c in range(4):
                    for k in range(4):
                        mm(bank[7][:, 16:16 + E], csum[:, k, :], same[:, 0:E], start=(k == 0), stop=(k == 3))\
                            if c == 0 else None
                    o_ = bank[5][:, c * P:(c + 1) * P]
                    mm(o_, tri[:], oh2[:, c * P:(c + 1) * P], start=True, stop=False)
                    for k in range(c):
                        mm(o_, csum[:, k, :], same[:], start=False, stop=False)
                    last = mm(o_, csum[:, c, :], pairm[:], start=False, stop=True)
                last.then_inc(S("counts"), 1)

            def experts(s):
                b, nf, wc = s["base"], s["f"], cols(s)
                nb = nf // P
                scale = 1

                def expert(t):
                    if s["shared"] is not None:
                        return E + s["shared"]
                    return nc.tensor.value_load(e_i[0:1, bass.ds(t.n, 1)], min_val=0, max_val=E - 1)

                def body(u, live):
                    if live(0):
                        ex = expert(u)
                        pe.wait_ge(S("xl_ready"), b + u.n + 1)
                        after(pe, S("h_ready"), b + u.n - 1)
                        wu = bass.ds(ex * wc, UP)
                        bk = bank[u.par][:]
                        mm(bk, ones_3[:], b_row[:, bass.ds(ex * BC, UP)], start=True, stop=False)
                        mm(bk, xh[u.par][:], w_r[:, 0, wu], start=False, stop=False)
                        mm(bk, xh[u.par][:], w_r[:, 1, wu], start=False, stop=False)
                        mm(bk, xl[u.par][:], w_r[:, 0, wu], start=False, stop=True).then_inc(S("up_done"), 1)
                    if live(-1):
                        t = u + -1
                        pe.wait_ge(S("h_ready"), b + t.n + 1)
                        after(pe, S("hTl_ready"), b + t.n - 1)
                        for c in range(nb):
                            last = turn(bank[2 + t.par][:, c * P:(c + 1) * P], hh[t.par][:, c * P:(c + 1) * P])
                        last.then_inc(S("hT_done"), 1)
                    if live(1):
                        t = u + 1
                        if s["shared"] is not None:
                            pe.wait_ge(S("xr_copied"), s["shared"] * NT + t.n + 1)
                        else:
                            pe.wait_ge(S(f"xr_in{s['l']}{t.par}"), 16 * (t.half + 1))
                        after(pe, S("xl_ready"), b + t.n)
                        turn(bank[6][:, 0:P], xr[t.par][:]).then_inc(S("xT_done"), 1)
                    if live(-2):
                        t = u + -2
                        ex = expert(t)
                        pe.wait_ge(S("hTl_ready"), b + t.n + 1)
                        after(pe, S("y_ready"), b + t.n - 1)
                        bk = bank[4 + t.par][:, 0:2 * P]
                        for c in range(nb):
                            wd = w_r[:, :, bass.ds(ex * wc + UP + c * P, P)]
                            mm(bk, hTh[t.par][:, c * P:(c + 1) * P], wd, start=(c == 0), stop=False)
                            mm(bk, hTl[t.par][:, c * P:(c + 1) * P], wd, start=False, stop=False)
                        last = mm(bk[:, 0:P], ones_3[:], b_row[:, bass.ds(ex * BC + UP, P)], start=False, stop=True)
                        last.then_inc(S("down_done"), 1)
                sweep(pe, s["n"], 1, 2, body)

            positions(0)
            pe.wait_ge(S("emap"), 1)
            pe.wait_ge(S("w_split0"), NT)
            pe.wait_ge(S("b_row_in"), 48)
            experts(SWEEPS[0])

            def attention1(u, live):
                if live(1):
                    t = u + 1
                    pe.wait_ge(S("xnT_ready1"), t.n + 1)
                    pe.wait_ge(S(f"ctx_in1{t.par}"), 16 * (t.half + 1))
                    after(pe, S("f_bias"), t.n)
                    one(bank[1][:, 0:P], xnT[t.par][:], wa[:, 4, :])
                    one(bank[1][:, P:3 * P], ctxT[t.par][:], wa[:, 5:7, :].rearrange("p i d -> p (i d)"))\
                        .then_inc(S("kv1_done"), 1)
                if live(-1):
                    t = u + -1
                    pe.wait_ge(S("kvm_ready"), 2 * (t.n + 1))
                    pe.wait_ge(S("qsT_ready"), t.n + 1)
                    after(pe, S("o_raw1"), t.n)
                    one(bank[4][:, 0:P + H], qsT[t.par][:], kvm[t.par][:]).then_inc(S("num_done"), 1)
                if live(0):
                    if isinstance(u.n, int) and u.n == 0:
                        pe.wait_ge(S("v_ones"), 2)
                    pe.wait_ge(S("f_soft"), u.n + 1)
                    after(pe, S("kvm_ready"), 2 * u.n)
                    one(bank[2][:, 0:P + 1], fsm[u.par][0:NK, P:2 * P], qkv[u.par][0:NK, 2 * P:3 * P + 1])\
                        .then_inc(S("kvp_done"), 1)
                    after(pe, S("qsT_ready"), u.n)
                    turn(bank[3][:, 0:P], fsm[u.par][:, 0:P]).then_inc(S("qsT_done"), 1)
                if live(-1):
                    t = u + -1
                    pe.wait_ge(S("o_raw1"), t.n + 1)
                    after(pe, S("oT_ready1"), t.n)
                    turn(bank[5][:, 0:P], oraw[t.par][:]).then_inc(S("oT_done1"), 1)
                if live(-2):
                    t = u + -2
                    pe.wait_ge(S("xe_ready1"), t.n + 1)
                    after(pe, S("lg_ready1"), t.n)
                    turn(bank[7][:, 0:P], xe[t.par][:]).then_inc(S("xeT_done1"), 1)
                if live(2):
                    t = u + 2
                    pe.wait_ge(S("xn_ready1"), t.n + 1)
                    after(pe, S("xnT_ready1"), t.n)
                    turn(bank[0][:, 0:P], xn[t.par][:]).then_inc(S("xnT_done1"), 1)
                if live(-2):
                    t = u + -2
                    pe.wait_ge(S("xeT_ready1"), t.n + 1)
                    one(bank[7][:, 2 * P:2 * P + E], xeT[t.par], wr[:, 1, :]).then_inc(S("logit_done1"), 1)
                if live(-1):
                    t = u + -1
                    pe.wait_ge(S("oT_ready1"), t.n + 1)
                    after(pe, S("x_added1"), t.n)
                    one(bank[6][:, 0:P], oT[t.par], wa[:, 7, :]).then_inc(S("proj_done1"), 1)
            sweep(pe, NT, 2, 2, attention1)
            positions(1)
            pe.wait_ge(S("emap"), 2)
            pe.wait_ge(S("w_split1"), NT)
            pe.wait_ge(S("b_row_in"), 96)
            for s in SWEEPS[1:]:
                experts(s)


def kernel(**inputs):
    import concourse.bacc as _bacc
    from concourse.bass_utils import run_bass_kernel_spmd as _run

    i = {k: np.asarray(v) for k, v in inputs.items()}
    A0, A1, M0, M1 = "L0_xattn_", "L1_xattn_", "L0_ffn_", "L1_ffn_"

    def rows_first(w):
        return np.moveaxis(w, -2, 0)

    def halves(w):
        e, f, d = w.shape
        return w.reshape(e, f // P, P, d).transpose(2, 0, 1, 3).reshape(P, e, f // P * d)

    w0 = np.concatenate([rows_first(i[M0 + "W1"].transpose(0, 2, 1)), rows_first(i[M0 + "W2"].transpose(0, 2, 1)),
                         halves(i[M0 + "W3"].transpose(0, 2, 1))], axis=2).reshape(P, -1)
    up = np.concatenate([i[M1 + "W1"], i[M1 + "sW1"]], axis=0)
    down = np.concatenate([i[M1 + "W2"], i[M1 + "sW2"]], axis=0)
    w1 = np.concatenate([rows_first(up), halves(down)], axis=2).reshape(P, -1)
    arrays = {
        "x": i["x"], "ctxT": i["ctx_1024"].transpose(0, 2, 1), "cst": constants(), "w0": w0, "w1": w1,
        "wq0": i[A0 + "Wq"].T, "wk0": i[A0 + "Wk"].T, "wv0": i[A0 + "Wv"].T, "wo0": i[A0 + "Wo"].T,
        "wq1": i[A1 + "Wq"].T, "wk1": i[A1 + "Wk"].T, "wv1": i[A1 + "Wv"].T, "wp1": i[A1 + "Wp"].T,
        "wr0": i[M0 + "Wg"].T, "wr1": i[M1 + "rW"], "rb": i[M1 + "rb"],
        "bq0": i[A0 + "bq"], "bk0": i[A0 + "bk"], "bv0": i[A0 + "bv"], "bo0": i[A0 + "bo"],
        "bq1": i[A1 + "bq"], "bk1": i[A1 + "bk"], "bv1": i[A1 + "bv"], "bp1": i[A1 + "bp"],
        "eb0": np.concatenate([i[M0 + "b1"], i[M0 + "b2"], i[M0 + "b3"]], axis=1),
        "eb1": np.concatenate([np.concatenate([i[M1 + "b1"], i[M1 + "sb1"]], axis=0),
                               np.concatenate([i[M1 + "b2"], i[M1 + "sb2"]], axis=0)], axis=1),
    }
    arrays = {"in_" + k: np.ascontiguousarray(v) for k, v in arrays.items()}
    nc = _bacc.Bacc("TRN2", target_bir_lowering=False, num_devices=1)
    aps = {k[3:]: nc.dram_tensor(k, v.shape, mybir.dt.from_np(v.dtype), kind="ExternalInput").ap()
           for k, v in arrays.items()}
    out = nc.dram_tensor("out", (NT, P, P), F32, kind="ExternalOutput").ap()
    build(nc, aps, out)
    r = _run(nc, [arrays], core_ids=[0])
    return r.results[0]["out"]
```

```python
import numpy as np
import concourse.bass as bass
from concourse import mybir
from contextlib import ExitStack

F32 = mybir.dt.float32
F32R = mybir.dt.float32r
BF16 = mybir.dt.bfloat16
F16 = mybir.dt.float16
I32 = mybir.dt.int32
ALU = mybir.AluOpType
ACT = mybir.ActivationFunctionType
AX = mybir.AxisListType

P = 128
NT = 32
NK = 77
H = 16
DH = P // H
HG = 4
NG = H // HG
E = 8
TOPK = 2
NSH = 2
NPAIR = NT * TOPK
NR = NPAIR + E
F0, F1 = 256, 512
UP = 512
W0C = UP + F0
W1C = UP + F1
C0 = E * W0C // NT
C1 = (E + NSH) * W1C // NT
BC = UP + P
POOL_GROUP = 1
QUAD = 4
ZR = 4
SCALE = float(1.0 / np.sqrt(np.float32(DH)))
EPS = 1e-5
BIG = 3.0e38

K_ID = 0
K_TRI = K_ID + P
K_PAIR = K_TRI + P
K_SAME = K_PAIR + P
K_BD = K_SAME + P
K_H16 = K_BD + P
K_H4 = K_H16 + H
K_REV = K_H4 + HG
K_LT = K_REV + E
K_LE = K_LT + E * E
K_TILE = K_LE + E * E
K_N = K_TILE + NR


def constants():
    c = np.zeros((P, K_N), np.float32)
    i = np.arange(P)
    c[:, K_ID:K_TRI] = np.eye(P)
    c[:, K_TRI:K_PAIR] = i[:, None] < i[None, :]
    same = i[:, None] % E == i[None, :] % E
    c[:, K_PAIR:K_SAME] = same & (i[:, None] // E < i[None, :] // E)
    c[:, K_SAME:K_BD] = same
    c[:, K_BD:K_H16] = i[:, None] // DH == i[None, :] // DH
    c[:, K_H16:K_H4] = i[:, None] // DH == np.arange(H)
    c[:, K_H4:K_REV] = i[:, None] // DH % HG == np.arange(HG)
    e = np.arange(E)
    c[:, K_REV:K_LT] = E - e
    c[:, K_LT:K_LE] = (e[None, :] < e[:, None]).reshape(-1)
    c[:, K_LE:K_TILE] = (e[None, :] <= e[:, None]).reshape(-1)
    c[:, K_TILE:] = np.arange(NR)
    return c


class Tile:

    def __init__(self, j, off, step=2):
        self.n = step * j + off
        self.half = step // 2 * j + off // 2
        self.par = off % 2
        self.j, self.off, self.step = j, off, step

    def __add__(self, k):
        return Tile(self.j, self.off + k, self.step)


def sweep(eng, n, ahead, behind, body, step=2):
    first = behind + 2
    first += (1 - first) % step
    last = n - ahead
    last -= (last - first) % step
    for u in range(-ahead, first):
        body(Tile(0, u), lambda k: 0 <= u + k < n)
    with eng.Fori(first // step, last // step) as j:
        for off in range(1, step + 1):
            body(Tile(j, off, step), lambda k: True)
    for u in range(last, n + behind):
        body(Tile(0, u), lambda k: 0 <= u + k < n)


def after(eng, sem, count):
    if isinstance(count, int) and count <= 0:
        return
    eng.wait_ge(sem, count)


def apart(eng, sem):
    eng.sem_inc(sem, 1)


def build(nc, a, out):
    ctx = ExitStack()
    with ctx:
        sems = {}

        def S(name):
            if name not in sems:
                sems[name] = ctx.enter_context(nc.semaphore(name))
            return sems[name]

        def sb(name, shape, dt=F32):
            return ctx.enter_context(nc.sbuf_tensor(name, shape, dt))

        x_sb = sb("x_sb", [P, NT, P])
        xn_sb = sb("xn_sb", [P, NT, P])
        w_r = sb("w_r", [P, 2, (E + NSH) * W1C], F32R)
        w_st = sb("w_st", [P, 2, max(C0, C1)])
        cst = sb("cst", [P, K_N])
        wa = sb("wa", [P, 8, P])
        wr = sb("wr", [P, 2, E])
        qk_col = sb("qk_col", [P, 2])
        bias = sb("bias", [P, 6, P])
        rb = sb("rb", [P, E])
        b_st = xn_sb[0:2 * E + NSH, NT - BC // P:NT, :].rearrange("p t d -> p (t d)")
        b_rest = xn_sb[0:2 * E + NSH, NT - 2 * BC // P:NT - BC // P, :].rearrange("p t d -> p (t d)")
        b_part = [sb(f"b_part{i}", [2 * E + NSH, BC], BF16) for i in range(3)]
        b_row = sb("b_row", [3, (E + NSH) * BC], BF16)
        ones_3 = sb("ones_3", [3, P], BF16)
        tri = sb("tri", [P, P], BF16)
        pairm = sb("pairm", [P, P], BF16)
        same = sb("same", [P, P], BF16)
        ones_b = sb("ones_b", [P, 1], BF16)
        half_neg = sb("half_neg", [P, 1])
        zeros = sb("zeros", [P, ZR, P])

        ident = cst[:, K_ID:K_TRI]

        stats = [[sb(f"stats{w}{i}", [P, 6]) for i in range(2)] for w in range(2)]
        meanv = [[sb(f"meanv{w}{i}", [P, 2]) for i in range(2)] for w in range(2)]
        vareps = [[sb(f"vareps{w}{i}", [P, 1]) for i in range(2)] for w in range(2)]
        rstd = [[sb(f"rstd{w}{i}", [P, 1]) for i in range(2)] for w in range(2)]
        xn = [sb(f"xn{i}", [P, P]) for i in range(2)]
        xnT = [sb(f"xnT{i}", [P, P]) for i in range(2)]
        xe = [sb(f"xe{i}", [P, P]) for i in range(2)]
        oxT = [sb(f"oxT{i}", [P, 2 * P]) for i in range(2)]
        ctxT = [sb(f"ctxT{i}", [P, P]) for i in range(2)]
        kvm_all = sb("kvm_all", [P, NT * (P + H)])
        taken = [0]

        def lent(rows, cols_):
            at = taken[0]
            taken[0] += cols_
            assert taken[0] <= NT * (P + H)
            return kvm_all[0:rows, at:at + cols_]

        kf = [lent(P, NK) for i in range(2)]
        kblk = [sb(f"kblk{i}", [P, HG, NK]) for i in range(2)]
        vpart = [lent(NK, H * 3 * (DH + 1) // 2).bitcast(BF16).rearrange("k (h c d) -> k h c d", h=H, c=3)
                 for i in range(2)]
        vrest = [lent(NK, P) for i in range(2)]
        qz = [lent(P, NG * P).rearrange("p (g q) -> p g q", g=NG) for i in range(2)]
        smax = [sb(f"smax{i}", [P, HG]) for i in range(2)]
        sm = [sb(f"sm{i}", [P, HG, NK]) for i in range(2)]
        wide = [sb(f"wide{g}", [P, 512]) for g in range(NG)]
        pT = [w[0:NK, :].rearrange("k (h q) -> k h q", h=HG) for w in wide]
        p_hi, p_lo = ([lent(NK, HG * P // 2).bitcast(F16).rearrange("k (h q) -> k h q", h=HG)
                       for g in range(NG)] for part in range(2))
        osum = [lent(P, H * (DH + 1)).rearrange("p (h d) -> p h d", h=H) for i in range(2)]
        rden = [sb(f"rden{i}", [P, H]) for i in range(2)]
        oraw = [sb(f"oraw{i}", [P, P]) for i in range(2)]
        o = [lent(P, P) for i in range(2)]
        oT = [b[:, 0:P] for b in oxT]
        xeT = [b[:, P:2 * P] for b in oxT]
        qkv = [wide[i][:, 0:3 * P + 1] for i in range(2)]
        fmax = [sb(f"fmax{i}", [P, 2 * H]) for i in range(2)]
        fsub = [wide[2 + i][:, 0:2 * P] for i in range(2)]
        fexp = [wide[2 + i][:, 2 * P:4 * P] for i in range(2)]
        fsum = [sb(f"fsum{i}", [P, 2 * H]) for i in range(2)]
        frec = [sb(f"frec{i}", [P, 2 * H]) for i in range(2)]
        fsm = [sb(f"fsm{i}", [P, 2 * P]) for i in range(2)]


        def kvm(t):
            return kvm_all[:, bass.ds(t.n * (P + H), P + H)]
        qsT = [k_[:].rearrange("p h k -> p (h k)")[:, 0:P] for k_ in kblk]
        yg = [sb(f"yg{i}", [P, TOPK, P]) for i in range(2)]
        idx = [sb(f"idx{i}", [P, TOPK], I32) for i in range(2)]

        lg = sb("lg", [P, NT, E])
        lg2 = wide[2][:, 0:NT * E].rearrange("p (t e) -> p t e", e=E)
        eqs = wide[2][:, NT * E:2 * NT * E].rearrange("p (t e) -> p t e", e=E)
        top = sb("top", [P, TOPK, NT])
        first = sb("first", [P, TOPK, NT])
        oh = sb("oh", [P, NT, TOPK, E], BF16)
        delta = sb("delta", [P, NT])
        exd = sb("exd", [P, NT])
        wsum = sb("wsum", [P, NT])
        gate = sb("gate", [P, NT, TOPK])
        csum = sb("csum", [P, 4, P], BF16)
        cnt = sb("cnt", [P, E])
        cnt_i = sb("cnt_i", [P, E], I32)
        til_i = sb("til_i", [P, E], I32)
        til = sb("til", [P, E])
        tmp64 = sb("tmp64", [P, 2, E, E])
        t_start = sb("t_start", [P, E])
        t_end = sb("t_end", [P, E])
        row0 = sb("row0", [P, E])
        posn = wide[3][:].rearrange("p (c e) -> p c e", e=E)
        slot = sb("slot", [P, NPAIR])
        slot_i = sb("slot_i", [P, NPAIR], I32)
        ecmp = sb("ecmp", [1, NR, E])
        eacc = sb("eacc", [1, NR])
        e_i = sb("e_i", [1, NR], I32)

        xr = [sb(f"xr{i}", [P, P]) for i in range(2)]
        xh = [sb(f"xh{i}", [P, P], F32R) for i in range(2)]
        xl = [sb(f"xl{i}", [P, P], F32R) for i in range(2)]
        hs = [wide[2 + i][:, 0:F0] for i in range(2)]
        hh = [wide[i] for i in range(2)]
        hTh = [sb(f"hTh{i}", [P, F1], F32R) for i in range(2)]
        hTl = [sb(f"hTl{i}", [P, F1], F32R) for i in range(2)]
        ysb = oraw

        bank = [ctx.enter_context(nc.psum_tensor(f"bank{i}", [P, 512], F32)) for i in range(8)]

        xs_dram = nc.dram_tensor("xs_sorted", (NR * P, P), F32).ap()
        ys_dram = nc.dram_tensor("ys_sorted", (NR * P, P), F32).ap()

        block = ctx.enter_context(nc.Block())

        SWEEPS = [dict(l=0, n=NR, f=F0, shared=None, base=0),
                  dict(l=1, n=NT, f=F1, shared=0, base=NR),
                  dict(l=1, n=NR, f=F1, shared=None, base=NR + NT),
                  dict(l=1, n=NT, f=F1, shared=1, base=2 * NR + NT)]
        for s in SWEEPS:
            assert s["base"] % 2 == 0

        def split_count(t, gr):
            if gr == POOL_GROUP:
                return S("p_split_pool"), t.n + 1
            return S("p_split"), (NG - 1) * t.n + gr - (gr > POOL_GROUP) + 1

        def split_exps(eng, ops, t, gr):
            eng.wait_ge(S("exp_done"), NG * t.n + gr + 1)
            after(eng, S("pv_done"), NG * (t.n - 1) + gr + 1)
            ops.tensor_tensor(p_lo[gr][:], pT[gr], p_hi[gr][:], ALU.subtract).then_inc(split_count(t, gr)[0], 1)

        def by_head(ap):
            return ap.rearrange("p (h d) -> p h d", d=DH)

        def cols(s):
            return W0C if s["l"] == 0 else W1C

        @block.sync
        def _(sp):
            sp.dma_start(cst[:], a["cst"]).then_inc(S("cst_in"), 16)
            sp.dma_start(x_sb[:, 0:2, :], a["x"][0:2].rearrange("b s d -> s b d")).then_inc(S("x_in0"), 16)
            def weights(l, names, router):
                for i, n in enumerate(names):
                    sp.dma_start(wa[:, 4 * l + i, :], a[n]).then_inc(S(f"wa_in{l}"), 16)
                sp.dma_start(wr[:, l, :], a[router]).then_inc(S(f"wa_in{l}"), 16)

            def biases(l, first, names):
                for i, n in enumerate(names):
                    sp.dma_start(bias[:, first + i, :], a[n].partition_broadcast(P)).then_inc(S(f"bias_in{l}"), 16)

            weights(0, ("wq0", "wk0", "wv0", "wo0"), "wr0")
            for i, n in enumerate(("bq0", "bk0")):
                sp.dma_start(qk_col[:, i:i + 1], a[n].rearrange("(p o) -> p o", o=1)).then_inc(S("bias_in0"), 16)
            biases(0, 0, ("bv0", "bo0"))

            def second_loads():
                sp.dma_start(x_sb[:, 2:NT, :], a["x"][2:NT].rearrange("b s d -> s b d")).then_inc(S("x_in"), 16)
                sp.dma_start(b_st[0:E, :], a["eb0"]).then_inc(S("b_in"), 16)
                sp.dma_start(b_st[E:, :], a["eb1"]).then_inc(S("b_in"), 16)

            def later_loads(part):
                if part == 0:
                    weights(1, ("wq1", "wk1", "wv1", "wp1"), "wr1")
                    biases(1, 2, ("bq1", "bk1", "bv1", "bp1"))
                    sp.dma_start(rb[:], a["rb"].partition_broadcast(P)).then_inc(S("bias_in1"), 16)
                    sp.wait_ge(S("zeros_set"), 1)
                else:
                    for r in range((part - 1) * NR * P // 2, part * NR * P // 2, ZR * P):
                        sp.dma_start(xs_dram[r:r + ZR * P, :].rearrange("(p r) d -> p r d", r=ZR), zeros[:])\
                            .then_inc(S("xs_zeroed"), 16)

            def bias_rows(l, n):
                for i in range(3):
                    sp.dma_start(b_row[i:i + 1, 0:n * BC], b_part[i][l * E:l * E + n, :]).then_inc(S("b_row_in"), 16)

            def context(l, t, done):
                after(sp, S(done), t.n - 1)
                sp.dma_start(ctxT[t.par][:, 0:NK], a["ctxT"][bass.ds(t.n, 1)].rearrange("o d k -> d (o k)"))\
                    .then_inc(S(f"ctx_in{l}{t.par}"), 16)

            def feed(l, wsrc, c):
                def body(u, live):
                    if live(1) and l == 0:
                        t = u + 1
                        context(l, t, "v_done")
                    if live(0):
                        after(sp, S(f"w_split{l}"), u.n - 1)
                        sp.dma_start(w_st[:, u.par, 0:c], wsrc[:, bass.ds(u.n * c, c)])\
                            .then_inc(S(f"w_in{l}{u.par}"), 16)
                    if l == 0 and isinstance(u.n, int) and u.n <= 2:
                        if u.n < 0:
                            second_loads()
                        else:
                            later_loads(u.n)
                sweep(sp, NT, 1, 0, body)

            def rows(s):
                def body(u, live):
                    if live(2):
                        t = u + 2
                        after(sp, S("xT_done"), s["base"] + t.n - 1)
                        sp.dma_start(xr[t.par][:], xs_dram[bass.ds(t.n * P, P), :])\
                            .then_inc(S(f"xr_in{s['l']}{t.par}"), 16)
                    if live(-3):
                        t = u + -3
                        sp.wait_ge(S("y_ready"), s["base"] + t.n + 1)
                        sp.dma_start(ys_dram[bass.ds(t.n * P, P), :], ysb[t.par][:])\
                            .then_inc(S(f"y_out{s['l']}{t.par}"), 16)
                sweep(sp, s["n"], 2, 3, body)

            feed(0, a["w0"], C0)
            sp.wait_ge(S("v_done"), NT)
            sweep(sp, NT, 0, 0, lambda u, live: context(1, u, "kc_done"))
            sp.wait_ge(S("b_split"), 4)
            bias_rows(0, E)
            sp.wait_ge(S("rows0"), TOPK * 16 * NT)
            rows(SWEEPS[0])
            sp.wait_ge(S("y_out00"), 16 * NR // 2)
            sp.wait_ge(S("y_out01"), 16 * NR // 2)
            bias_rows(1, E + NSH)
            feed(1, a["w1"], C1)
            sp.wait_ge(S("rows1"), TOPK * 16 * NT)
            rows(SWEEPS[2])
            sp.wait_ge(S("y_out10"), 16 * NR // 2)
            sp.wait_ge(S("y_out11"), 16 * NR // 2)

            def store(u, live):
                sp.wait_ge(S("x_final"), u.n + 1)
                sp.dma_start(out[bass.ds(u.n, 1)].rearrange("o s d -> s (o d)"),
                             x_sb[:, bass.ds(u.n, 1), :].rearrange("p o d -> p (o d)")).then_inc(S("stored"), 16)
            sweep(sp, NT, 0, 0, store)
            sp.wait_ge(S("stored"), 16 * NT)

        @block.gpsimd
        def _(pool):
            g = nc.gpsimd
            g.memset(zeros[:], 0.0).then_inc(S("zeros_set"), 1)
            g.memset(half_neg[:], -0.5).then_inc(S("pool_const"), 1)
            for i in range(2):
                g.memset(vpart[i][:, :, 0, DH:DH + 1], 1.0).then_inc(S("pool_const"), 1)
                g.memset(vpart[i][:, :, 1:3, DH:DH + 1], 0.0).then_inc(S("pool_const"), 1)
                g.memset(qz[i][:], 0.0).then_inc(S("pool_const"), 1)
                g.memset(ctxT[i][:, NK:P], 0.0).then_inc(S("pool_const"), 1)
            pool.wait_ge(S("pool_const"), 9)
            pool.wait_ge(S("bias_in0"), 16 * 4)
            pool.wait_ge(S("cst_in"), 16)

            def split_biases(step):
                if step == 0:
                    pool.wait_ge(S("b_in"), 32)
                    g.tensor_copy(b_part[0][:], b_st).then_inc(S("b_split"), 1)
                    return
                pool.wait_ge(S("b_split"), step)
                if step == 1:
                    g.tensor_tensor(b_rest, b_st, b_part[0][:], ALU.subtract).then_inc(S("b_split"), 1)
                elif step == 2:
                    g.tensor_copy(b_part[1][:], b_rest).then_inc(S("b_split"), 1)
                else:
                    g.tensor_tensor(b_part[2][:], b_rest, b_part[1][:], ALU.subtract).then_inc(S("b_split"), 1)

            def inverse_std(tag, w, t):
                pool.wait_ge(S(f"{tag}_var"), t.n + 1)
                apart(pool, S("pool_apart"))
                g.tensor_scalar(vareps[w][t.par][:], meanv[w][t.par][:, 1:2], EPS, None, ALU.add)\
                    .then_inc(S(f"{tag}_eps"), 1)
                pool.wait_ge(S(f"{tag}_eps"), t.n + 1)
                g.tensor_tensor(rstd[w][t.par][:], vareps[w][t.par][:], half_neg[:], ALU.pow)\
                    .then_inc(S(f"{tag}_rstd"), 1)

            def split_weights(l, c, t):
                pool.wait_ge(S(f"w_half{l}"), t.n + 1)
                g.tensor_tensor(w_r[:, 1, bass.ds(t.n * c, c)], w_st[:, t.par, 0:c],
                                w_r[:, 0, bass.ds(t.n * c, c)].bitcast(F32), ALU.subtract)\
                    .then_inc(S(f"w_split{l}"), 1)

            def residual_bias(l, b, normed, t):
                pool.wait_ge(S(normed), t.n + 1)
                xt = x_sb[:, bass.ds(t.n, 1), :].rearrange("p o d -> p (o d)")
                g.tensor_tensor(xt, xt, bias[:, b, :], ALU.add).then_inc(S(f"x_bias{l}"), 1)

            def attention0(u, live):
                if live(-1):
                    split_exps(pool, g, u + -1, 1)
                if live(-2):
                    t = u + -2
                    pool.wait_ge(S("o_raw0"), t.n + 1)
                    after(pool, S("ox_done"), t.n - 1)
                    g.tensor_tensor(o[t.par][:], oraw[t.par][:], bias[:, 0, :], ALU.add).then_inc(S("o_ready0"), 1)
                if live(-3):
                    inverse_std("lne0", 1, u + -3)
                if live(1):
                    t = u + 1
                    pool.wait_ge(S("kf_ready"), t.n + 1)
                    after(pool, S("s_done"), NG * (t.n - 1))
                    g.tensor_tensor(kblk[t.par][:], kf[t.par][:].unsqueeze(1).to_broadcast([P, HG, NK]),
                                    cst[:, K_H4:K_REV].unsqueeze(2).to_broadcast([P, HG, NK]), ALU.mult)\
                        .then_inc(S("kblk_ready"), 1)
                if live(0):
                    pool.wait_ge(S("v_rest"), u.n + 1)
                    after(pool, S("pv_done"), NG * (u.n - 1))
                    apart(pool, S("pool_apart"))
                    vr = vrest[u.par][:].rearrange("k (h d) -> k h d", d=DH)
                    g.tensor_copy(vpart[u.par][:, :, 1, 0:DH], vr).then_inc(S("v_part2"), 1)
                    pool.wait_ge(S("v_part2"), u.n + 1)
                    g.tensor_tensor(vpart[u.par][:, :, 2, 0:DH], vr, vpart[u.par][:, :, 1, 0:DH], ALU.subtract)\
                        .then_inc(S("v_ready"), 1)
                if live(2):
                    inverse_std("ln0", 0, u + 2)
                if live(-1):
                    residual_bias(0, 1, "xn_ready0", u + -1)
                if live(-1):
                    split_weights(0, C0, u + -1)
                if isinstance(u.n, int) and 1 <= u.n <= 4:
                    split_biases(u.n - 1)
            sweep(pool, NT, 2, 3, attention0)

            def scatter(l):
                pool.wait_ge(S("slots"), l + 1)
                pool.wait_ge(S(f"xn_kept{l}"), NT)
                if l == 0:
                    for i in range(2):
                        g.memset(qkv[i][:, 3 * P:3 * P + 1], 1.0).then_inc(S("v_ones"), 1)
                    pool.wait_ge(S("xs_zeroed"), 16 * (NR // ZR))
                for t in range(NT):
                    for c in range(TOPK):
                        g.indirect_dma_start(xs_dram, bass.IndirectOffsetOnAxis(
                            ap=slot_i[:, TOPK * t + c:TOPK * t + c + 1], axis=0), xn_sb[:, t, :], None)\
                            .then_inc(S(f"rows{l}"), 16)

            def gather(l, t):
                after(pool, S(("combined0", "x_final")[l]), t.n - 1)
                if isinstance(t.n, int):
                    cols_ = [slot_i[:, TOPK * t.n + c:TOPK * t.n + c + 1] for c in range(TOPK)]
                    apart(pool, S("pool_apart"))
                    if l == 0:
                        g.tensor_copy(idx[t.par][:], slot_i[:, TOPK * t.n:TOPK * (t.n + 1)])\
                            .then_inc(S(f"ga_idx{l}"), 1)
                else:
                    g.tensor_copy(idx[t.par][:], slot_i[:, bass.ds(TOPK * t.n, TOPK)]).then_inc(S(f"ga_idx{l}"), 1)
                    pool.wait_ge(S(f"ga_idx{l}"), t.n + 1)
                    apart(pool, S("pool_apart"))
                    cols_ = [idx[t.par][:, c:c + 1] for c in range(TOPK)]
                for c in range(TOPK):
                    g.indirect_dma_start(yg[t.par][:, c, :], None, ys_dram,
                                         bass.IndirectOffsetOnAxis(ap=cols_[c], axis=0))\
                        .then_inc(S(f"yg_in{l}{t.par}"), 16)

            scatter(0)
            for p in range(2):
                pool.wait_ge(S(f"y_out0{p}"), 16 * NR // 2)
            pool.wait_ge(S("bias_in1"), 16 * 5)

            def attention1(u, live):
                if live(4):
                    gather(0, u + 4)
                if live(0):
                    residual_bias(1, 5, "xn_ready1", u)
                if live(3):
                    inverse_std("ln1", 0, u + 3)
                if live(-2):
                    split_weights(1, C1, u + -2)
                if live(-1):
                    inverse_std("lne1", 1, u + -1)
            sweep(pool, NT, 4, 2, attention1)
            scatter(1)

            for p in range(2):
                pool.wait_ge(S(f"y_out1{p}"), 16 * NR // 2)
            for t in range(NT):
                gather(1, Tile(0, t))

        @block.scalar
        def _(act):
            s_ = nc.scalar
            act.wait_ge(S("bias_in0"), 16 * 4)
            act.wait_ge(S("pool_const"), 9)

            def copy_out(dst, src):
                return s_.activation(dst, src, ACT.Copy)

            def weights_hi(l, c, t):
                act.wait_ge(S(f"w_in{l}{t.par}"), 16 * (t.half + 1))
                copy_out(w_r[:, 0, bass.ds(t.n * c, c)], w_st[:, t.par, 0:c]).then_inc(S(f"w_half{l}"), 1)

            def keep_expert_input(l, t):
                act.wait_ge(S(f"xe_ready{l}"), t.n + 1)
                copy_out(xn_sb[:, bass.ds(t.n, 1), :].rearrange("p o d -> p (o d)"), xe[t.par][:])\
                    .then_inc(S(f"xn_kept{l}"), 1)

            def attention0(u, live):
                def exps(t, gr):
                    G = NG * t.n + gr
                    src = bank[2 + gr % 2][0:NK, :].rearrange("k (h q) -> k h q", h=HG)
                    act.wait_ge(S("t_done"), G + 1)
                    after(act, *split_count(t + -1, gr))
                    s_.activation(pT[gr], src, ACT.Exp, scale=SCALE)
                    after(act, S("pv_done"), G - NG + 1)
                    s_.activation(p_hi[gr][:], src, ACT.Exp, scale=SCALE).then_inc(S("exp_done"), 1)
                if live(-1):
                    exps(u + -1, 2)
                if live(1):
                    t = u + 1
                    act.wait_ge(S("kx_done"), t.n + 1)
                    after(act, S("qT_done"), t.n - 1)
                    copy_out(xnT[t.par][:], bank[4][:, 0:P]).then_inc(S("xnT_ready0"), 1)
                    after(act, S("kblk_ready"), t.n - 1)
                    s_.activation(kf[t.par][:], bank[4][:, P:P + NK], ACT.Identity, bias=qk_col[:, 1:2])\
                        .then_inc(S("kf_ready"), 1)
                if live(0):
                    act.wait_ge(S("v_done"), u.n + 1)
                    after(act, S("pv_done"), NG * (u.n - 1))
                    copy_out(vpart[u.par][:, :, 0, 0:DH], bank[4][0:NK, 2 * P:3 * P].rearrange("k (h d) -> k h d", d=DH))\
                        .then_inc(S("v_part1"), 1)
                if live(-1):
                    exps(u + -1, 3)
                if live(-2) or live(-4):
                    w = u + -2
                    c = slice(0 if live(-2) else P, 2 * P if live(-4) else P)
                    act.wait_ge(S("ox_done"), w.n + 1)
                    after(act, S("pl_done"), w.n - 1)
                    copy_out(oxT[w.par][:, c], bank[7][:, c]).then_inc(S("ox_ready"), 1)
                if live(0):
                    exps(u, 0)
                if live(1):
                    t = u + 1
                    act.wait_ge(S("qT_done"), t.n + 1)
                    after(act, S("s_done"), NG * (t.n - 1))
                    for gr in range(NG):
                        r = slice(32 * gr, 32 * gr + 32)
                        last = s_.activation(qz[t.par][r, gr, :], bank[4][r, 3 * P:4 * P], ACT.Identity,
                                             bias=qk_col[r, 0:1])
                    last.then_inc(S("qT_ready"), 1)
                if live(0):
                    exps(u, 1)
                if live(0):
                    weights_hi(0, C0, u)
                if live(-4):
                    keep_expert_input(0, u + -4)
            sweep(act, NT, 1, 4, attention0)

            def gate_exp(l):
                act.wait_ge(S("delta"), l + 1)
                s_.activation(exd[:], delta[:], ACT.Exp).then_inc(S("exd"), 1)

            def experts(s):
                b, nf = s["base"], s["f"]

                def body(u, live):
                    if live(-1):
                        t = u + -1
                        act.wait_ge(S("hT_done"), b + t.n + 1)
                        after(act, S("down_done"), b + t.n - 1)
                        copy_out(hTh[t.par][:, 0:nf], bank[2 + t.par][:, 0:nf]).then_inc(S("hTh_ready"), 1)
                    if live(1):
                        t = u + 1
                        act.wait_ge(S("xT_done"), b + t.n + 1)
                        after(act, S("up_done"), b + t.n - 1)
                        copy_out(xh[t.par][:], bank[6][:, 0:P]).then_inc(S("xh_ready"), 1)
                    if live(0):
                        act.wait_ge(S("up_done"), b + u.n + 1)
                        if s["l"] == 0:
                            after(act, S("h_ready"), b + u.n - 1)
                            s_.activation(hs[u.par][:], bank[u.par][:, 0:F0], ACT.Silu).then_inc(S("silu_done"), 1)
                        else:
                            after(act, S("hT_done"), b + u.n - 1)
                            s_.activation(hh[u.par][:], bank[u.par][:], ACT.Gelu).then_inc(S("h_ready"), 1)
                sweep(act, s["n"], 1, 1, body)

            gate_exp(0)

            def context1(u, live):
                act.wait_ge(S("c_sub"), u.n + 1)
                after(act, S("c_soft"), u.n - 1)
                s_.activation(fexp[u.par][:, P:2 * P], fsub[u.par][:, P:2 * P], ACT.Exp).then_inc(S("c_exp"), 1)
            sweep(act, NT, 0, 0, context1)
            experts(SWEEPS[0])

            def attention1(u, live):
                if live(0):
                    act.wait_ge(S("f_sub"), u.n + 1)
                    after(act, S("f_soft"), u.n - 1)
                    s_.activation(fexp[u.par][:, 0:P], fsub[u.par][:, 0:P], ACT.Exp).then_inc(S("f_exp"), 1)
                if live(0):
                    act.wait_ge(S("qsT_done"), u.n + 1)
                    after(act, S("num_done"), u.n - 1)
                    after(act, S("oT_ready1"), u.n - 1)
                    copy_out(qsT[u.par][:], bank[3][:, 0:P]).then_inc(S("qsT_ready"), 1)
                if live(-2):
                    t = u + -2
                    act.wait_ge(S("xeT_done1"), t.n + 1)
                    after(act, S("logit_done1"), t.n - 1)
                    copy_out(xeT[t.par], bank[7][:, 0:P]).then_inc(S("xeT_ready1"), 1)
                if live(2):
                    t = u + 2
                    act.wait_ge(S("xnT_done1"), t.n + 1)
                    after(act, S("q1_done"), t.n - 1)
                    copy_out(xnT[t.par][:], bank[0][:, 0:P]).then_inc(S("xnT_ready1"), 1)
                if live(-2):
                    keep_expert_input(1, u + -2)
                if live(-2):
                    weights_hi(1, C1, u + -2)
            act.wait_ge(S("down_done"), NR)
            sweep(act, NT, 2, 2, attention1)
            gate_exp(1)
            for s in SWEEPS[1:]:
                experts(s)

        @block.vector
        def _(dve):
            v = nc.vector
            dve.wait_ge(S("cst_in"), 16)
            v.tensor_copy(tri[:], cst[:, K_TRI:K_PAIR]).then_inc(S("dve_const"), 1)
            v.tensor_copy(pairm[:], cst[:, K_PAIR:K_SAME]).then_inc(S("dve_const"), 1)
            v.tensor_copy(same[:], cst[:, K_SAME:K_BD]).then_inc(S("dve_const"), 1)
            v.memset(ones_b[:], 1.0).then_inc(S("dve_const"), 1)
            v.memset(ones_3[:], 1.0).then_inc(S("dve_const"), 1)
            dve.wait_ge(S("bias_in0"), 16 * 4)
            dve.wait_ge(S("pool_const"), 9)

            def xt(t):
                return x_sb[:, bass.ds(t.n, 1), :].rearrange("p o d -> p (o d)")

            def ln_stats(tag, w, t):
                apart(dve, S("dve_apart"))
                v.bn_stats(stats[w][t.par][:], xt(t)).then_inc(S(f"{tag}_stats"), 1)

            def ln_var(tag, w, t):
                dve.wait_ge(S(f"{tag}_stats"), t.n + 1)
                apart(dve, S("dve_apart"))
                v.bn_aggr(meanv[w][t.par][:], stats[w][t.par][:]).then_inc(S(f"{tag}_var"), 1)

            def ln_apply(tag, w, t, dst):
                dve.wait_ge(S(f"{tag}_rstd"), t.n + 1)
                return v.tensor_scalar(dst, xt(t), meanv[w][t.par][:, 0:1], rstd[w][t.par][:],
                                       ALU.subtract, ALU.mult)

            def expert_input(l, t):
                after(dve, S(f"xeT_done{l}"), t.n - 1)
                after(dve, S(f"xn_kept{l}"), t.n - 1)
                ln_apply(f"lne{l}", 1, t, xe[t.par][:]).then_inc(S(f"xe_ready{l}"), 1)

            def attention0(u, live):
                def score(gr):
                    return bank[gr % 2][:, 0:HG * NK].rearrange("q (h k) -> q h k", h=HG)

                def score_max(gr):
                    dve.wait_ge(S("s_done"), NG * u.n + gr + 1)
                    v.reduce_max(smax[gr % 2][:], score(gr), AX.X).then_inc(S("s_max"), 1)

                def score_sub(gr):
                    G = NG * u.n + gr
                    dve.wait_ge(S("s_max"), G + 1)
                    after(dve, S("t_done"), G - 1)
                    v.tensor_tensor(sm[gr % 2][:], score(gr), smax[gr % 2][:].unsqueeze(2).to_broadcast([P, HG, NK]),
                                    ALU.subtract).then_inc(S("s_sub"), 1)

                done, added, ahead = u + -2, u + -3, u + 2
                ov = osum[done.par]
                if live(-2):
                    dve.wait_ge(S("pv_done"), NG * (done.n + 1))
                    v.reduce_sum(ov[:], bank[5 + done.par][:, 0:3 * H * (DH + 1)]
                                 .rearrange("q (h c d) -> q h d c", h=H, c=3), AX.X).then_inc(S("o_sum"), 1)
                if live(0):
                    score_max(0)
                if live(-2):
                    dve.wait_ge(S("o_sum"), done.n + 1)
                    v.reciprocal(rden[done.par][:], ov[:, :, DH]).then_inc(S("rden0"), 1)
                if live(0):
                    score_sub(0)
                if live(-2):
                    dve.wait_ge(S("rden0"), done.n + 1)
                    after(dve, S("o_ready0"), done.n - 1)
                    v.tensor_tensor(oraw[done.par][:].rearrange("q (h d) -> q h d", h=H), ov[:, :, 0:DH],
                                    rden[done.par][:].unsqueeze(2).to_broadcast([P, H, DH]), ALU.mult)\
                        .then_inc(S("o_raw0"), 1)
                if live(0):
                    dve.wait_ge(S("v_part1"), u.n + 1)
                    after(dve, S("v_ready"), u.n - 1)
                    v.tensor_tensor(vrest[u.par][:].rearrange("k (h d) -> k h d", d=DH),
                                    bank[4][0:NK, 2 * P:3 * P].rearrange("k (h d) -> k h d", d=DH),
                                    vpart[u.par][:, :, 0, 0:DH], ALU.subtract).then_inc(S("v_rest"), 1)
                if live(-3) or live(-5):
                    dve.wait_ge(S("pl_done"), added.n + 1)
                if live(-5):
                    t = u + -5
                    lgt = lg[:, bass.ds(t.n, 1), :].rearrange("p o e -> p (o e)")
                    v.tensor_copy(lgt, bank[7][:, 3 * P:3 * P + E])\
                        .then_inc(S("lg_ready0"), 1)
                    if not live(-3):
                        dve.wait_ge(S("lg_ready0"), t.n + 1)
                if live(-3):
                    dve.wait_ge(S("x_bias0"), added.n + 1)
                    v.tensor_tensor(xt(added), xt(added), bank[7][:, 2 * P:3 * P], ALU.add).then_inc(S("x_added0"), 1)
                if live(0):
                    score_max(1)
                if live(-3):
                    dve.wait_ge(S("x_added0"), added.n + 1)
                    ln_stats("lne0", 1, added)
                if live(0):
                    score_sub(1)
                if live(-3):
                    ln_var("lne0", 1, added)
                if live(-1):
                    split_exps(dve, v, u + -1, 2)
                if live(0):
                    score_max(2)
                if live(2):
                    if isinstance(ahead.n, int) and ahead.n == 0:
                        dve.wait_ge(S("x_in0"), 16)
                    if isinstance(ahead.n, int) and ahead.n == 2:
                        dve.wait_ge(S("x_in"), 16)
                    ln_stats("ln0", 0, ahead)
                if live(0):
                    score_sub(2)
                if live(2):
                    ln_var("ln0", 0, ahead)
                if live(-1):
                    split_exps(dve, v, u + -1, 3)
                if live(0):
                    score_max(3)
                if live(-3):
                    after(dve, S("ox_done"), added.n + 1)
                    after(dve, S("xn_kept0"), added.n - 1)
                    ln_apply("lne0", 1, added, xe[added.par][:]).then_inc(S("xe_ready0"), 1)
                if live(0):
                    score_sub(3)
                    split_exps(dve, v, u, 0)
                if live(2):
                    after(dve, S("kx_done"), ahead.n - 1)
                    ln_apply("ln0", 0, ahead, xn[ahead.par][:]).then_inc(S("xn_ready0"), 1)
            sweep(dve, NT, 2, 5, attention0)

            def route(l):
                count = [0]
                link_sem = S(f"route{l}")

                def link(ins):
                    count[0] += 1
                    ins.then_inc(link_sem, 1)
                    dve.wait_ge(link_sem, count[0])

                def over_e(ap):
                    return ap.unsqueeze(2).to_broadcast([P, NT, E])

                rev = cst[:, K_REV:K_LT].unsqueeze(1).to_broadcast([P, NT, E])
                dve.wait_ge(S(f"lg_ready{l}"), NT)
                src = lg
                for c in range(TOPK):
                    link(v.reduce_max(top[:, c, :], src[:], AX.X))
                    link(v.tensor_tensor(eqs[:], src[:], over_e(top[:, c, :]), ALU.is_equal))
                    link(v.tensor_tensor(eqs[:], eqs[:], rev, ALU.mult))
                    link(v.reduce_max(first[:, c, :], eqs[:], AX.X))
                    link(v.tensor_tensor(oh[:, :, c, :], rev, over_e(first[:, c, :]), ALU.is_equal))
                    if c == 0:
                        link(v.tensor_scalar(eqs[:], oh[:, :, 0, :], -BIG, None, ALU.mult))
                        link(v.tensor_tensor(lg2[:], eqs[:], lg[:], ALU.add))
                        src = lg2
                v.tensor_tensor(delta[:], top[:, 1, :], top[:, 0, :], ALU.subtract).then_inc(S("delta"), 1)
                dve.wait_ge(S("colsum"), l + 1)
                link(v.tensor_copy(csum[:], bank[7][:, 0:4].unsqueeze(2).to_broadcast([P, 4, P])))
                v.tensor_copy(ones_b[:], ones_b[:]).then_inc(S("csum"), 1)
                dve.wait_ge(S("counts"), l + 1)
                link(v.tensor_scalar(cnt[:], bank[7][:, 16:16 + E], float(P - 1), None, ALU.add))
                link(v.tensor_copy(cnt_i[:], cnt[:]))
                link(v.tensor_single_scalar(til_i[:], cnt_i[:], 7, ALU.arith_shift_right))
                link(v.tensor_copy(til[:], til_i[:]))
                tb = til[:].unsqueeze(1).to_broadcast([P, E, E])
                for i, (k, dst) in enumerate(((K_LT, t_start), (K_LE, t_end))):
                    link(v.tensor_tensor(tmp64[:, i], tb, cst[:, k:k + E * E].rearrange("p (a b) -> p a b", a=E),
                                         ALU.mult))
                    link(v.reduce_sum(dst[:], tmp64[:, i], AX.X))
                link(v.tensor_scalar(row0[:], t_start[:], float(P), None, ALU.mult))
                link(v.tensor_tensor(posn[:], bank[5][:].rearrange("p (c e) -> p c e", e=E),
                                     row0[:].unsqueeze(1).to_broadcast([P, NPAIR, E]), ALU.add))
                link(v.tensor_tensor(posn[:], posn[:], oh[:].rearrange("p t c e -> p (t c) e"), ALU.mult))
                link(v.reduce_sum(slot[:], posn[:], AX.X))
                v.tensor_copy(slot_i[:], slot[:]).then_inc(S("slots"), 1)
                link(v.tensor_tensor(ecmp[:], t_end[0:1, :].unsqueeze(1).to_broadcast([1, NR, E]),
                                     cst[0:1, K_TILE:K_TILE + NR].unsqueeze(2).to_broadcast([1, NR, E]), ALU.is_le))
                link(v.reduce_sum(eacc[:], ecmp[:], AX.X))
                link(v.tensor_scalar(eacc[:], eacc[:], float(E - 1), None, ALU.min))
                v.tensor_copy(e_i[:], eacc[:]).then_inc(S("emap"), 1)
                dve.wait_ge(S("exd"), l + 1)
                link(v.tensor_scalar(wsum[:], exd[:], 1.0, None, ALU.add))
                link(v.reciprocal(gate[:, :, 0], wsum[:]))
                link(v.tensor_tensor(gate[:, :, 1], exd[:], gate[:, :, 0], ALU.mult))

            def experts(s):
                b, nf = s["base"], s["f"]

                def body(u, live):
                    if live(-1):
                        t = u + -1
                        dve.wait_ge(S("hTh_ready"), b + t.n + 1)
                        v.tensor_tensor(hTl[t.par][:, 0:nf], bank[2 + t.par][:, 0:nf], hTh[t.par][:, 0:nf].bitcast(F32),
                                        ALU.subtract).then_inc(S("hTl_ready"), 1)
                    if live(1):
                        t = u + 1
                        dve.wait_ge(S("xh_ready"), b + t.n + 1)
                        v.tensor_tensor(xl[t.par][:], bank[6][:, 0:P], xh[t.par][:].bitcast(F32), ALU.subtract)\
                            .then_inc(S("xl_ready"), 1)
                    if live(0) and s["l"] == 0:
                        dve.wait_ge(S("silu_done"), b + u.n + 1)
                        after(dve, S("hT_done"), b + u.n - 1)
                        v.tensor_tensor(hh[u.par][:, 0:F0], hs[u.par][:], bank[u.par][:, F0:2 * F0], ALU.mult)\
                            .then_inc(S("h_ready"), 1)
                    if live(2) and s["shared"] is not None:
                        t = u + 2
                        after(dve, S("xT_done"), b + t.n - 1)
                        v.tensor_copy(xr[t.par][:], xn_sb[:, bass.ds(t.n, 1), :].rearrange("p o d -> p (o d)"))\
                            .then_inc(S("xr_copied"), 1)
                    if live(-2):
                        t = u + -2
                        dve.wait_ge(S("down_done"), b + t.n + 1)
                        bk = bank[4 + t.par]
                        if s["shared"] is not None:
                            v.scalar_tensor_tensor(xt(t), bk[:, 0:P], 1.0 / NSH, xt(t), ALU.mult, ALU.add)\
                                .then_inc(S("y_half"), 1)
                            dve.wait_ge(S("y_half"), s["shared"] * NT + t.n + 1)
                            v.scalar_tensor_tensor(xt(t), bk[:, P:2 * P], 1.0 / NSH, xt(t), ALU.mult, ALU.add)\
                                .then_inc(S("y_ready"), 1)
                        else:
                            after(dve, S(f"y_out{s['l']}{t.par}"), 16 * t.half)
                            v.reduce_sum(ysb[t.par][:], bk[:, 0:2 * P].rearrange("p (a d) -> p d a", a=2), AX.X)\
                                .then_inc(S("y_ready"), 1)
                    if s["shared"] == 1 and live(-6):
                        dve.wait_ge(S("y_ready"), b + u.n - 6 + 1)
                        combine(1, u + -6, 0, "comb1")
                        dve.wait_ge(S("comb1"), u.n - 6 + 1)
                        combine(1, u + -6, 1, "x_final")
                sweep(dve, s["n"], 2, 6 if s["shared"] == 1 else 2, body)

            def combine(l, t, c, done):
                dve.wait_ge(S(f"yg_in{l}{t.par}"), 32 * (t.half + 1))
                v.scalar_tensor_tensor(xt(t), yg[t.par][:, c, :], gate[:, bass.ds(t.n, 1), c], xt(t),
                                       ALU.mult, ALU.add).then_inc(S(done), 1)

            route(0)

            def feature_softmax(tag, part, used, t):
                c, h = slice(part * P, (part + 1) * P), slice(part * H, (part + 1) * H)

                def exp_sum():
                    dve.wait_ge(S(f"{tag}_exp"), t.n + 1)
                    v.reduce_sum(fsum[t.par][:, h], by_head(fexp[t.par][:, c]), AX.X).then_inc(S(f"{tag}_sum"), 1)

                def exp_rec():
                    dve.wait_ge(S(f"{tag}_sum"), t.n + 1)
                    v.reciprocal(frec[t.par][:, h], fsum[t.par][:, h]).then_inc(S(f"{tag}_rec"), 1)

                def exp_soft():
                    dve.wait_ge(S(f"{tag}_rec"), t.n + 1)
                    after(dve, S(used), t.n - 1)
                    v.tensor_tensor(by_head(fsm[t.par][:, c]), by_head(fexp[t.par][:, c]),
                                    frec[t.par][:, h].unsqueeze(2).to_broadcast([P, H, DH]), ALU.mult)\
                        .then_inc(S(f"{tag}_soft"), 1)
                return exp_sum, exp_rec, exp_soft

            def context1(u, live):
                old = u + -2
                k = by_head(qkv[u.par][:, P:2 * P])
                exp_sum, exp_rec, exp_soft = feature_softmax("c", 1, "kvp_done", u + -1)
                if live(-1):
                    exp_sum()
                if live(0):
                    dve.wait_ge(S("kc_done"), u.n + 1)
                    after(dve, S("kvp_done"), u.n - 1)
                    v.tensor_tensor(qkv[u.par][:, P:3 * P], bank[u.par][:, 0:2 * P],
                                    bias[:, 3:5, :].rearrange("p i d -> p (i d)"), ALU.add).then_inc(S("c_bias"), 1)
                if live(-1):
                    exp_rec()
                if live(0):
                    dve.wait_ge(S("c_bias"), u.n + 1)
                    v.reduce_max(fmax[u.par][:, H:2 * H], k, AX.X).then_inc(S("c_max"), 1)
                if live(-1):
                    exp_soft()
                if live(0):
                    dve.wait_ge(S("c_max"), u.n + 1)
                    after(dve, S("c_exp"), u.n - 1)
                    v.tensor_tensor(by_head(fsub[u.par][:, P:2 * P]), k,
                                    fmax[u.par][:, H:2 * H].unsqueeze(2).to_broadcast([P, H, DH]), ALU.subtract)\
                        .then_inc(S("c_sub"), 1)
                if live(-2):
                    dve.wait_ge(S("kvp_done"), old.n + 1)
                    v.tensor_tensor(kvm(old)[:, 0:P], bank[2 + old.par][:, 0:P], cst[:, K_BD:K_H16], ALU.mult)\
                        .then_inc(S("kvm_ready"), 1)
                    v.tensor_scalar(kvm(old)[:, P:P + H], cst[:, K_H16:K_H4], bank[2 + old.par][:, P:P + 1], None,
                                    ALU.mult).then_inc(S("kvm_ready"), 1)
            dve.wait_ge(S("bias_in1"), 16 * 5)
            sweep(dve, NT, 0, 2, context1)
            experts(SWEEPS[0])

            def attention1(u, live):
                q, done, ahead = u + 1, u + -1, u + 3
                exp_sum, exp_rec, exp_soft = feature_softmax("f", 0, "qsT_done", u)
                if live(0):
                    exp_sum()
                if live(1):
                    dve.wait_ge(S("q1_done"), q.n + 1)
                    v.tensor_tensor(qkv[q.par][:, 0:P], bank[1][:, 0:P], bias[:, 2, :], ALU.add)\
                        .then_inc(S("f_bias"), 1)
                if live(0):
                    exp_rec()
                if live(1):
                    dve.wait_ge(S("f_bias"), q.n + 1)
                    v.reduce_max(fmax[q.par][:, 0:H], by_head(qkv[q.par][:, 0:P]), AX.X)\
                        .then_inc(S("f_max"), 1)
                if live(0):
                    exp_soft()
                if live(1):
                    dve.wait_ge(S("f_max"), q.n + 1)
                    after(dve, S("f_exp"), q.n - 1)
                    v.tensor_tensor(by_head(fsub[q.par][:, 0:P]), by_head(qkv[q.par][:, 0:P]),
                                    fmax[q.par][:, 0:H].unsqueeze(2).to_broadcast([P, H, DH]), ALU.subtract)\
                        .then_inc(S("f_sub"), 1)
                if live(-1):
                    dve.wait_ge(S("num_done"), done.n + 1)
                    v.reciprocal(rden[done.par][:], bank[4][:, P:P + H]).then_inc(S("rden1"), 1)
                if live(-2):
                    expert_input(1, u + -2)
                if live(-1):
                    dve.wait_ge(S("rden1"), done.n + 1)
                    after(dve, S("oT_done1"), done.n - 1)
                    v.tensor_tensor(oraw[done.par][:].rearrange("q (h d) -> q h d", h=H),
                                    bank[4][:, 0:P].rearrange("q (h d) -> q h d", h=H),
                                    rden[done.par][:].unsqueeze(2).to_broadcast([P, H, DH]), ALU.mult)\
                        .then_inc(S("o_raw1"), 1)
                if live(3):
                    combine(0, ahead, 0, "comb0")
                if live(2):
                    t = u + 2
                    after(dve, S("xnT_done1"), t.n - 1)
                    ln_apply("ln1", 0, t, xn[t.par][:]).then_inc(S("xn_ready1"), 1)
                if live(3):
                    dve.wait_ge(S("comb0"), ahead.n + 1)
                    combine(0, ahead, 1, "combined0")
                if live(-1):
                    dve.wait_ge(S("oT_done1"), done.n + 1)
                    dve.wait_ge(S("qsT_ready"), done.n + 1)
                    after(dve, S("proj_done1"), done.n - 1)
                    v.tensor_tensor(oT[done.par], bank[5][:, 0:P], qsT[done.par][:], ALU.add)\
                        .then_inc(S("oT_ready1"), 1)
                if live(3):
                    dve.wait_ge(S("combined0"), ahead.n + 1)
                    ln_stats("ln1", 0, ahead)
                if live(-1):
                    dve.wait_ge(S("proj_done1"), done.n + 1)
                    dve.wait_ge(S("x_bias1"), done.n + 1)
                    v.tensor_tensor(xt(done), xt(done), bank[6][:, 0:P], ALU.add).then_inc(S("x_added1"), 1)
                if live(3):
                    ln_var("ln1", 0, ahead)
                if live(-1):
                    dve.wait_ge(S("x_added1"), done.n + 1)
                    ln_stats("lne1", 1, done)
                if live(-2):
                    t = u + -2
                    dve.wait_ge(S("logit_done1"), t.n + 1)
                    v.tensor_tensor(lg[:, bass.ds(t.n, 1), :].rearrange("p o e -> p (o e)"), bank[7][:, 2 * P:2 * P + E],
                                    rb[:], ALU.add).then_inc(S("lg_ready1"), 1)
                if live(-1):
                    ln_var("lne1", 1, done)
            sweep(dve, NT, 3, 2, attention1)
            route(1)
            dve.wait_ge(S("xn_kept1"), NT)
            for s in SWEEPS[1:]:
                experts(s)

        @block.tensor
        def _(pe):
            mm = nc.tensor.matmul
            pe.wait_ge(S("cst_in"), 16)
            pe.wait_ge(S("wa_in0"), 16 * 5)
            pe.wait_ge(S("dve_const"), 5)

            def one(out_, l_, r_):
                return mm(out_, l_, r_, start=True, stop=True)

            def turn(out_, in_):
                return nc.tensor.transpose(out_, in_, ident)

            def attention0(u, live):
                def scores(gr):
                    G = NG * u.n + gr
                    if gr == 0:
                        pe.wait_ge(S("qT_ready"), u.n + 1)
                        pe.wait_ge(S("kblk_ready"), u.n + 1)
                    after(pe, S("s_sub"), G - 1)
                    one(bank[gr % 2][:, 0:HG * NK], qz[u.par][:, gr, :],
                        kblk[u.par][:].rearrange("p h k -> p (h k)")).then_inc(S("s_done"), 1)

                def turns(t, gr):
                    G = NG * t.n + gr
                    pe.wait_ge(S("s_sub"), G + 1)
                    after(pe, S("exp_done"), G - 1)
                    for h in range(HG):
                        last = turn(bank[2 + gr % 2][0:NK, h * P:(h + 1) * P], sm[gr % 2][:, h, :])
                    last.then_inc(S("t_done"), 1)

                def values(t, gr):
                    if gr == 0:
                        pe.wait_ge(S("v_ready"), t.n + 1)
                        after(pe, S("o_sum"), t.n - 1)
                    pe.wait_ge(*split_count(t, gr))
                    for h in range(HG):
                        hd = HG * gr + h
                        w = 3 * (DH + 1)
                        vp = vpart[t.par][:, hd, :, :].rearrange("k c d -> k (c d)")
                        mm(bank[5 + t.par][:, hd * w:(hd + 1) * w], p_hi[gr][:, h, :], vp, start=True, stop=False)
                        last = mm(bank[5 + t.par][:, hd * w:(hd + 1) * w], p_lo[gr][:, h, :], vp, start=False, stop=True)
                    last.then_inc(S("pv_done"), 1)

                prev = u + -1
                if live(-1):
                    turns(prev, 2)
                if live(0):
                    scores(0)
                if live(0) or live(1):
                    after(pe, S("qT_ready"), u.n + 1)
                if live(0):
                    one(bank[4][0:NK, 2 * P:3 * P], ctxT[u.par][:, 0:NK], wa[:, 2, :]).then_inc(S("v_done"), 1)
                if live(1):
                    t = u + 1
                    pe.wait_ge(S("xn_ready0"), t.n + 1)
                    pe.wait_ge(S(f"ctx_in0{t.par}"), 16 * (t.half + 1))
                    turn(bank[4][:, 0:P], xn[t.par][:])
                    one(bank[4][:, P:P + NK], wa[:, 1, :], ctxT[t.par][:, 0:NK]).then_inc(S("kx_done"), 1)
                if live(-1):
                    values(prev, 0)
                    turns(prev, 3)
                if live(0):
                    scores(1)
                if live(-1):
                    values(prev, 1)
                if live(-2) or live(-4):
                    w = u + -2
                    if live(-3):
                        after(pe, S("x_added0"), w.n)
                    if live(-5):
                        after(pe, S("lg_ready0"), w.n - 2)
                    if live(-2):
                        t = u + -2
                        pe.wait_ge(S("o_ready0"), t.n + 1)
                        last = turn(bank[7][:, 0:P], o[t.par][:])
                    if live(-4):
                        t = u + -4
                        pe.wait_ge(S("xe_ready0"), t.n + 1)
                        last = turn(bank[7][:, P:2 * P], xe[t.par][:])
                    last.then_inc(S("ox_done"), 1)
                if live(0):
                    turns(u, 0)
                    scores(2)
                if live(1):
                    t = u + 1
                    pe.wait_ge(S("xnT_ready0"), t.n + 1)
                    pe.wait_ge(S("kf_ready"), t.n + 1)
                    if live(0):
                        pe.wait_ge(S("v_rest"), u.n + 1)
                    one(bank[4][:, 3 * P:4 * P], wa[:, 0, :], xnT[t.par][:]).then_inc(S("qT_done"), 1)
                if live(-1):
                    values(prev, 2)
                if live(0):
                    turns(u, 1)
                    scores(3)
                if live(-1):
                    values(prev, 3)
                if live(-2) or live(-4):
                    w = u + -2
                    pe.wait_ge(S("ox_ready"), w.n + 1)
                    if live(-2):
                        last = one(bank[7][:, 2 * P:3 * P], oT[w.par], wa[:, 3, :])
                    if live(-4):
                        last = one(bank[7][:, 3 * P:3 * P + E], xeT[w.par], wr[:, 0, :])
                    last.then_inc(S("pl_done"), 1)
            sweep(pe, NT, 1, 4, attention0)

            def positions(l):
                oh2 = oh[:].rearrange("p t c e -> p (t c e)")
                pe.wait_ge(S("delta"), l + 1)
                for c in range(4):
                    last = one(bank[7][:, c:c + 1], oh2[:, c * P:(c + 1) * P], ones_b[:])
                last.then_inc(S("colsum"), 1)
                pe.wait_ge(S("csum"), l + 1)
                for k in range(4):
                    mm(bank[7][:, 16:16 + E], csum[:, k, :], same[:, 0:E], start=(k == 0), stop=(k == 3))
                for c in range(4):
                    o_ = bank[5][:, c * P:(c + 1) * P]
                    mm(o_, tri[:], oh2[:, c * P:(c + 1) * P], start=True, stop=False)
                    for k in range(c):
                        mm(o_, csum[:, k, :], same[:], start=False, stop=False)
                    last = mm(o_, csum[:, c, :], pairm[:], start=False, stop=True)
                last.then_inc(S("counts"), 1)

            expert_reg = [pe.alloc_register(f"expert{k}") for k in range(QUAD)]

            def experts(s):
                b, nf, wc = s["base"], s["f"], cols(s)
                nb = nf // P

                def expert(t):
                    if s["shared"] is not None:
                        return E + s["shared"]
                    return pe.snap(expert_reg[t.off % QUAD], min_val=0, max_val=E - 1)

                def body(u, live):
                    if live(-1):
                        t = u + -1
                        pe.wait_ge(S("h_ready"), b + t.n + 1)
                        after(pe, S("hTl_ready"), b + t.n - 1)
                        for c in range(nb):
                            last = turn(bank[2 + t.par][:, c * P:(c + 1) * P], hh[t.par][:, c * P:(c + 1) * P])
                        last.then_inc(S("hT_done"), 1)
                    if live(1):
                        t = u + 1
                        if s["shared"] is not None:
                            pe.wait_ge(S("xr_copied"), s["shared"] * NT + t.n + 1)
                        else:
                            pe.wait_ge(S(f"xr_in{s['l']}{t.par}"), 16 * (t.half + 1))
                        after(pe, S("xl_ready"), b + t.n)
                        turn(bank[6][:, 0:P], xr[t.par][:]).then_inc(S("xT_done"), 1)
                    if live(0):
                        ex = expert(u)
                        pe.wait_ge(S("xl_ready"), b + u.n + 1)
                        after(pe, S("h_ready"), b + u.n - 1)
                        wu = bass.ds(ex * wc, UP)
                        bk = bank[u.par][:]
                        mm(bk, ones_3[:], b_row[:, bass.ds(ex * BC, UP)], start=True, stop=False)
                        mm(bk, xh[u.par][:], w_r[:, 0, wu], start=False, stop=False)
                        mm(bk, xl[u.par][:], w_r[:, 0, wu], start=False, stop=False)
                        mm(bk, xh[u.par][:], w_r[:, 1, wu], start=False, stop=True).then_inc(S("up_done"), 1)
                    if live(-2):
                        t = u + -2
                        ex = expert(t)
                        pe.wait_ge(S("hTl_ready"), b + t.n + 1)
                        after(pe, S("y_ready"), b + t.n - 1)
                        bk = bank[4 + t.par][:, 0:2 * P]
                        for c in range(nb):
                            wd = w_r[:, :, bass.ds(ex * wc + UP + c * P, P)]
                            mm(bk, hTh[t.par][:, c * P:(c + 1) * P], wd, start=(c == 0), stop=False)
                            mm(bk, hTl[t.par][:, c * P:(c + 1) * P], wd, start=False, stop=False)
                        last = mm(bk[:, 0:P], ones_3[:], b_row[:, bass.ds(ex * BC + UP, P)], start=False, stop=True)
                        last.then_inc(S("down_done"), 1)
                    if live(1) and s["shared"] is None:
                        pe.reg_load(expert_reg[(u.off + 1) % QUAD], e_i[0:1, bass.ds((u + 1).n, 1)])
                sweep(pe, s["n"], 1, 2, body, QUAD)

            def context1(u, live):
                if live(1):
                    t = u + 1
                    pe.wait_ge(S(f"ctx_in1{t.par}"), 16 * (t.half + 1))
                    after(pe, S("c_bias"), t.n - 1)
                    one(bank[t.par][:, 0:2 * P], ctxT[t.par][:], wa[:, 5:7, :].rearrange("p i d -> p (i d)"))\
                        .then_inc(S("kc_done"), 1)
                if live(-1):
                    t = u + -1
                    pe.wait_ge(S("c_soft"), t.n + 1)
                    after(pe, S("kvm_ready"), 2 * (t.n - 1))
                    one(bank[2 + t.par][:, 0:P + 1], fsm[t.par][0:NK, P:2 * P], qkv[t.par][0:NK, 2 * P:3 * P + 1])\
                        .then_inc(S("kvp_done"), 1)

            positions(0)
            pe.wait_ge(S("wa_in1"), 16 * 5)
            pe.wait_ge(S("v_ones"), 2)
            sweep(pe, NT, 1, 1, context1)
            pe.wait_ge(S("kvm_ready"), 2 * NT)
            pe.wait_ge(S("emap"), 1)
            pe.wait_ge(S("w_split0"), NT)
            pe.wait_ge(S("b_row_in"), 48)
            experts(SWEEPS[0])

            def attention1(u, live):
                if live(1):
                    t = u + 1
                    pe.wait_ge(S("xnT_ready1"), t.n + 1)
                    after(pe, S("f_bias"), t.n)
                    one(bank[1][:, 0:P], xnT[t.par][:], wa[:, 4, :]).then_inc(S("q1_done"), 1)
                if live(-1):
                    t = u + -1
                    pe.wait_ge(S("qsT_ready"), t.n + 1)
                    after(pe, S("o_raw1"), t.n)
                    one(bank[4][:, 0:P + H], qsT[t.par][:], kvm(t)).then_inc(S("num_done"), 1)
                if live(0):
                    pe.wait_ge(S("f_soft"), u.n + 1)
                    after(pe, S("qsT_ready"), u.n)
                    turn(bank[3][:, 0:P], fsm[u.par][:, 0:P]).then_inc(S("qsT_done"), 1)
                if live(-1):
                    t = u + -1
                    pe.wait_ge(S("o_raw1"), t.n + 1)
                    after(pe, S("oT_ready1"), t.n)
                    turn(bank[5][:, 0:P], oraw[t.par][:]).then_inc(S("oT_done1"), 1)
                if live(-2):
                    t = u + -2
                    pe.wait_ge(S("xe_ready1"), t.n + 1)
                    after(pe, S("lg_ready1"), t.n)
                    turn(bank[7][:, 0:P], xe[t.par][:]).then_inc(S("xeT_done1"), 1)
                if live(2):
                    t = u + 2
                    pe.wait_ge(S("xn_ready1"), t.n + 1)
                    after(pe, S("xnT_ready1"), t.n)
                    turn(bank[0][:, 0:P], xn[t.par][:]).then_inc(S("xnT_done1"), 1)
                if live(-1):
                    t = u + -1
                    pe.wait_ge(S("oT_ready1"), t.n + 1)
                    after(pe, S("x_added1"), t.n)
                    one(bank[6][:, 0:P], oT[t.par], wa[:, 7, :]).then_inc(S("proj_done1"), 1)
                if live(-2):
                    t = u + -2
                    pe.wait_ge(S("xeT_ready1"), t.n + 1)
                    one(bank[7][:, 2 * P:2 * P + E], xeT[t.par], wr[:, 1, :]).then_inc(S("logit_done1"), 1)
            sweep(pe, NT, 2, 2, attention1)
            positions(1)
            pe.wait_ge(S("emap"), 2)
            pe.wait_ge(S("w_split1"), NT)
            pe.wait_ge(S("b_row_in"), 96)
            for s in SWEEPS[1:]:
                experts(s)


def kernel(**inputs):
    import concourse.bacc as _bacc
    from concourse.bass_utils import run_bass_kernel_spmd as _run

    i = {k: np.asarray(v) for k, v in inputs.items()}
    A0, A1, M0, M1 = "L0_xattn_", "L1_xattn_", "L0_ffn_", "L1_ffn_"

    def rows_first(w):
        return np.moveaxis(w, -2, 0)

    def halves(w):
        e, f, d = w.shape
        return w.reshape(e, f // P, P, d).transpose(2, 0, 1, 3).reshape(P, e, f // P * d)

    w0 = np.concatenate([rows_first(i[M0 + "W1"].transpose(0, 2, 1)), rows_first(i[M0 + "W2"].transpose(0, 2, 1)),
                         halves(i[M0 + "W3"].transpose(0, 2, 1))], axis=2).reshape(P, -1)
    up = np.concatenate([i[M1 + "W1"], i[M1 + "sW1"]], axis=0)
    down = np.concatenate([i[M1 + "W2"], i[M1 + "sW2"]], axis=0)
    w1 = np.concatenate([rows_first(up), halves(down)], axis=2).reshape(P, -1)
    arrays = {
        "x": i["x"], "ctxT": i["ctx_1024"].transpose(0, 2, 1), "cst": constants(), "w0": w0, "w1": w1,
        "wq0": i[A0 + "Wq"].T, "wk0": i[A0 + "Wk"].T, "wv0": i[A0 + "Wv"].T, "wo0": i[A0 + "Wo"].T,
        "wq1": i[A1 + "Wq"].T, "wk1": i[A1 + "Wk"].T, "wv1": i[A1 + "Wv"].T, "wp1": i[A1 + "Wp"].T,
        "wr0": i[M0 + "Wg"].T, "wr1": i[M1 + "rW"], "rb": i[M1 + "rb"],
        "bq0": i[A0 + "bq"], "bk0": i[A0 + "bk"], "bv0": i[A0 + "bv"], "bo0": i[A0 + "bo"],
        "bq1": i[A1 + "bq"], "bk1": i[A1 + "bk"], "bv1": i[A1 + "bv"], "bp1": i[A1 + "bp"],
        "eb0": np.concatenate([i[M0 + "b1"], i[M0 + "b2"], i[M0 + "b3"]], axis=1),
        "eb1": np.concatenate([np.concatenate([i[M1 + "b1"], i[M1 + "sb1"]], axis=0),
                               np.concatenate([i[M1 + "b2"], i[M1 + "sb2"]], axis=0)], axis=1),
    }
    arrays = {"in_" + k: np.ascontiguousarray(v) for k, v in arrays.items()}
    nc = _bacc.Bacc("TRN2", target_bir_lowering=False, num_devices=1)
    aps = {k[3:]: nc.dram_tensor(k, v.shape, mybir.dt.from_np(v.dtype), kind="ExternalInput").ap()
           for k, v in arrays.items()}
    out = nc.dram_tensor("out", (NT, P, P), F32, kind="ExternalOutput").ap()
    build(nc, aps, out)
    r = _run(nc, [arrays], core_ids=[0])
    return r.results[0]["out"]
```
